# Optimizing a Trainium2 kernel written in Bass

```python
import numpy as np
import jax
import jax.numpy as jnp

def _softmax(x, axis=-1):
    return jax.nn.softmax(x, axis=axis)

def _gelu(x):
    return jax.nn.gelu(x, approximate=True)

def _silu(x):
    return jax.nn.silu(x)

def _sigmoid(x):
    return jax.nn.sigmoid(x)

def _layernorm(x, axis=-1, eps=1e-05):
    m = jnp.mean(x, axis=axis, keepdims=True)
    v = jnp.var(x, axis=axis, keepdims=True)
    return (x - m) / jnp.sqrt(v + eps)

def _scatter_add(tgt, idx, src, axis=0):
    return tgt.at[idx].add(src)

def _segment_sum(src, seg, n):
    return jax.ops.segment_sum(src, seg, n)
kernel_name = 'mk_xattn_ffn_d1_seqx_r4_b4e355'

def setup_inputs(seed: int=0):
    np.random.seed(seed)
    _w = jnp.asarray

    def _rec_inputs():
        import jax
        import jax.numpy as jnp
        _rk = jax.random.key(seed)
        x = -0.000125 + 0.9999 * jax.random.normal(jax.random.fold_in(_rk, 1), (16, 256, 512), jnp.float32)
        _lenS = 256 - jax.random.randint(jax.random.fold_in(_rk, 7), (16,), 0, max(1, 256 // 4) + 1, jnp.int32)
        _lenS2 = 256 - jax.random.randint(jax.random.fold_in(_rk, 8), (16,), 0, max(1, 256 // 4) + 1, jnp.int32)
        _ctx_2048P = jax.random.normal(jax.random.fold_in(_rk, 11), (16, 16, 512), jnp.float32)
        _ctx_2048c = jax.random.dirichlet(jax.random.fold_in(_rk, 511), 0.3 * jnp.ones((16,), jnp.float32), (16, 256))
        _ctx_2048t = jnp.einsum('bsk,bkd->bsd', _ctx_2048c, _ctx_2048P)
        _ctx_2048t = _ctx_2048t * jax.lax.rsqrt(jnp.mean(jnp.square(_ctx_2048t)) + 1e-12) * 0.953939
        ctx_2048 = -0.000540021 + 0.99982 * (_ctx_2048t + 0.3 * jax.random.normal(jax.random.fold_in(_rk, 611), (16, 256, 512), jnp.float32))
        return (x, ctx_2048)
    x, ctx_2048 = _rec_inputs()

    def _L0_xattn_setup():
        import jax, jax.numpy as jnp
        import numpy as np
        DIM = 512
        N_HEADS = 16
        HEAD_DIM = DIM // N_HEADS
        EPS = 1e-06
        IMG_LEN = 257

        def rms_norm(x, g, eps=EPS):
            var = jnp.mean(x * x, axis=-1, keepdims=True)
            return x * jax.lax.rsqrt(var + eps) * g

        def _attend(q, k, v, k_mask=None):
            scale = 1.0 / jnp.sqrt(jnp.asarray(HEAD_DIM, q.dtype))
            scores = jnp.einsum('bqnd,bknd->bnqk', q, k) * scale
            if k_mask is not None:
                neg = jnp.asarray(jnp.finfo(scores.dtype).min, scores.dtype)
                scores = jnp.where(k_mask[:, None, None, :], scores, neg)
            probs = jax.nn.softmax(scores, axis=-1)
            return jnp.einsum('bnqk,bknd->bqnd', probs, v)
        key = jax.random.key(seed)
        ks = jax.random.split(key, 16)
        B, L1, L2 = (1, 4096, 769)
        std = 0.02
        inp = {'x': jax.random.normal(ks[0], (B, L1, DIM), jnp.float32), 'context': jax.random.normal(ks[1], (B, L2, DIM), jnp.float32), 'context_lens': jax.random.randint(ks[2], (B,), 64, 513, jnp.int32), 'Wq': jax.random.normal(ks[3], (DIM, DIM), jnp.float32) * std, 'bq': jnp.zeros((DIM,), jnp.float32), 'gq': jnp.ones((DIM,), jnp.float32), 'Wk': jax.random.normal(ks[4], (DIM, DIM), jnp.float32) * std, 'bk': jnp.zeros((DIM,), jnp.float32), 'gk': jnp.ones((DIM,), jnp.float32), 'Wv': jax.random.normal(ks[5], (DIM, DIM), jnp.float32) * std, 'bv': jnp.zeros((DIM,), jnp.float32), 'Wk_img': jax.random.normal(ks[6], (DIM, DIM), jnp.float32) * std, 'bk_img': jnp.zeros((DIM,), jnp.float32), 'gk_img': jnp.ones((DIM,), jnp.float32), 'Wv_img': jax.random.normal(ks[7], (DIM, DIM), jnp.float32) * std, 'bv_img': jnp.zeros((DIM,), jnp.float32), 'Wo': jax.random.normal(ks[8], (DIM, DIM), jnp.float32) * std, 'bo': jnp.zeros((DIM,), jnp.float32)}
        return inp
    _L0_xattn_all = _L0_xattn_setup()
    _L0_xattn_in = {k: v for k, v in _L0_xattn_all.items() if k in ('context_lens', 'Wq', 'bq', 'gq', 'Wk', 'bk', 'gk', 'Wv', 'bv', 'Wk_img', 'bk_img', 'gk_img', 'Wv_img', 'bv_img', 'Wo', 'bo')}
    del _L0_xattn_all

    def _L0_ffn_setup():
        import jax, jax.numpy as jnp
        import numpy as np
        TOP_K = 6
        N_GROUP = 8
        TOPK_GROUP = 3
        CAPACITY = 192
        RSF = 1.0
        key = jax.random.key(seed)
        ks = jax.random.split(key, 8)
        B, S, H = (1, 1024, 512)
        E, M = (64, 352)
        MS = 704
        sc = 0.02
        return {'hidden_states': jax.random.normal(ks[0], (B, S, H), jnp.float32), 'gate_weight': jax.random.normal(ks[1], (E, H), jnp.float32) * sc, 'Wg': jax.random.normal(ks[2], (E, M, H), jnp.float32) * sc, 'Wu': jax.random.normal(ks[3], (E, M, H), jnp.float32) * sc, 'Wd': jax.random.normal(ks[4], (E, H, M), jnp.float32) * sc, 'Sg': jax.random.normal(ks[5], (MS, H), jnp.float32) * sc, 'Su': jax.random.normal(ks[6], (MS, H), jnp.float32) * sc, 'Sd': jax.random.normal(ks[7], (H, MS), jnp.float32) * sc}
    _L0_ffn_all = _L0_ffn_setup()
    _L0_ffn_in = {k: v for k, v in _L0_ffn_all.items() if k in ('gate_weight', 'Wg', 'Wu', 'Wd', 'Sg', 'Su', 'Sd')}
    del _L0_ffn_all
    return {'x': x, 'ctx_2048': ctx_2048, 'L0_xattn_context_lens': _L0_xattn_in['context_lens'], 'L0_xattn_Wq': _L0_xattn_in['Wq'], 'L0_xattn_bq': _L0_xattn_in['bq'], 'L0_xattn_gq': _L0_xattn_in['gq'], 'L0_xattn_Wk': _L0_xattn_in['Wk'], 'L0_xattn_bk': _L0_xattn_in['bk'], 'L0_xattn_gk': _L0_xattn_in['gk'], 'L0_xattn_Wv': _L0_xattn_in['Wv'], 'L0_xattn_bv': _L0_xattn_in['bv'], 'L0_xattn_Wk_img': _L0_xattn_in['Wk_img'], 'L0_xattn_bk_img': _L0_xattn_in['bk_img'], 'L0_xattn_gk_img': _L0_xattn_in['gk_img'], 'L0_xattn_Wv_img': _L0_xattn_in['Wv_img'], 'L0_xattn_bv_img': _L0_xattn_in['bv_img'], 'L0_xattn_Wo': _L0_xattn_in['Wo'], 'L0_xattn_bo': _L0_xattn_in['bo'], 'L0_ffn_gate_weight': _L0_ffn_in['gate_weight'], 'L0_ffn_Wg': _L0_ffn_in['Wg'], 'L0_ffn_Wu': _L0_ffn_in['Wu'], 'L0_ffn_Wd': _L0_ffn_in['Wd'], 'L0_ffn_Sg': _L0_ffn_in['Sg'], 'L0_ffn_Su': _L0_ffn_in['Su'], 'L0_ffn_Sd': _L0_ffn_in['Sd']}

def reference(x, ctx_2048, L0_xattn_context_lens, L0_xattn_Wq, L0_xattn_bq, L0_xattn_gq, L0_xattn_Wk, L0_xattn_bk, L0_xattn_gk, L0_xattn_Wv, L0_xattn_bv, L0_xattn_Wk_img, L0_xattn_bk_img, L0_xattn_gk_img, L0_xattn_Wv_img, L0_xattn_bv_img, L0_xattn_Wo, L0_xattn_bo, L0_ffn_gate_weight, L0_ffn_Wg, L0_ffn_Wu, L0_ffn_Wd, L0_ffn_Sg, L0_ffn_Su, L0_ffn_Sd):
    import jax
    import jax.numpy as jnp

    def _L0_xattn_ref(x, context, context_lens, Wq, bq, gq, Wk, bk, gk, Wv, bv, Wk_img, bk_img, gk_img, Wv_img, bv_img, Wo, bo):
        import jax, jax.numpy as jnp
        import numpy as np
        DIM = 512
        N_HEADS = 16
        HEAD_DIM = DIM // N_HEADS
        EPS = 1e-06
        IMG_LEN = 257

        def rms_norm(x, g, eps=EPS):
            var = jnp.mean(x * x, axis=-1, keepdims=True)
            return x * jax.lax.rsqrt(var + eps) * g

        def _attend(q, k, v, k_mask=None):
            scale = 1.0 / jnp.sqrt(jnp.asarray(HEAD_DIM, q.dtype))
            scores = jnp.einsum('bqnd,bknd->bnqk', q, k) * scale
            if k_mask is not None:
                neg = jnp.asarray(jnp.finfo(scores.dtype).min, scores.dtype)
                scores = jnp.where(k_mask[:, None, None, :], scores, neg)
            probs = jax.nn.softmax(scores, axis=-1)
            return jnp.einsum('bnqk,bknd->bqnd', probs, v)
        b = x.shape[0]
        n, d = (N_HEADS, HEAD_DIM)
        ctx_img = context[:, :IMG_LEN]
        ctx_txt = context[:, IMG_LEN:]
        q = rms_norm(x @ Wq + bq, gq).reshape(b, -1, n, d)
        k = rms_norm(ctx_txt @ Wk + bk, gk).reshape(b, -1, n, d)
        v = (ctx_txt @ Wv + bv).reshape(b, -1, n, d)
        k_img = rms_norm(ctx_img @ Wk_img + bk_img, gk_img).reshape(b, -1, n, d)
        v_img = (ctx_img @ Wv_img + bv_img).reshape(b, -1, n, d)
        img_x = _attend(q, k_img, v_img)
        k_mask = jnp.arange(k.shape[1])[None, :] < context_lens[:, None]
        txt_x = _attend(q, k, v, k_mask)
        out = (txt_x + img_x).reshape(b, -1, n * d)
        return out @ Wo + bo

    def _L0_ffn_ref(hidden_states, gate_weight, Wg, Wu, Wd, Sg, Su, Sd):
        import jax, jax.numpy as jnp
        import numpy as np
        TOP_K = 6
        N_GROUP = 8
        TOPK_GROUP = 3
        CAPACITY = 192
        RSF = 1.0
        B, S, H = hidden_states.shape
        E, M, _ = Wg.shape
        K, NG, TG, C = (TOP_K, N_GROUP, TOPK_GROUP, CAPACITY)
        x = hidden_states.reshape(-1, H)
        T = x.shape[0]
        logits = x.astype(jnp.float32) @ gate_weight.astype(jnp.float32).T
        scores = jax.nn.softmax(logits, axis=-1)
        group_scores = scores.reshape(T, NG, E // NG).max(axis=-1)
        _, gidx = jax.lax.top_k(group_scores, TG)
        gmask = jnp.zeros((T, NG), scores.dtype).at[jnp.arange(T)[:, None], gidx].set(1.0)
        smask = jnp.repeat(gmask, E // NG, axis=1)
        tmp_scores = jnp.where(smask > 0, scores, 0.0)
        topk_w, topk_i = jax.lax.top_k(tmp_scores, K)
        topk_w = topk_w * RSF
        flat = topk_i.reshape(-1)
        oh = jax.nn.one_hot(flat, E, dtype=jnp.int32)
        pos = jnp.sum(jnp.cumsum(oh, axis=0) * oh, axis=-1) - 1
        slot = flat * C + jnp.minimum(pos, C - 1)
        tok = jnp.arange(T * K) // K
        buf = jnp.zeros((E * C, H), x.dtype).at[slot].set(x[tok]).reshape(E, C, H)
        g = jnp.einsum('ech,emh->ecm', buf, Wg)
        u = jnp.einsum('ech,emh->ecm', buf, Wu)
        out = jnp.einsum('ecm,ehm->ech', jax.nn.silu(g) * u, Wd).reshape(E * C, H)
        yk = out[slot].reshape(T, K, H)
        y = jnp.sum(yk * topk_w[..., None].astype(yk.dtype), axis=1)
        shared = jax.nn.silu(x @ Sg.T) * (x @ Su.T) @ Sd.T
        return (y + shared).reshape(B, S, H)
    x = x + _L0_xattn_ref(_layernorm(x, axis=-1), ctx_2048, L0_xattn_context_lens, L0_xattn_Wq, L0_xattn_bq, L0_xattn_gq, L0_xattn_Wk, L0_xattn_bk, L0_xattn_gk, L0_xattn_Wv, L0_xattn_bv, L0_xattn_Wk_img, L0_xattn_bk_img, L0_xattn_gk_img, L0_xattn_Wv_img, L0_xattn_bv_img, L0_xattn_Wo, L0_xattn_bo)
    x = x + _L0_ffn_ref(_layernorm(x, axis=-1), L0_ffn_gate_weight, L0_ffn_Wg, L0_ffn_Wu, L0_ffn_Wd, L0_ffn_Sg, L0_ffn_Su, L0_ffn_Sd)
    return x

_drawn_inputs = setup_inputs


def setup_inputs(seed=0):
    import zlib

    import numpy as np

    out = dict(_drawn_inputs(seed))
    spreads = {'L0_xattn_bq': (0.0, 0.8),
     'L0_xattn_gq': (1.0, 0.6),
     'L0_xattn_bk': (0.0, 0.1),
     'L0_xattn_gk': (1.0, 0.2),
     'L0_xattn_bv': (0.0, 0.1),
     'L0_xattn_bk_img': (0.0, 0.8),
     'L0_xattn_gk_img': (1.0, 0.6),
     'L0_xattn_bv_img': (0.0, 0.1),
     'L0_xattn_bo': (0.0, 0.1)}
    factors = {'L0_ffn_gate_weight': 8.0,
     'L0_ffn_Wg': 8.0,
     'L0_ffn_Wu': 8.0,
     'L0_ffn_Wd': 8.0,
     'L0_ffn_Sg': 8.0,
     'L0_ffn_Su': 8.0,
     'L0_ffn_Sd': 8.0}
    for name, (base, spread) in spreads.items():
        noise = np.random.default_rng([zlib.crc32(name.encode()), seed]).standard_normal(out[name].shape)
        drawn = base * np.exp(spread * noise) if base else spread * noise
        out[name] = jnp.asarray(drawn.astype(out[name].dtype))
    for name, factor in factors.items():
        out[name] = (out[name] * factor).astype(out[name].dtype)
    return out
```

```python
from contextlib import ExitStack

import concourse.bass as bass
from concourse import mybir

F32 = mybir.dt.float32
F32R = mybir.dt.float32r
BF16 = mybir.dt.bfloat16
I32 = mybir.dt.int32
U32 = mybir.dt.uint32
ALU = mybir.AluOpType
ACT = mybir.ActivationFunctionType
X = mybir.AxisListType.X

P = 128
HEAD_DIM = 32
TOP_K = 6
N_GROUP = 8
TOPK_GROUP = 3
CAPACITY = 192
RMS_EPS = 1e-6
LN_EPS = 1e-5
SCALE = float(HEAD_DIM) ** -0.5
OVER = 65536.0



def need(eng, sem, value):
    if isinstance(value, int) and value <= 0:
        return
    eng.wait_ge(sem, value)


class Kind:
    def __init__(self, prep, attend, post, scatter):
        self.prep, self.attend, self.post, self.scatter = prep, attend, post, scatter


SHARED_USES = [
    ("v0", "attend"), ("pv3", "post"), ("v1", "attend"), ("o0", "post"), ("o1", "post"),
    ("k01", "prep"), ("k23", "prep"), ("pv0", "attend"), ("nT0", "post"), ("nT1", "post"),
    ("logits", "post"), ("xT0", "prep"), ("xT1", "prep"), ("q01", "prep"), ("pv1", "attend"),
    ("ssk", "prep"), ("q23", "prep"), ("pv2", "attend"), ("pos", "post"), ("ssq", "prep"),
]


def shared_plan(kinds):
    before = [None, None]
    n = 0
    plans = []
    for at, kind in enumerate(kinds):
        plan = {}
        for name, stage in SHARED_USES:
            if {"attend": kind.attend, "post": kind.post, "prep": kind.prep}[stage]:
                last = before[n % 2]
                plan[name] = (n % 2, last and last[0], last and at - last[1])
                before[n % 2] = (name, at)
                n += 1
        plans.append(plan)
    return plans


def phase_a(nc, d, keep):
    B, S, D = d["x"].shape
    KC = D // P
    QT = S // P
    H = D // HEAD_DIM
    HC = P // HEAD_DIM
    CK = d["ctxT"].shape[2]
    KT = CK // P
    UNITS = KC * QT
    E = d["gateT"].shape[1]
    GE = E // N_GROUP
    assert (KC, QT, HC, KT, UNITS) == (4, 2, 4, 2, 8)

    prologue = [Kind(True, False, False, False), Kind(True, True, False, False), Kind(True, True, True, False)]
    steady = Kind(True, True, True, True)
    epilogue = [Kind(False, True, True, True), Kind(False, False, True, True), Kind(False, False, False, True)]
    LOOP = B - 3
    plans = shared_plan([*prologue, steady, steady, *epilogue])
    assert plans[len(prologue)] == plans[len(prologue) + 1]

    def pipeline(eng, body):
        for at, kind in enumerate(prologue):
            body(at - 1, kind, plans[at])
        with eng.Fori(2, 2 + LOOP) as i:
            body(i, steady, plans[len(prologue)])
        for at, kind in enumerate(epilogue):
            body(2 + LOOP + at, kind, plans[len(prologue) + 2 + at])

    with ExitStack() as ctx:
        def sb(name, shape, dt=F32):
            return ctx.enter_context(nc.sbuf_tensor(name, shape, dt))

        def ps(name, shape, dt=F32):
            return ctx.enter_context(nc.psum_tensor(name, shape, dt))

        def sem(name):
            return ctx.enter_context(nc.semaphore(name))

        w_hi = {n: sb(f"w{n}_hi", [P, KC, D], F32R) for n in "kqvo"}
        w_lo = {n: sb(f"w{n}_lo", [P, KC, D], F32R) for n in "kqvo"}
        gate_hi, gate_lo = sb("gate_hi", [P, KC, E], F32R), sb("gate_lo", [P, KC, E], F32R)
        vecs = sb("vec_cols", [P, 5, KC])
        bo_row = sb("bo_row", [P, D])
        consts = sb("const_cols", [P, d["consts"].shape[1]])
        ident, ones = consts[:, 0:P], consts[:, 2 * P:3 * P]
        iota_e, iota_g = consts[:, 3 * P:3 * P + E], consts[:, 3 * P:3 * P + N_GROUP]
        slot_base = consts[:, 3 * P + E:3 * P + 2 * E]
        tok_col = consts[:, 3 * P + 2 * E:3 * P + 2 * E + QT]
        tri_b, ones_b = sb("tri_b", [P, P], BF16), sb("ones_b", [P, P], BF16)
        eps_rms = sb("eps_rms", [P, 1])
        minus_half = sb("minus_half", [P, QT])
        x_raw = sb("x_raw", [P, QT, D])
        ctx_raw = sb("ctx_raw", [P, KC, CK])
        ctx_hi, ctx_lo = sb("ctx_hi", [P, KC, CK], F32R), sb("ctx_lo", [P, KC, CK], F32R)
        tT_hi, tT_lo = sb("tT_hi", [P, KC, S], F32R), sb("tT_lo", [P, KC, S], F32R)
        full = {n: sb(f"{n}_full", [P, KC, S]) for n in "kq"}
        sq_sum, rms_a, rms_b = sb("sq_sum", [P, S]), sb("rms_a", [P, S]), sb("rms_b", [P, S])
        hT = {n: (sb(f"{n}T_hi", [P, KC, S], F32R), sb(f"{n}T_lo", [P, KC, S], F32R)) for n in "kq"}
        ln_stats, ln_mv = sb("ln_stats", [P, QT, 6]), sb("ln_mv", [P, QT, 2])
        ln_var, ln_rstd = sb("ln_var", [P, QT]), sb("ln_rstd", [P, QT])
        v_hi, v_lo = sb("v_hi", [P, KT, H, P], F32R), sb("v_lo", [P, KT, H, P], F32R)
        probs = sb("probs", [P, 2, HC, CK])
        neg_max, row_sum, row_inv = sb("neg_max", [P, 2, HC]), sb("row_sum", [P, 2, HC]), sb("row_inv", [P, 2, HC])
        row_max = sb("row_max", [P, 2, HC])
        pT_hi, pT_lo = sb("pT_hi", [P, HC * KT, S], F32R), sb("pT_lo", [P, HC * KT, S], F32R)
        aT_hi, aT_lo = sb("aT_hi", [P, KC, S], F32R), sb("aT_lo", [P, KC, S], F32R)
        x2 = sb("x2_rows", [P, QT, D])
        xn2 = sb("xn2_rows", [P, QT, D])
        n2_stats, n2_mv = sb("n2_stats", [P, QT, 6]), sb("n2_mv", [P, QT, 2])
        n2_var, n2_rstd = sb("n2_var", [P, QT]), sb("n2_rstd", [P, QT])
        lg_max, lg_sum = sb("lg_max", [P, QT]), sb("lg_sum", [P, QT])
        score = sb("score", [P, QT, E])
        g_score, g_top, g_idx, g_idxf = (sb("g_score", [P, QT, N_GROUP]), sb("g_top", [P, QT, 8]),
                                         sb("g_idx", [P, QT, 8], U32), sb("g_idxf", [P, QT, 8]))
        g_hot, g_mask = sb("g_hot", [P, QT, TOPK_GROUP, N_GROUP]), sb("g_mask", [P, QT, N_GROUP])
        e_top, e_idx, e_idxf = sb("e_top", [P, QT, 8]), sb("e_idx", [P, QT, 8], U32), sb("e_idxf", [P, QT, 8])
        e_hot = sb("e_hot", [P, QT, TOP_K, E], BF16)
        e_slot = sb("e_slot", [P, QT, TOP_K, E])
        mask_f, mask_b = sb("mask_f", [P, QT, E]), sb("mask_b", [P, QT, E], BF16)
        seen, seen_b = sb("seen", [P, E]), sb("seen_b", [P, E], BF16)
        slot_val = sb("slot_val", [P, QT, E])
        last_tok = sb("last_tok", [P, E])
        slot_f, last_slot, is_last, scat_f = (sb("slot_f", [P, QT, TOP_K]), sb("last_slot", [P, QT, TOP_K]),
                                              sb("is_last", [P, QT, TOP_K]), sb("scat_f", [P, QT, TOP_K]))
        scat_idx = sb("scat_idx", [P, QT * TOP_K], U32)
        scat_tok = sb("scat_tok", [P, QT], I32)
        zero_i = sb("zero_i", [P, E * CAPACITY // P], I32)
        lastT, lastT_i = sb("lastT", [E, 1]), sb("lastT_i", [E, 1], I32)

        settled = sb("settled", [P, 8])

        scores_ps = [ps(f"scores_ps{n}", [P, HC, CK]) for n in range(2)]
        pT_ps = ps("pT_ps", [P, HC * KT, P])
        shared_ps = [ps(f"shared_ps{n}", [P, 512]) for n in range(2)]

        in_sem = sem("a_params_loaded")
        vec_sem = sem("a_vectors_loaded")
        stage_in = [sem(f"a_weight_half_loaded{n}") for n in range(2)]
        w_hi_done, w_lo_done = sem("a_weight_hi_done"), sem("a_weight_lo_done")
        gate_split = sem("a_gate_split")
        chain = {n: sem(f"a_vector_{n}_chain") for n in ("setup", "prep", "attend", "post")}
        setup_p = sem("a_setup_by_pool")
        table_zeroed = sem("a_table_zeroed")
        x_in, ctx_in, res_in = sem("a_x_loaded"), sem("a_ctx_loaded"), sem("a_residual_loaded")
        ctx_hi_s, ctx_lo_s = sem("a_ctx_hi_done"), sem("a_ctx_lo_done")
        stats1, rstd1, xn_s = sem("a_ln1_var_done"), sem("a_ln1_rstd_done"), sem("a_ln1_done")
        x_turned, x_hi_s, x_lo_s = sem("a_x_turned"), sem("a_xT_hi_done"), sem("a_xT_lo_done")
        proj = {n: sem(f"a_{n}_product_done") for n in "kq"}
        full_s = {n: sem(f"a_{n}_biased") for n in "kq"}
        sq_s = {n: sem(f"a_{n}_squared") for n in "kq"}
        sqsum_s = {n: sem(f"a_{n}_squares_summed") for n in "kq"}
        ss_s = {n: sem(f"a_{n}_sum_of_squares_done") for n in "kq"}
        ms_s = {n: sem(f"a_{n}_mean_square_done") for n in "kq"}
        ln_s = {n: sem(f"a_{n}_log_done") for n in "kq"}
        ry_s = {n: sem(f"a_{n}_rms_guess_done") for n in "kq"}
        fin_s = {n: sem(f"a_{n}_normed") for n in "kq"}
        hi_s = {n: sem(f"a_{n}_hi_done") for n in "kq"}
        lo_s = {n: sem(f"a_{n}_lo_done") for n in "kq"}
        v_done, v_hi_s, v_lo_s = sem("a_v_product_done"), sem("a_v_hi_done"), sem("a_v_lo_done")
        head_done = sem("a_head_scores_done")
        scores_done, max_done, exp_done = sem("a_scores_done"), sem("a_max_done"), sem("a_exp_done")
        inv_done, probs_done = sem("a_row_inv_done"), sem("a_probs_normed")
        p_turned, p_hi_s, p_lo_s = sem("a_probs_turned"), sem("a_pT_hi_done"), sem("a_pT_lo_done")
        pv_done, a_hi_s, a_lo_s = sem("a_pv_done"), sem("a_aT_hi_done"), sem("a_aT_lo_done")
        bo_added, o_done, x2_s = sem("a_residual_plus_bo"), sem("a_o_product_done"), sem("a_x2_done")
        stats2, rstd2, xn2_s = sem("a_ln2_var_done"), sem("a_ln2_rstd_done"), sem("a_ln2_done")
        x2_out, xn2_out = sem("a_x2_stored"), sem("a_xn2_stored")
        n_turned, n_hi_s, n_lo_s = sem("a_xn2_turned"), sem("a_xn2T_hi_done"), sem("a_xn2T_lo_done")
        logits_done, lgmax_s, lgexp_s = sem("a_logits_done"), sem("a_logit_max_done"), sem("a_logit_exp_done")
        mask_s, pos_done, scat_rdy = sem("a_mask_done"), sem("a_positions_done"), sem("a_scatter_index_done")
        scattered = sem("a_tokens_scattered")
        lastT_s, last_i_s, last_out = (sem("a_last_turned"), sem("a_last_index_done"),
                                               sem("a_last_stored"))
        pos_read = sem("a_positions_read")

        def read_of(name, i):
            kind, n = name.rstrip("0123456789"), name.lstrip("abcdefghijklmnopqrstuvwxyzT")
            if kind == "v":
                return v_lo_s, KT * i + int(n) + 1
            if kind == "pv":
                b = i - 1 if n == "3" else i
                return a_lo_s, KC * b + int(n) + 1
            if kind == "o":
                return x2_s, QT * (i - 1) + int(n) + 1
            if kind in ("k", "q"):
                return full_s[kind], KC * (i + 1) + int(n[-1]) + 1
            if kind == "nT":
                return n_lo_s, QT * (i - 1) + int(n) + 1
            if kind == "xT":
                return x_lo_s, QT * (i + 1) + int(n) + 1
            if kind == "logits":
                return lgexp_s, i
            if kind == "pos":
                return pos_read, i
            return ms_s[kind[-1]], i + 2

        block = ctx.enter_context(nc.Block())
        halves = [(n, h) for n in "kqvo" for h in range(2)]
        stage = [full["k"], full["q"]]

        @block.sync
        def _(sp):
            sp.dma_start(ctx_raw[:], d["ctxT"][0].rearrange("(c p) t -> p c t", p=P)).then_inc(ctx_in, 16)
            for n, (w, h) in enumerate(halves[:2]):
                sp.dma_start(stage[n % 2][:].rearrange("p c t -> p (c t)"),
                             d["w" + w].rearrange("(c p) n -> p c n", p=P)[:, 2 * h:2 * h + 2, :]
                             ).then_inc(stage_in[n % 2], 16)
            sp.dma_start(x_raw[:], d["x"][0].rearrange("(q p) n -> p q n", p=P)).then_inc(x_in, 16)
            sp.dma_start(consts[:], d["consts"]).then_inc(in_sem, 16)
            sp.dma_start(vecs[:], d["vecs"]).then_inc(vec_sem, 16)
            sp.dma_start(bo_row[:], d["bo"].rearrange("(a n) -> a n", a=1).to_broadcast([P, D])).then_inc(vec_sem, 16)
            sp.dma_start(x2[:, 0, 0:KC * E].rearrange("p (c e) -> p c e", c=KC),
                         d["gateT"].rearrange("(c p) e -> p c e", p=P)).then_inc(vec_sem, 16)
            for n, (w, h) in enumerate(halves):
                if n < 2:
                    continue
                sp.wait_ge(w_hi_done, n - 1)
                sp.wait_ge(w_lo_done, n - 1)
                sp.dma_start(stage[n % 2][:].rearrange("p c t -> p (c t)"),
                             d["w" + w].rearrange("(c p) n -> p c n", p=P)[:, 2 * h:2 * h + 2, :]
                             ).then_inc(stage_in[n % 2], 16)
            sp.wait_ge(setup_p, 1)
            sp.dma_start(d["table"].rearrange("(p j) o -> p (j o)", p=P), zero_i[:]).then_inc(table_zeroed, 16)

            def body(i, kind, use):
                if kind.prep and not (isinstance(i, int) and i < 0):
                    b = i + 1
                    need(sp, ctx_lo_s, b)
                    need(sp, ctx_hi_s, b)
                    sp.dma_start(ctx_raw[:], d["ctxT"][b].rearrange("(c p) t -> p c t", p=P)).then_inc(ctx_in, 16)
                    sp.wait_ge(x_turned, QT * b)
                    sp.dma_start(x_raw[:], d["x"][b].rearrange("(q p) n -> p q n", p=P)).then_inc(x_in, 16)
                if kind.post:
                    b = i - 1
                    if isinstance(b, int) and b == 0:
                        sp.wait_ge(gate_split, 1)
                    else:
                        need(sp, x2_out, 16 * b)
                        need(sp, xn2_s, QT * i - QT)
                    sp.dma_start(x2[:], d["x"][b].rearrange("(q p) n -> p q n", p=P)).then_inc(res_in, 16)
                if kind.post:
                    b = i - 1
                    sp.wait_ge(x2_s, QT * b + QT)
                    sp.dma_start(d["x2"][b].rearrange("(q p) n -> p q n", p=P), x2[:]).then_inc(x2_out, 16)
                    sp.wait_ge(xn2_s, QT * b + QT)
                    sp.dma_start(d["xn2"][b].rearrange("(q p) n -> p q n", p=P), xn2[:]).then_inc(xn2_out, 16)

            pipeline(sp, body)
            sp.wait_ge(x2_out, 16 * B)
            sp.wait_ge(xn2_out, 16 * B)
            sp.wait_ge(scattered, 16 * QT * TOP_K * B)
            sp.wait_ge(last_i_s, 1)
            sp.dma_start(d["table"].rearrange("(e s) o -> e (s o)", s=CAPACITY)[:, CAPACITY - 1:CAPACITY],
                         lastT_i[:], allow_slow_non_contiguous=True).then_inc(last_out, 16)
            sp.wait_ge(last_out, 16)

        @block.tensor
        def _(pe):
            def mm3(out, a_hi, a_lo, b_hi, b_lo, first, last):
                pe.matmul(out, a_hi, b_hi, start=first, stop=False)
                pe.matmul(out, a_hi, b_lo, start=False, stop=False)
                return pe.matmul(out, a_lo, b_hi, start=False, stop=last)

            def shared(use, name, i, waited=None):
                bank, before, ago = use[name]
                if before:
                    signal, value = read_of(before, i - ago)
                    if signal is not waited:
                        need(pe, signal, value)
                return shared_ps[bank]

            def turn(use, name, src, q, i):
                bank = shared(use, name, i)
                for c in range(KC):
                    last = pe.transpose(bank[:, c * P:(c + 1) * P], src[:, q, c * P:(c + 1) * P], ident)
                return last

            def body(i, kind, use):
                def project(n, name, pair):
                    src_hi, src_lo = (ctx_hi, ctx_lo) if n == "k" else (tT_hi, tT_lo)
                    bank = shared(use, name, i, x_lo_s if name == "q01" else None)
                    for j in range(2):
                        c = 2 * pair + j
                        for kc in range(KC):
                            last = mm3(bank[:, j * S:(j + 1) * S], w_hi[n][:, kc, c * P:(c + 1) * P],
                                       w_lo[n][:, kc, c * P:(c + 1) * P], src_hi[:, kc, :], src_lo[:, kc, :],
                                       kc == 0, kc == KC - 1)
                    last.then_inc(proj[n], 1)

                def v_tile(t):
                    bank = shared(use, f"v{t}", i)
                    if isinstance(i, int) and i == 0 and t == 0:
                        pe.wait_ge(w_lo_done, 6)
                        pe.wait_ge(w_hi_done, 6)
                    for kc in range(KC):
                        last = mm3(bank[:], ctx_hi[:, kc, t * P:(t + 1) * P], ctx_lo[:, kc, t * P:(t + 1) * P],
                                   w_hi["v"][:, kc, :], w_lo["v"][:, kc, :], kc == 0, kc == KC - 1)
                    last.then_inc(v_done, 1)

                def scores(u):
                    c, q = divmod(u, QT)
                    if u == 0:
                        for n in "kq":
                            pe.wait_ge(hi_s[n], i + 1)
                            pe.wait_ge(lo_s[n], i + 1)
                    need(pe, exp_done, UNITS * i + u - 1)
                    for n, g in enumerate((0, 2, 1, 3)):
                        if n >= 2:
                            pe.wait_ge(head_done, (HC - 1) * (UNITS * i + u) + n - 1)
                        r = slice(g * HEAD_DIM, (g + 1) * HEAD_DIM)
                        last = mm3(scores_ps[u % 2][:, g, :], hT["q"][0][r, c, q * P:(q + 1) * P],
                                   hT["q"][1][r, c, q * P:(q + 1) * P], hT["k"][0][r, c, :], hT["k"][1][r, c, :],
                                   True, True)
                        last.then_inc(scores_done if n == HC - 1 else head_done, 1)

                def turn_probs(u):
                    pe.wait_ge(probs_done, UNITS * i + u + 1)
                    need(pe, p_lo_s, UNITS * i + u)
                    for g in range(HC):
                        for t in range(KT):
                            last = pe.transpose(pT_ps[:, g * KT + t, :], probs[:, u % 2, g, t * P:(t + 1) * P], ident)
                    last.then_inc(p_turned, 1)

                def pv(b, c):
                    pe.wait_ge(p_hi_s, UNITS * b + 2 * c + 2)
                    pe.wait_ge(p_lo_s, UNITS * b + 2 * c + 2)
                    if c == 0:
                        pe.wait_ge(v_hi_s, KT * b + KT)
                        pe.wait_ge(v_lo_s, KT * b + KT)
                    bank = shared(use, f"pv{c}", i)
                    hi, lo = v_hi[:].rearrange("p t h n -> p t (h n)"), v_lo[:].rearrange("p t h n -> p t (h n)")
                    for g in range(HC):
                        w = slice((c * HC + g) * P - g * HEAD_DIM, (c * HC + g) * P - g * HEAD_DIM + P)
                        for t in range(KT):
                            last = mm3(bank[:, 0:S], hi[:, t, w], lo[:, t, w], pT_hi[:, g * KT + t, :],
                                       pT_lo[:, g * KT + t, :], g == 0 and t == 0, g == HC - 1 and t == KT - 1)
                    last.then_inc(pv_done, 1)

                def o_tile(q):
                    b = i - 1
                    pe.wait_ge(a_hi_s, KC * b + KC)
                    pe.wait_ge(a_lo_s, KC * b + KC)
                    bank = shared(use, f"o{q}", i, a_lo_s)
                    for c in range(KC):
                        last = mm3(bank[:], aT_hi[:, c, q * P:(q + 1) * P], aT_lo[:, c, q * P:(q + 1) * P],
                                   w_hi["o"][:, c, :], w_lo["o"][:, c, :], c == 0, c == KC - 1)
                    last.then_inc(o_done, 1)

                def logits():
                    b = i - 1
                    pe.wait_ge(n_hi_s, QT * b + QT)
                    pe.wait_ge(n_lo_s, QT * b + QT)
                    bank = shared(use, "logits", i, n_lo_s)
                    for q in range(QT):
                        for c in range(KC):
                            last = mm3(bank[:, q * E:(q + 1) * E], tT_hi[:, c, q * P:(q + 1) * P],
                                       tT_lo[:, c, q * P:(q + 1) * P], gate_hi[:, c, :], gate_lo[:, c, :],
                                       c == 0, c == KC - 1)
                    last.then_inc(logits_done, 1)

                def sum_squares(n):
                    pe.wait_ge(sqsum_s[n], i + 2)
                    bank = shared(use, f"ss{n}", i)
                    pe.matmul(bank[:, 0:S], ones, sq_sum[:], start=True, stop=True).then_inc(ss_s[n], 1)

                def positions():
                    b = i - 1
                    pe.wait_ge(mask_s, b + 1)
                    bank = shared(use, "pos", i)
                    for q in range(QT):
                        o = bank[:, q * E:(q + 1) * E]
                        pe.matmul(o, tri_b[:], mask_b[:, q, :], start=True, stop=False)
                        for r in range(q):
                            pe.matmul(o, ones_b[:], mask_b[:, r, :], start=False, stop=False)
                        last = pe.matmul(o, ones_b[:], seen_b[:], start=False, stop=True)
                    last.then_inc(pos_done, 1)

                att, post, prep = kind.attend, kind.post, kind.prep
                if att:
                    v_tile(0)
                    scores(0)
                if post:
                    pv(i - 1, 3)
                if att:
                    scores(1)
                    v_tile(1)
                if post:
                    if isinstance(i, int) and i == 1:
                        pe.wait_ge(w_hi_done, 8)
                        pe.wait_ge(w_lo_done, 8)
                    o_tile(0)
                if att:
                    scores(2)
                    turn_probs(0)
                if post:
                    o_tile(1)
                if att:
                    scores(3)
                    turn_probs(1)
                if prep:
                    if isinstance(i, int) and i < 0:
                        pe.wait_ge(w_hi_done, 4)
                        pe.wait_ge(w_lo_done, 4)
                        pe.wait_ge(in_sem, 16)
                    pe.wait_ge(ctx_hi_s, i + 2)
                    pe.wait_ge(ctx_lo_s, i + 2)
                    project("k", "k01", 0)
                    project("k", "k23", 1)
                if att:
                    pv(i, 0)
                    scores(4)
                    turn_probs(2)
                if post:
                    for q in range(QT):
                        pe.wait_ge(xn2_s, QT * (i - 1) + q + 1)
                        turn(use, f"nT{q}", xn2, q, i).then_inc(n_turned, 1)
                    logits()
                if att:
                    scores(5)
                    turn_probs(3)
                if prep:
                    for q in range(QT):
                        pe.wait_ge(xn_s, QT * (i + 1) + q + 1)
                        turn(use, f"xT{q}", x_raw, q, i).then_inc(x_turned, 1)
                    pe.wait_ge(x_hi_s, QT * (i + 1) + QT)
                    pe.wait_ge(x_lo_s, QT * (i + 1) + QT)
                    project("q", "q01", 0)
                if att:
                    pv(i, 1)
                    scores(6)
                    turn_probs(4)
                if prep:
                    sum_squares("k")
                if att:
                    scores(7)
                    turn_probs(5)
                if prep:
                    project("q", "q23", 1)
                if att:
                    pv(i, 2)
                    turn_probs(6)
                if post:
                    positions()
                if att:
                    turn_probs(7)
                if prep:
                    sum_squares("q")

            pipeline(pe, body)
            pe.wait_ge(scat_rdy, B)
            pe.wait_ge(pos_read, B)
            bank = plans[-2]["pos"][0]
            pe.transpose(shared_ps[bank][0:E, 0:P], last_tok[:], ident).then_inc(lastT_s, 1)

        @block.scalar
        def _(act):
            act.preload_act_table_set("natural_log_exp_and_others")
            for n, (w, h) in enumerate(halves):
                act.wait_ge(stage_in[n % 2], 16 * (n // 2 + 1))
                act.copy(w_hi[w][:, 2 * h:2 * h + 2, :].rearrange("p c n -> p (c n)"),
                         stage[n % 2][:].rearrange("p c t -> p (c t)")).then_inc(w_hi_done, 1)
            act.wait_ge(vec_sem, 48)
            act.wait_ge(setup_p, 3)

            def body(i, kind, use):
                def exp_unit(u):
                    act.wait_ge(max_done, UNITS * i + u + 1)
                    need(act, p_turned, UNITS * i + u - 1)
                    need(act, inv_done, UNITS * i + u - 1)
                    for g in range(HC):
                        last = act.activation(probs[:, u % 2, g, :], scores_ps[u % 2][:, g, :], ACT.Exp,
                                              bias=neg_max[:, u % 2, g:g + 1], scale=SCALE,
                                              accum_out=row_sum[:, u % 2, g:g + 1])
                    last.then_inc(exp_done, 1)

                def turned_hi(u):
                    q = u % QT
                    act.wait_ge(p_turned, UNITS * i + u + 1)
                    act.copy(pT_hi[:, :, q * P:(q + 1) * P], pT_ps[:]).then_inc(p_hi_s, 1)

                def attended_hi(b, c):
                    bank = use[f"pv{c}"][0]
                    act.wait_ge(pv_done, KC * b + c + 1)
                    act.activation(aT_hi[:, c, :], shared_ps[bank][:, 0:S], ACT.Identity,
                                   bias=vecs[:, 4, c:c + 1]).then_inc(a_hi_s, 1)

                def v_part(t):
                    bank = use[f"v{t}"][0]
                    act.wait_ge(v_done, KT * i + t + 1)
                    need(act, pv_done, KC * i)
                    act.copy(v_hi[:, t, :, 0:HEAD_DIM],
                             shared_ps[bank][:].rearrange("p (h n) -> p h n", n=HEAD_DIM)).then_inc(v_hi_s, 1)

                def biased(n, pair):
                    bank = use[f"{n}{2 * pair}{2 * pair + 1}"][0]
                    b = i + 1
                    act.wait_ge(proj[n], 2 * b + pair + 1)
                    if pair == 0:
                        need(act, lo_s[n], b)
                    if isinstance(i, int) and i < 0 and pair == 0:
                        act.wait_ge(w_lo_done, len(halves))
                    bias = 2 if n == "k" else 0
                    for j in range(2):
                        c = 2 * pair + j
                        last = act.activation(full[n][:, c, :], shared_ps[bank][:, j * S:(j + 1) * S], ACT.Identity,
                                              bias=vecs[:, bias, c:c + 1])
                        last.then_inc(full_s[n], 1)

                def squared(n):
                    b = i + 1
                    act.wait_ge(full_s[n], KC * b + KC)
                    if n == "k":
                        need(act, xn2_out, 16 * i)
                        need(act, n_turned, QT * i)
                        need(act, sqsum_s["q"], b)
                    else:
                        act.wait_ge(sqsum_s["k"], b + 1)
                    act.activation(xn2[:].rearrange("p q n -> p (q n)"), full[n][:].rearrange("p c t -> p (c t)"),
                                   ACT.Square).then_inc(sq_s[n], 1)

                def rms_guess(n):
                    act.wait_ge(ms_s[n], i + 2)
                    act.activation(rms_a[:], sq_sum[:], ACT.Ln).then_inc(ln_s[n], 1)
                    act.wait_ge(ln_s[n], i + 2)
                    act.activation(rms_a[:], rms_a[:], ACT.Exp, scale=-0.5).then_inc(ry_s[n], 1)

                def normed_hi(n):
                    need(act, scores_done, UNITS * (i + 1))
                    act.wait_ge(fin_s[n], KC * (i + 2))
                    act.copy(hT[n][0][:], full[n][:]).then_inc(hi_s[n], 1)

                att, post, prep = kind.attend, kind.post, kind.prep
                if att:
                    exp_unit(0)
                if post:
                    attended_hi(i - 1, 3)
                if att:
                    v_part(0)
                    exp_unit(1)
                    v_part(1)
                    turned_hi(0)
                    exp_unit(2)
                if prep:
                    act.wait_ge(ctx_in, 16 * (i + 2))
                    need(act, v_done, KT * (i + 1))
                    act.copy(ctx_hi[:], ctx_raw[:]).then_inc(ctx_hi_s, 1)
                if att:
                    turned_hi(1)
                    exp_unit(3)
                if prep:
                    biased("k", 0)
                    biased("k", 1)
                if att:
                    attended_hi(i, 0)
                    turned_hi(2)
                    exp_unit(4)
                if post:
                    for q in range(QT):
                        bank = use[f"nT{q}"][0]
                        act.wait_ge(n_turned, QT * (i - 1) + q + 1)
                        act.copy(tT_hi[:, :, q * P:(q + 1) * P],
                                 shared_ps[bank][:].rearrange("p (c t) -> p c t", c=KC)).then_inc(n_hi_s, 1)
                if prep:
                    squared("k")
                if att:
                    turned_hi(3)
                    exp_unit(5)
                if post:
                    bank = use["logits"][0]
                    act.wait_ge(lgmax_s, i)
                    for q in range(QT):
                        last = act.activation(score[:, q, :], shared_ps[bank][:, q * E:(q + 1) * E], ACT.Exp,
                                              bias=lg_max[:, q:q + 1], accum_out=lg_sum[:, q:q + 1])
                    last.then_inc(lgexp_s, 1)
                if prep:
                    for q in range(QT):
                        bank = use[f"xT{q}"][0]
                        act.wait_ge(x_turned, QT * (i + 1) + q + 1)
                        act.copy(tT_hi[:, :, q * P:(q + 1) * P],
                                 shared_ps[bank][:].rearrange("p (c t) -> p c t", c=KC)).then_inc(x_hi_s, 1)
                    biased("q", 0)
                if att:
                    attended_hi(i, 1)
                    turned_hi(4)
                    exp_unit(6)
                if prep:
                    rms_guess("k")
                if att:
                    turned_hi(5)
                    exp_unit(7)
                if prep:
                    biased("q", 1)
                    normed_hi("k")
                    squared("q")
                if att:
                    attended_hi(i, 2)
                    turned_hi(6)
                    turned_hi(7)
                if prep:
                    rms_guess("q")
                    normed_hi("q")

            pipeline(act, body)

        @block.vector
        def _(v):
            class Chain:

                def __init__(self, name, per, b):
                    self.sem, self.per, self.b, self.n = chain[name], per, b, 0

                def step(self, ins):
                    self.n += 1
                    ins.then_inc(self.sem, 1)
                    v.wait_ge(self.sem, self.per * self.b + self.n)

            def settle(n):
                v.memset(settled[0:1, n:n + 1], 0.0)

            PREP_STEPS, POST_STEPS = 10, 27
            v.memset(seen[:], 0.0)
            v.memset(seen_b[:], 0.0)
            v.memset(last_tok[:], 0.0)
            setup = Chain("setup", 0, 0)
            v.wait_ge(in_sem, 16)
            v.tensor_copy(tri_b[:], consts[:, P:2 * P])
            v.tensor_copy(ones_b[:], ones)
            v.wait_ge(vec_sem, 48)
            raw = x2[:, 0, 0:KC * E].rearrange("p (c e) -> p c e", c=KC)
            setup.step(v.tensor_copy(gate_hi[:], raw))
            v.tensor_tensor(gate_lo[:], raw, gate_hi[:].bitcast(F32), ALU.subtract).then_inc(gate_split, 1)
            for n, (w, h) in enumerate(halves):
                v.wait_ge(w_hi_done, n + 1)
                c = slice(2 * h, 2 * h + 2)
                v.tensor_tensor(w_lo[w][:, c, :].rearrange("p c n -> p (c n)"),
                                stage[n % 2][:].rearrange("p c t -> p (c t)"),
                                w_hi[w][:, c, :].rearrange("p c n -> p (c n)").bitcast(F32),
                                ALU.subtract).then_inc(w_lo_done, 1)

            def body(i, kind, use):
                prep, attend, post = Chain("prep", PREP_STEPS, i + 1), Chain("attend", UNITS, i), Chain("post", POST_STEPS, i - 1)

                def unit_max(u):
                    v.wait_ge(scores_done, UNITS * i + u + 1)
                    attend.step(v.tensor_reduce(row_max[:, u % 2, :], scores_ps[u % 2][:], X, ALU.max))
                    need(v, exp_done, UNITS * i + u - 1)
                    v.tensor_scalar(neg_max[:, u % 2, :], row_max[:, u % 2, :], -SCALE, None,
                                    ALU.mult).then_inc(max_done, 1)

                def unit_inv(u):
                    v.wait_ge(exp_done, UNITS * i + u + 1)
                    need(v, probs_done, UNITS * i + u - 1)
                    v.reciprocal(row_inv[:, u % 2, :], row_sum[:, u % 2, :]).then_inc(inv_done, 1)

                def turned_lo(u):
                    c = slice((u % QT) * P, (u % QT + 1) * P)
                    v.wait_ge(p_hi_s, UNITS * i + u + 1)
                    v.tensor_tensor(pT_lo[:, :, c], pT_ps[:], pT_hi[:, :, c].bitcast(F32),
                                    ALU.subtract).then_inc(p_lo_s, 1)

                def attended_lo(b, c):
                    bank = use[f"pv{c}"][0]
                    v.wait_ge(a_hi_s, KC * b + c + 1)
                    v.scalar_tensor_tensor(aT_lo[:, c, :], shared_ps[bank][:, 0:S], vecs[:, 4, c:c + 1],
                                           aT_hi[:, c, :].bitcast(F32), ALU.add, ALU.subtract).then_inc(a_lo_s, 1)

                def v_part(t):
                    bank = use[f"v{t}"][0]
                    v.wait_ge(v_hi_s, KT * i + t + 1)
                    v.tensor_tensor(v_lo[:, t, :, 0:HEAD_DIM],
                                    shared_ps[bank][:].rearrange("p (h n) -> p h n", n=HEAD_DIM),
                                    v_hi[:, t, :, 0:HEAD_DIM].bitcast(F32), ALU.subtract).then_inc(v_lo_s, 1)

                def ln_stats_of(src, stats, mv, var, ch, at):
                    for q in range(QT):
                        last = v.bn_stats(stats[:, q, :], src[:, q, :])
                    ch.step(last)
                    settle(at)
                    for q in range(QT):
                        last = v.bn_aggr(mv[:, q, :], stats[:, q, :])
                    ch.step(last)
                    return v.tensor_scalar(var[:], mv[:, :, 1], LN_EPS, None, ALU.add)

                def squares_summed(n):
                    v.wait_ge(sq_s[n], i + 2)
                    v.tensor_reduce(sq_sum[:], xn2[:].rearrange("p q n -> p (q n)")
                                    .rearrange("p (c t) -> p t c", c=KC), X, ALU.add).then_inc(sqsum_s[n], 1)

                def mean_square(n):
                    bank = use[f"ss{n}"][0]
                    v.wait_ge(ss_s[n], i + 2)
                    v.tensor_scalar(sq_sum[:], shared_ps[bank][:, 0:S], 1.0 / D, RMS_EPS, ALU.mult,
                                    ALU.add).then_inc(ms_s[n], 1)

                def normed(n):
                    v.wait_ge(ry_s[n], i + 2)
                    prep.step(v.tensor_tensor(rms_b[:], rms_a[:], rms_a[:], ALU.mult))
                    prep.step(v.tensor_tensor(rms_b[:], rms_b[:], sq_sum[:], ALU.mult))
                    prep.step(v.tensor_scalar(rms_b[:], rms_b[:], -0.5, 1.5, ALU.mult, ALU.add))
                    prep.step(v.tensor_tensor(rms_b[:], rms_b[:], rms_a[:], ALU.mult))
                    gain = 3 if n == "k" else 1
                    for c in range(KC):
                        v.scalar_tensor_tensor(full[n][:, c, :], full[n][:, c, :], vecs[:, gain, c:c + 1], rms_b[:],
                                               ALU.mult, ALU.mult).then_inc(fin_s[n], 1)

                if kind.attend:
                    unit_max(0)
                if kind.post:
                    attended_lo(i - 1, 3)
                if kind.attend:
                    v_part(0)
                    unit_inv(0)
                    unit_max(1)
                    v_part(1)
                    unit_inv(1)
                if kind.post:
                    v.wait_ge(bo_added, i)
                    v.wait_ge(o_done, QT * (i - 1) + 1)
                    v.tensor_tensor(x2[:, 0, :], shared_ps[use["o0"][0]][:], x2[:, 0, :], ALU.add).then_inc(x2_s, 1)
                if kind.attend:
                    unit_max(2)
                    turned_lo(0)
                    unit_inv(2)
                if kind.post:
                    v.wait_ge(o_done, QT * (i - 1) + 2)
                    v.tensor_tensor(x2[:, 1, :], shared_ps[use["o1"][0]][:], x2[:, 1, :], ALU.add).then_inc(x2_s, 1)
                    v.wait_ge(x2_s, QT * i)
                    ln_stats_of(x2, n2_stats, n2_mv, n2_var, post, 0).then_inc(stats2, 1)
                if kind.attend:
                    unit_max(3)
                    turned_lo(1)
                if kind.post:
                    v.wait_ge(rstd2, i)
                    need(v, xn2_out, 16 * (i - 1))
                    for q in range(QT):
                        v.tensor_scalar(xn2[:, q, :], x2[:, q, :], n2_mv[:, q, 0:1], n2_rstd[:, q:q + 1],
                                        ALU.subtract, ALU.mult).then_inc(xn2_s, 1)
                if kind.prep:
                    v.wait_ge(x_in, 16 * (i + 2))
                    ln_stats_of(x_raw, ln_stats, ln_mv, ln_var, prep, 1).then_inc(stats1, 1)
                if kind.attend:
                    unit_inv(3)
                    attended_lo(i, 0)
                    unit_max(4)
                    turned_lo(2)
                if kind.post:
                    for q in range(QT):
                        c = slice(q * P, (q + 1) * P)
                        v.wait_ge(n_hi_s, QT * (i - 1) + q + 1)
                        v.tensor_tensor(tT_lo[:, :, c], shared_ps[use[f"nT{q}"][0]][:]
                                        .rearrange("p (c t) -> p c t", c=KC), tT_hi[:, :, c].bitcast(F32),
                                        ALU.subtract).then_inc(n_lo_s, 1)
                if kind.prep:
                    v.wait_ge(rstd1, i + 2)
                    for q in range(QT):
                        v.tensor_scalar(x_raw[:, q, :], x_raw[:, q, :], ln_mv[:, q, 0:1], ln_rstd[:, q:q + 1],
                                        ALU.subtract, ALU.mult).then_inc(xn_s, 1)
                if kind.attend:
                    unit_inv(4)
                if kind.post:
                    v.wait_ge(logits_done, i)
                    post.step(v.tensor_reduce(lg_max[:], shared_ps[use["logits"][0]][:, 0:QT * E]
                                              .rearrange("p (q e) -> p q e", q=QT), X, ALU.max))
                    v.tensor_scalar(lg_max[:], lg_max[:], -1.0, None, ALU.mult).then_inc(lgmax_s, 1)
                if kind.attend:
                    unit_max(5)
                    turned_lo(3)
                if kind.prep:
                    for q in range(QT):
                        c = slice(q * P, (q + 1) * P)
                        v.wait_ge(x_hi_s, QT * (i + 1) + q + 1)
                        v.tensor_tensor(tT_lo[:, :, c], shared_ps[use[f"xT{q}"][0]][:]
                                        .rearrange("p (c t) -> p c t", c=KC), tT_hi[:, :, c].bitcast(F32),
                                        ALU.subtract).then_inc(x_lo_s, 1)
                    squares_summed("k")
                if kind.attend:
                    unit_inv(5)
                    attended_lo(i, 1)
                    unit_max(6)
                    turned_lo(4)
                    unit_inv(6)
                if kind.prep:
                    mean_square("k")
                    normed("k")
                if kind.attend:
                    unit_max(7)
                    turned_lo(5)
                    unit_inv(7)
                if kind.prep:
                    squares_summed("q")
                if kind.post:
                    v.wait_ge(lgexp_s, i)
                    post.step(v.reciprocal(lg_sum[:], lg_sum[:]))
                    post.step(v.tensor_tensor(score[:], score[:], lg_sum[:].unsqueeze(2).to_broadcast([P, QT, E]),
                                              ALU.mult))
                    groups = score[:].rearrange("p q e -> p (q e)").rearrange("p (g e) -> p g e", e=GE)
                    post.step(v.tensor_reduce(g_score[:].rearrange("p q g -> p (q g)"), groups, X, ALU.max))
                    settle(2)
                    for q in range(QT):
                        last = v.max(g_top[:, q, :], g_score[:, q, :])
                    post.step(last)
                    settle(3)
                    for q in range(QT):
                        last = v.max_index(g_idx[:, q, :], g_top[:, q, :], g_score[:, q, :])
                    post.step(last)
                    post.step(v.tensor_copy(g_idxf[:], g_idx[:]))
                    post.step(v.tensor_tensor(
                        g_hot[:], iota_g.unsqueeze(1).unsqueeze(1).to_broadcast([P, QT, TOPK_GROUP, N_GROUP]),
                        g_idxf[:, :, 0:TOPK_GROUP].unsqueeze(3).to_broadcast([P, QT, TOPK_GROUP, N_GROUP]),
                        ALU.is_equal))
                    post.step(v.tensor_reduce(g_mask[:], g_hot[:].rearrange("p q k g -> p q g k"), X, ALU.add))
                    post.step(v.tensor_tensor(groups, groups, g_mask[:].rearrange("p q g -> p (q g)").unsqueeze(2)
                                              .to_broadcast([P, QT * N_GROUP, GE]), ALU.mult))
                    settle(4)
                    for q in range(QT):
                        last = v.max(e_top[:, q, :], score[:, q, :])
                    post.step(last)
                if kind.attend:
                    attended_lo(i, 2)
                    turned_lo(6)
                if kind.post:
                    settle(5)
                    for q in range(QT):
                        last = v.max_index(e_idx[:, q, :], e_top[:, q, :], score[:, q, :])
                    post.step(last)
                    post.step(v.tensor_copy(e_idxf[:], e_idx[:]))
                    post.step(v.tensor_tensor(
                        e_hot[:], iota_e.unsqueeze(1).unsqueeze(1).to_broadcast([P, QT, TOP_K, E]),
                        e_idxf[:, :, 0:TOP_K].unsqueeze(3).to_broadcast([P, QT, TOP_K, E]), ALU.is_equal))
                    post.step(v.tensor_reduce(mask_f[:], e_hot[:].rearrange("p q k e -> p q e k"), X, ALU.add))
                    v.tensor_copy(mask_b[:], mask_f[:]).then_inc(mask_s, 1)
                    for q in range(QT):
                        post.step(v.scalar_tensor_tensor(last_tok[:], mask_f[:, q, :], tok_col[:, q:q + 1],
                                                         last_tok[:], ALU.mult, ALU.max))
                    v.tensor_copy(keep["weight"][:, bass.ds((i - 1) * QT * TOP_K, QT * TOP_K)]
                                  .rearrange("p (q k) -> p q k", q=QT), e_top[:, :, 0:TOP_K])
                    v.wait_ge(pos_done, i)
                    v.scalar_tensor_tensor(slot_val[:], shared_ps[use["pos"][0]][:, 0:QT * E]
                                           .rearrange("p (q e) -> p q e", q=QT), float(CAPACITY - 1),
                                           slot_base.unsqueeze(1).to_broadcast([P, QT, E]), ALU.min,
                                           ALU.add).then_inc(pos_read, 1)
                    for q in range(QT):
                        post.step(v.tensor_tensor(seen[:], seen[:], mask_f[:, q, :], ALU.add))
                    v.tensor_copy(seen_b[:], seen[:])
                    v.wait_ge(pos_read, i)
                    post.step(v.tensor_tensor(e_slot[:], e_hot[:], slot_val[:].unsqueeze(2)
                                              .to_broadcast([P, QT, TOP_K, E]), ALU.mult))
                    post.step(v.tensor_reduce(slot_f[:], e_slot[:], X, ALU.add))
                if kind.attend:
                    turned_lo(7)
                if kind.prep:
                    mean_square("q")
                    normed("q")
                if kind.post:
                    v.tensor_copy(keep["slot"][:, bass.ds((i - 1) * QT * TOP_K, QT * TOP_K)],
                                  slot_f[:].rearrange("p q k -> p (q k)"))
                    post.step(v.tensor_scalar(last_slot[:], e_idxf[:, :, 0:TOP_K], float(CAPACITY),
                                              float(CAPACITY - 1), ALU.mult, ALU.add))
                    post.step(v.tensor_tensor(is_last[:], slot_f[:], last_slot[:], ALU.is_equal))
                    post.step(v.scalar_tensor_tensor(scat_f[:], is_last[:], OVER, slot_f[:], ALU.mult, ALU.add))
                    need(v, scattered, 16 * QT * TOP_K * (i - 1))
                    v.tensor_copy(scat_idx[:], scat_f[:].rearrange("p q k -> p (q k)"))
                    v.tensor_scalar(scat_tok[:], tok_col, -1.0, None, ALU.add).then_inc(scat_rdy, 1)
                    post.step(v.tensor_scalar(tok_col, tok_col, float(S), None, ALU.add))
                assert prep.n in (0, PREP_STEPS) and attend.n in (0, UNITS) and post.n in (0, POST_STEPS)

            pipeline(v, body)
            v.wait_ge(lastT_s, 1)
            bank = plans[-2]["pos"][0]
            end = Chain("setup", 1, 1)
            end.step(v.tensor_reduce(lastT[:], shared_ps[bank][0:E, 0:P], X, ALU.max))
            end.step(v.tensor_scalar(lastT[:], lastT[:], -1.0, 0.0, ALU.add, ALU.max))
            v.tensor_copy(lastT_i[:], lastT[:]).then_inc(last_i_s, 1)

        @block.gpsimd
        def _(g):
            g.memset(zero_i[:], 0).then_inc(setup_p, 1)
            g.memset(v_hi[:].bitcast(F32), 0.0).then_inc(setup_p, 1)
            g.memset(v_lo[:].bitcast(F32), 0.0).then_inc(setup_p, 1)
            g.memset(minus_half[:], -0.5).then_inc(setup_p, 1)
            g.wait_ge(setup_p, 4)
            g.wait_ge(vec_sem, 48)
            g.wait_ge(table_zeroed, 16)

            def body(i, kind, use):
                def norm_unit(u):
                    g.wait_ge(inv_done, UNITS * i + u + 1)
                    pr = probs[:, u % 2, :, :]
                    g.tensor_tensor(pr, pr, row_inv[:, u % 2, :].unsqueeze(2).to_broadcast([P, HC, CK]),
                                    ALU.mult).then_inc(probs_done, 1)

                def normed_lo(n):
                    g.wait_ge(hi_s[n], i + 2)
                    g.tensor_tensor(hT[n][1][:], full[n][:], hT[n][0][:].bitcast(F32), ALU.subtract).then_inc(lo_s[n], 1)

                def scatter(s):
                    if not kind.scatter:
                        return
                    for j in (2 * s, 2 * s + 1):
                        q = j // TOP_K
                        g.indirect_dma_start(
                            out=d["table"], out_offset=bass.IndirectOffsetOnAxis(ap=scat_idx[:, j:j + 1], axis=0),
                            in_=scat_tok[:, q:q + 1], in_offset=None, bounds_check=E * CAPACITY - 1,
                            oob_is_err=False).then_inc(scattered, 16)

                if kind.post:
                    g.wait_ge(res_in, 16 * i)
                    g.tensor_tensor(x2[:], x2[:], bo_row[:].unsqueeze(1).to_broadcast([P, QT, D]),
                                    ALU.add).then_inc(bo_added, 1)
                if kind.scatter:
                    g.wait_ge(scat_rdy, i - 1)
                if kind.attend:
                    norm_unit(0)
                scatter(0)
                if kind.attend:
                    norm_unit(1)
                scatter(1)
                if kind.prep:
                    g.wait_ge(ctx_hi_s, i + 2)
                    g.tensor_tensor(ctx_lo[:], ctx_raw[:], ctx_hi[:].bitcast(F32), ALU.subtract).then_inc(ctx_lo_s, 1)
                if kind.post:
                    g.wait_ge(stats2, i)
                    g.tensor_tensor(n2_rstd[:], n2_var[:], minus_half[:], ALU.pow).then_inc(rstd2, 1)
                if kind.attend:
                    norm_unit(2)
                if kind.prep:
                    g.wait_ge(stats1, i + 2)
                    g.tensor_tensor(ln_rstd[:], ln_var[:], minus_half[:], ALU.pow).then_inc(rstd1, 1)
                if kind.attend:
                    norm_unit(3)
                scatter(2)
                if kind.attend:
                    norm_unit(4)
                scatter(3)
                if kind.attend:
                    norm_unit(5)
                scatter(4)
                if kind.attend:
                    norm_unit(6)
                scatter(5)
                if kind.prep:
                    normed_lo("k")
                if kind.attend:
                    norm_unit(7)
                if kind.prep:
                    normed_lo("q")

            pipeline(g, body)
            g.wait_ge(scattered, 16 * QT * TOP_K * B)


def phase_b(nc, d):
    E = d["experts"].shape[0]
    D = d["xn2"].shape[-1]
    KC = D // P
    M = d["m"]
    ROWS = CAPACITY // 2
    MC = -(-M // P)
    col = [min(m * P, M - P) for m in range(MC)]
    GU, DN = 2 * KC * M, MC * D

    with ExitStack() as ctx:
        def sb(name, shape, dt=F32):
            return ctx.enter_context(nc.sbuf_tensor(name, shape, dt))

        def ps(name, shape, dt=F32):
            return ctx.enter_context(nc.psum_tensor(name, shape, dt))

        def sem(name):
            return ctx.enter_context(nc.semaphore(name))

        ident = sb("b_ident", [P, P])
        table_i, table_f = sb("table_i", [P, ROWS], I32), sb("table_f", [P, ROWS])
        idxT = sb("idxT", [ROWS, 2 * E], I32)
        idx_now = sb("idx_now", [ROWS, 2, 2], I32)
        rows = sb("rows", [ROWS, 2, 2, D])
        gu_raw, dn_raw = sb("gu_raw", [P, 2, GU]), sb("dn_raw", [P, 2, DN])
        gu_hi, gu_lo = sb("gu_hi", [P, 2, GU], F32R), sb("gu_lo", [P, 2, GU], F32R)
        dn_hi, dn_lo = sb("dn_hi", [P, 2, MC, D], F32R), sb("dn_lo", [P, 2, MC, D], F32R)
        bT_hi, bT_lo = sb("bT_hi", [P, 2, KC, CAPACITY], F32R), sb("bT_lo", [P, 2, KC, CAPACITY], F32R)
        gate_act, hid = sb("gate_act", [P, MC, CAPACITY]), sb("hid", [P, MC, CAPACITY])
        h_hi, h_lo = sb("h_hi", [P, 2, MC, CAPACITY], F32R), sb("h_lo", [P, 2, MC, CAPACITY], F32R)
        out_rows = sb("out_rows", [ROWS, 2, 2, D])

        gu_ps = [ps(f"gu_ps{m}", [P, 512]) for m in range(MC)]
        bT_ps = [ps(f"bT_ps{n}", [P, 512]) for n in range(2)]
        dn_ps = [ps(f"dn_ps{t}", [P, 512]) for t in range(2)]

        setup_in, idx_f_s, idx_turned, idx_s = (sem("b_table_loaded"), sem("b_table_float"), sem("b_table_turned"),
                                                sem("b_index_ready"))
        gu_in, dn_in, rows_in, stored = ([sem(f"b_{what}{n}") for n in range(2)]
                                         for what in ("gu_loaded", "down_loaded", "rows_gathered", "out_stored"))
        staged = sem("b_index_staged")
        turned, bT_hi_s, bT_lo_s = sem("b_rows_turned"), sem("b_rowsT_hi_done"), sem("b_rowsT_lo_done")
        gu_hi_s, gu_lo_s = sem("b_gu_hi_done"), sem("b_gu_lo_done")
        dn_hi_s, dn_lo_s = sem("b_down_hi_done"), sem("b_down_lo_done")
        gu_done, act_s, hid_s = sem("b_gu_product_done"), sem("b_silu_done"), sem("b_hidden_done")
        h_hi_s, h_lo_s = sem("b_hidden_hi_done"), sem("b_hidden_lo_done")
        dn_done, out_s = sem("b_down_product_done"), sem("b_out_copied")

        def pipeline(eng, body):
            for e in (-1, 0, 1, 2):
                body(e, e % 2, e // 2)
            with eng.Fori(0, (E - 6) // 2) as j:
                for s in range(2):
                    body(2 * j + (3 + s), (3 + s) % 2, j + (3 + s) // 2)
            for e in (E - 3, E - 2, E - 1, E):
                body(e, e % 2, e // 2)

        def at_most(e, last):
            return not isinstance(e, int) or e <= last

        def at_least(e, first):
            return not isinstance(e, int) or e >= first

        block = ctx.enter_context(nc.Block())

        @block.sync
        def _(sp):
            sp.dma_start(table_i[:], d["table"].rearrange("(k r) o -> k (r o)", r=ROWS)).then_inc(setup_in, 16)
            sp.dma_start(ident[:], d["consts"][:, 0:P]).then_inc(setup_in, 16)

            def body(e, par, half):
                if not at_most(e, E - 2):
                    return
                need(sp, gu_hi_s, e)
                need(sp, gu_lo_s, e)
                sp.dma_start(gu_raw[:, 1 - par, :], d["experts"][e + 1][:, 0:GU]).then_inc(gu_in[1 - par], 16)
                need(sp, dn_hi_s, e)
                need(sp, dn_lo_s, e)
                sp.dma_start(dn_raw[:, 1 - par, :], d["experts"][e + 1][:, GU:GU + DN]).then_inc(dn_in[1 - par], 16)

            pipeline(sp, body)

        @block.tensor
        def _(pe):
            def mm3(out, a_hi, a_lo, b_hi, b_lo, first, last):
                pe.matmul(out, a_hi, b_hi, start=first, stop=False)
                pe.matmul(out, a_hi, b_lo, start=False, stop=False)
                return pe.matmul(out, a_lo, b_hi, start=False, stop=last)

            pe.wait_ge(setup_in, 32)
            pe.wait_ge(idx_f_s, 1)
            pe.transpose(bT_ps[0][0:ROWS, 0:P], table_f[:], ident[:]).then_inc(idx_turned, 1)

            def body(e, par, half):
                def turn_rows():
                    nxt = 1 - par
                    pe.wait_ge(rows_in[nxt], 32 * (half + par + 1))
                    if isinstance(e, int) and e < 0:
                        pe.wait_ge(idx_s, 1)
                    for n in range(2):
                        need(pe, bT_lo_s, 2 * e + n + 1 if at_least(e, 0) else 0)
                        for k in range(2):
                            for t in range(2):
                                c = (2 * n + k) * P
                                last = pe.transpose(bT_ps[n][:, k * CAPACITY + t * ROWS:k * CAPACITY + (t + 1) * ROWS],
                                                    rows[:, nxt, t, c:c + P], ident[0:ROWS, 0:ROWS])
                        last.then_inc(turned, 1)

                def gate_up(m):
                    if m == 0:
                        pe.wait_ge(bT_lo_s, 2 * (e + 1))
                        pe.wait_ge(gu_hi_s, e + 1)
                        pe.wait_ge(gu_lo_s, e + 1)
                    need(pe, hid_s, MC * e + (m + 1 - MC) if at_least(e, 1) else 0)
                    for g in range(2):
                        for kc in range(KC):
                            w = (g * KC + kc) * M + col[m]
                            last = mm3(gu_ps[m][:, g * CAPACITY:(g + 1) * CAPACITY], gu_hi[:, par, w:w + P],
                                       gu_lo[:, par, w:w + P], bT_hi[:, par, kc, :], bT_lo[:, par, kc, :],
                                       kc == 0, kc == KC - 1)
                    last.then_inc(gu_done, 1)

                def down(t):
                    o = 1 - par
                    if t == 0:
                        pe.wait_ge(h_lo_s, MC * e)
                        pe.wait_ge(dn_hi_s, e)
                        pe.wait_ge(dn_lo_s, e)
                    need(pe, out_s, 2 * e + (t - 3))
                    r = slice(t * ROWS, (t + 1) * ROWS)
                    for m in range(MC):
                        last = mm3(dn_ps[t][0:ROWS, :], h_hi[:, o, m, r], h_lo[:, o, m, r], dn_hi[:, o, m, :],
                                   dn_lo[:, o, m, :], m == 0, m == MC - 1)
                    last.then_inc(dn_done, 1)

                mid = at_least(e, 0) and at_most(e, E - 1)
                if mid:
                    gate_up(0)
                if at_most(e, E - 2):
                    turn_rows()
                if mid:
                    gate_up(1)
                    gate_up(2)
                if at_least(e, 1):
                    down(0)
                    down(1)

            pipeline(pe, body)

        @block.scalar
        def _(act):
            def body(e, par, half):
                ahead, mid, late = at_most(e, E - 2), at_least(e, 0) and at_most(e, E - 1), at_least(e, 1)

                def rows_hi(n):
                    act.wait_ge(turned, 2 * e + (n + 3))
                    act.copy(bT_hi[:, 1 - par, 2 * n:2 * n + 2, :].rearrange("p k t -> p (k t)"),
                             bT_ps[n][:, 0:2 * CAPACITY]).then_inc(bT_hi_s, 1)

                def silu(m):
                    act.wait_ge(gu_done, MC * e + (m + 1))
                    act.activation(gate_act[:, m, :], gu_ps[m][:, 0:CAPACITY], ACT.Silu).then_inc(act_s, 1)

                def hidden_hi(m):
                    act.wait_ge(hid_s, MC * e + (m + 1))
                    act.copy(h_hi[:, par, m, :], hid[:, m, :]).then_inc(h_hi_s, 1)

                if mid:
                    silu(0)
                if ahead:
                    rows_hi(0)
                    rows_hi(1)
                if mid:
                    hidden_hi(0)
                if ahead:
                    act.wait_ge(gu_in[1 - par], 16 * (half + par + 1))
                    act.copy(gu_hi[:, 1 - par, :], gu_raw[:, 1 - par, :]).then_inc(gu_hi_s, 1)
                if mid:
                    silu(1)
                    hidden_hi(1)
                    act.wait_ge(dn_in[par], 16 * (half + 1))
                    act.copy(dn_hi[:, par, :, :].rearrange("p m n -> p (m n)"), dn_raw[:, par, :]).then_inc(dn_hi_s, 1)
                    silu(2)
                    hidden_hi(2)
                if late:
                    o = 1 - par
                    need(act, stored[o], 16 * (half + par - 1))
                    for t in range(2):
                        act.wait_ge(dn_done, 2 * e + (t - 1))
                        act.copy(out_rows[:, o, t, :], dn_ps[t][0:ROWS, :]).then_inc(out_s, 1)
                    act.wait_ge(out_s, 2 * e)
                    act.dma_start(d["eo"].rearrange("(e t r) n -> e r t n", t=2, r=ROWS)[e - 1],
                                  out_rows[:, o, :, :]).then_inc(stored[o], 16)

            pipeline(act, body)
            for n in range(2):
                act.wait_ge(stored[n], 16 * (E // 2))

        @block.vector
        def _(v):
            v.wait_ge(setup_in, 32)
            v.tensor_copy(table_f[:], table_i[:]).then_inc(idx_f_s, 1)
            v.wait_ge(idx_turned, 1)
            v.tensor_copy(idxT[:, 0:2 * E], bT_ps[0][0:ROWS, 0:P]).then_inc(idx_s, 1)

            def body(e, par, half):
                ahead, mid = at_most(e, E - 2), at_least(e, 0) and at_most(e, E - 1)

                def hidden(m):
                    v.wait_ge(act_s, MC * e + (m + 1))
                    v.tensor_tensor(hid[:, m, :], gate_act[:, m, :], gu_ps[m][:, CAPACITY:2 * CAPACITY],
                                    ALU.mult).then_inc(hid_s, 1)

                def hidden_lo(m):
                    v.wait_ge(h_hi_s, MC * e + (m + 1))
                    v.tensor_tensor(h_lo[:, par, m, :], hid[:, m, :], h_hi[:, par, m, :].bitcast(F32),
                                    ALU.subtract).then_inc(h_lo_s, 1)

                if mid:
                    hidden(0)
                if ahead:
                    for n in range(2):
                        v.wait_ge(bT_hi_s, 2 * e + (n + 3))
                        v.tensor_tensor(bT_lo[:, 1 - par, 2 * n:2 * n + 2, :].rearrange("p k t -> p (k t)"),
                                        bT_ps[n][:, 0:2 * CAPACITY],
                                        bT_hi[:, 1 - par, 2 * n:2 * n + 2, :].rearrange("p k t -> p (k t)").bitcast(F32),
                                        ALU.subtract).then_inc(bT_lo_s, 1)
                if mid:
                    hidden_lo(0)
                    hidden(1)
                    hidden_lo(1)
                if ahead:
                    v.wait_ge(gu_hi_s, e + 2)
                    v.tensor_tensor(gu_lo[:, 1 - par, :], gu_raw[:, 1 - par, :], gu_hi[:, 1 - par, :].bitcast(F32),
                                    ALU.subtract).then_inc(gu_lo_s, 1)
                if mid:
                    hidden(2)
                    hidden_lo(2)

            pipeline(v, body)

        @block.gpsimd
        def _(g):
            def stage(expert, place):
                g.tensor_copy(idx_now[:, place, :], idxT[:, bass.ds(2 * expert, 2)]).then_inc(staged, 1)

            def gather(place):
                for t in range(2):
                    g.indirect_dma_start(
                        out=rows[:, place, t, :], out_offset=None, in_=d["xn2_rows"],
                        in_offset=bass.IndirectOffsetOnAxis(ap=idx_now[:, place, t:t + 1], axis=0),
                    ).then_inc(rows_in[place], 16)

            def body(e, par, half):
                nxt = 1 - par
                if isinstance(e, int) and e < 0:
                    g.wait_ge(idx_s, 1)
                    for n in range(2):
                        stage(n, n)
                        g.wait_ge(staged, n + 1)
                        gather(n)
                    g.wait_ge(rows_in[0], 32)
                    stage(2, 0)
                    return
                if at_most(e, E - 3):
                    g.wait_ge(turned, 2 * e + 2)
                    g.wait_ge(staged, e + 3)
                    g.wait_ge(rows_in[nxt], 32 * (half + par + 1))
                if at_least(e, 1):
                    g.wait_ge(dn_hi_s, e)
                    g.tensor_tensor(dn_lo[:, nxt, :, :].rearrange("p m n -> p (m n)"), dn_raw[:, nxt, :],
                                    dn_hi[:, nxt, :, :].rearrange("p m n -> p (m n)").bitcast(F32),
                                    ALU.subtract).then_inc(dn_lo_s, 1)
                if at_most(e, E - 3):
                    gather(par)
                    if at_most(e, E - 4):
                        stage(e + 3, nxt)

            pipeline(g, body)


def phase_c(nc, d, keep):
    T, D = d["xn2_rows"].shape
    KC = D // P
    MS = d["sg"].shape[2]
    MC = -(-MS // P)
    col = [min(m * P, MS - P) for m in range(MC)]
    GT = 4
    GROUPS = T // (GT * P)
    NT = GT * P
    POOL_LO = GT

    with ExitStack() as ctx:
        def sb(name, shape, dt=F32):
            return ctx.enter_context(nc.sbuf_tensor(name, shape, dt))

        def ps(name, shape, dt=F32):
            return ctx.enter_context(nc.psum_tensor(name, shape, dt))

        def sem(name):
            return ctx.enter_context(nc.semaphore(name))

        ident = sb("c_ident", [P, P])
        raw = [sb(f"c_raw{n}", [P, max(KC * MS, MC * D)]) for n in range(2)]
        sg = [sb(f"sg_{part}", [P, KC, MS], F32R) for part in ("hi", "lo")]
        su = [sb(f"su_{part}", [P, KC, MS], F32R) for part in ("hi", "lo")]
        sd = [sb(f"sd_{part}", [P, MC, D], F32R) for part in ("hi", "lo")]
        x_rows = sb("c_x_rows", [P, GT, D])
        xT_hi, xT_lo = sb("c_xT_hi", [P, KC, NT], F32R), sb("c_xT_lo", [P, KC, NT], F32R)
        gate_act, hid = sb("c_gate_act", [P, 2, NT]), sb("c_hid", [P, 2, NT])
        h_hi, h_lo = sb("c_h_hi", [P, MC, NT], F32R), sb("c_h_lo", [P, MC, NT], F32R)
        idx_now = sb("c_idx_now", [P, GT * TOP_K], U32)
        w_now = sb("c_w_now", [P, GT * TOP_K])
        rows = sb("c_rows", [P, 2, TOP_K, D])
        acc = sb("c_acc", [P, GT, D])
        out_rows = sb("c_out_rows", [P, 2, D])

        xT_ps = [ps(f"c_xT_ps{n}", [P, NT]) for n in range(2)]
        g_ps, u_ps = [ps(f"c_g_ps{n}", [P, NT]) for n in range(2)], [ps(f"c_u_ps{n}", [P, NT]) for n in range(2)]
        dn_ps = [ps(f"c_dn_ps{n}", [P, D]) for n in range(2)]

        id_in, w_in = sem("c_ident_loaded"), [sem(f"c_weight_loaded{n}") for n in range(3)]
        w_hi_s, w_lo_s = sem("c_weight_hi_done"), sem("c_weight_lo_done")
        x_in, acc_in = sem("c_rows_loaded"), sem("c_residual_loaded")
        turned, xT_hi_s, xT_lo_s = sem("c_rows_turned"), sem("c_rowsT_hi_done"), sem("c_rowsT_lo_done")
        gu_done, act_s, hid_s = sem("c_gu_product_done"), sem("c_silu_done"), sem("c_hidden_done")
        h_hi_s, h_lo_v, h_lo_p = sem("c_hidden_hi_done"), sem("c_hidden_lo_by_vector"), sem("c_hidden_lo_by_pool")
        staged = sem("c_index_staged")
        gathered = [sem(f"c_gathered{n}") for n in range(2)]
        routed_s, step_s = sem("c_routed_done"), sem("c_routed_step")
        dn_done, out_s = sem("c_down_product_done"), sem("c_out_done")
        stored = [sem(f"c_out_stored{n}") for n in range(2)]

        def pipeline(eng, body):
            for g in (-1, 0):
                body(g)
            with eng.Fori(1, GROUPS - 1) as g:
                body(g)
            body(GROUPS - 1)

        def is_int(g):
            return isinstance(g, int)

        block = ctx.enter_context(nc.Block())

        @block.sync
        def _(sp):
            sp.dma_start(ident[:], d["consts"][:, 0:P]).then_inc(id_in, 16)
            rows_of = d["xn2_rows"].rearrange("(g q p) n -> g p q n", q=GT, p=P)
            x2_of = d["x2_rows"].rearrange("(g q p) n -> g p q n", q=GT, p=P)
            out_of = d["out"].rearrange("(g q p) n -> g p q n", q=GT, p=P)
            sp.dma_start(x_rows[:], rows_of[0]).then_inc(x_in, 16)
            sp.dma_start(raw[0][:, 0:KC * MS], d["sg"].rearrange("p c m -> p (c m)")).then_inc(w_in[0], 16)
            sp.dma_start(raw[1][:, 0:KC * MS], d["su"].rearrange("p c m -> p (c m)")).then_inc(w_in[1], 16)
            sp.wait_ge(w_hi_s, 1)
            sp.wait_ge(w_lo_s, 1)
            sp.dma_start(raw[0][:, 0:MC * D], d["sd"].rearrange("p c m -> p (c m)")).then_inc(w_in[2], 16)

            def body(g):
                if is_int(g) and g < 0:
                    sp.dma_start(acc[:], x2_of[0]).then_inc(acc_in, 16)
                    return
                if not (is_int(g) and g == GROUPS - 1):
                    sp.wait_ge(turned, KC * (g + 1))
                    sp.dma_start(x_rows[:], rows_of[g + 1]).then_inc(x_in, 16)
                for q in range(GT):
                    sp.wait_ge(out_s, GT * g + (q + 1))
                    sp.dma_start(out_of[g][:, q, :], out_rows[:, q % 2, :]).then_inc(stored[q % 2], 16)
                if not (is_int(g) and g == GROUPS - 1):
                    sp.dma_start(acc[:], x2_of[g + 1]).then_inc(acc_in, 16)

            pipeline(sp, body)
            for n in range(2):
                sp.wait_ge(stored[n], 16 * GROUPS * GT // 2)

        @block.tensor
        def _(pe):
            def mm3(out, a, b, a_at, b_at, first, last):
                pe.matmul(out, a[0][a_at], b[0][b_at], start=first, stop=False)
                pe.matmul(out, a[0][a_at], b[1][b_at], start=False, stop=False)
                return pe.matmul(out, a[1][a_at], b[0][b_at], start=False, stop=last)

            full = slice(None)

            def body(g):
                def turn_rows():
                    pe.wait_ge(x_in, 16 * (g + 2))
                    for kc in range(KC):
                        need(pe, xT_lo_s, KC * g + (KC + kc - 1) if not (is_int(g) and g < 0) else kc - 1)
                        for q in range(GT):
                            last = pe.transpose(xT_ps[kc % 2][:, q * P:(q + 1) * P], x_rows[:, q, kc * P:(kc + 1) * P],
                                                ident[:])
                        last.then_inc(turned, 1)

                def gate_up(m):
                    if m == 0:
                        pe.wait_ge(xT_lo_s, KC * (g + 1))
                    need(pe, hid_s, MC * g + (m - 1))
                    for n, (bank, w) in enumerate(((g_ps[m % 2], sg), (u_ps[m % 2], su))):
                        if is_int(g) and g == 0 and m == 0:
                            pe.wait_ge(w_lo_s, n + 1)
                        for kc in range(KC):
                            last = mm3(bank[:], w, (xT_hi, xT_lo), (full, kc, slice(col[m], col[m] + P)),
                                       (full, kc, full), kc == 0, kc == KC - 1)
                        last.then_inc(gu_done, 1)

                def down(q):
                    if q == 0:
                        pe.wait_ge(h_lo_p, POOL_LO * (g + 1))
                        pe.wait_ge(h_lo_v, (MC - POOL_LO) * (g + 1))
                        if is_int(g) and g == 0:
                            pe.wait_ge(w_lo_s, 3)
                    need(pe, out_s, GT * g + (q - 1))
                    for m in range(MC):
                        last = mm3(dn_ps[q % 2][:], (h_hi, h_lo), sd, (full, m, slice(q * P, (q + 1) * P)),
                                   (full, m, full), m == 0, m == MC - 1)
                    last.then_inc(dn_done, 1)

                if is_int(g) and g < 0:
                    pe.wait_ge(id_in, 16)
                    turn_rows()
                    return
                for m in range(MC):
                    gate_up(m)
                if not (is_int(g) and g == GROUPS - 1):
                    turn_rows()
                for q in range(GT):
                    down(q)

            pipeline(pe, body)

        @block.scalar
        def _(act):
            for n, (w, size) in enumerate(((sg, KC * MS), (su, KC * MS), (sd, MC * D))):
                act.wait_ge(w_in[n], 16)
                act.copy(w[0][:].rearrange("p c m -> p (c m)"), raw[n % 2][:, 0:size]).then_inc(w_hi_s, 1)

            def body(g):
                def rows_hi():
                    for kc in range(KC):
                        act.wait_ge(turned, KC * (g + 1) + (kc + 1))
                        act.copy(xT_hi[:, kc, :], xT_ps[kc % 2][:]).then_inc(xT_hi_s, 1)

                if is_int(g) and g < 0:
                    rows_hi()
                    return
                for m in range(MC):
                    act.wait_ge(gu_done, 2 * MC * g + (2 * m + 1))
                    need(act, hid_s, MC * g + (m - 1))
                    act.activation(gate_act[:, m % 2, :], g_ps[m % 2][:], ACT.Silu).then_inc(act_s, 1)
                    act.wait_ge(hid_s, MC * g + (m + 1))
                    if m == 0:
                        need(act, dn_done, GT * g)
                    act.copy(h_hi[:, m, :], hid[:, m % 2, :]).then_inc(h_hi_s, 1)
                if not (is_int(g) and g == GROUPS - 1):
                    rows_hi()

            pipeline(act, body)

        @block.vector
        def _(v):
            for n, (w, size) in enumerate(((sg, KC * MS), (su, KC * MS), (sd, MC * D))):
                v.wait_ge(w_hi_s, n + 1)
                v.tensor_tensor(w[1][:].rearrange("p c m -> p (c m)"), raw[n % 2][:, 0:size],
                                w[0][:].rearrange("p c m -> p (c m)").bitcast(F32), ALU.subtract).then_inc(w_lo_s, 1)

            def body(g):
                def rows_lo():
                    for kc in range(KC):
                        v.wait_ge(xT_hi_s, KC * (g + 1) + (kc + 1))
                        v.tensor_tensor(xT_lo[:, kc, :], xT_ps[kc % 2][:], xT_hi[:, kc, :].bitcast(F32),
                                        ALU.subtract).then_inc(xT_lo_s, 1)

                def routed(q):
                    v.wait_ge(gathered[q % 2], 16 * TOP_K * (2 * g + (q // 2 + 1)))
                    if q == 0:
                        v.wait_ge(acc_in, 16 * (g + 1))
                        v.wait_ge(staged, g + 1)
                    for k in range(TOP_K):
                        last = v.scalar_tensor_tensor(acc[:, q, :], rows[:, q % 2, k, :],
                                                      w_now[:, q * TOP_K + k:q * TOP_K + k + 1], acc[:, q, :],
                                                      ALU.mult, ALU.add)
                        if k < TOP_K - 1:
                            last.then_inc(step_s, 1)
                            v.wait_ge(step_s, (TOP_K - 1) * GT * g + ((TOP_K - 1) * q + k + 1))
                    last.then_inc(routed_s, 1)

                def stage(group):
                    at = bass.ds(group * (GT * TOP_K), GT * TOP_K)
                    v.tensor_scalar(w_now[:], keep["weight"][:, at], 1.0, None, ALU.mult)
                    v.tensor_copy(idx_now[:], keep["slot"][:, at]).then_inc(staged, 1)

                if is_int(g) and g < 0:
                    stage(0)
                    rows_lo()
                    return
                for m in range(MC):
                    v.wait_ge(act_s, MC * g + (m + 1))
                    v.wait_ge(gu_done, 2 * MC * g + (2 * m + 2))
                    if m < POOL_LO:
                        need(v, h_lo_p, POOL_LO * g + (m - 1 if m >= 2 else 0))
                    elif m - 2 < POOL_LO:
                        v.wait_ge(h_lo_p, POOL_LO * g + (m - 1))
                    v.tensor_tensor(hid[:, m % 2, :], gate_act[:, m % 2, :], u_ps[m % 2][:],
                                    ALU.mult).then_inc(hid_s, 1)
                    if m >= POOL_LO:
                        v.wait_ge(h_hi_s, MC * g + (m + 1))
                        v.tensor_tensor(h_lo[:, m, :], hid[:, m % 2, :], h_hi[:, m, :].bitcast(F32),
                                        ALU.subtract).then_inc(h_lo_v, 1)
                    if 1 <= m <= 3:
                        routed(m - 1)
                if not (is_int(g) and g == GROUPS - 1):
                    rows_lo()
                routed(GT - 1)
                if not (is_int(g) and g == GROUPS - 1):
                    v.wait_ge(routed_s, GT * (g + 1))
                    stage(g + 1)
                for q in range(GT):
                    v.wait_ge(dn_done, GT * g + (q + 1))
                    need(v, stored[q % 2], 16 * 2 * g + 16 * (q // 2))
                    if q == 0:
                        v.wait_ge(routed_s, GT * (g + 1))
                    v.tensor_tensor(out_rows[:, q % 2, :], dn_ps[q % 2][:], acc[:, q, :], ALU.add).then_inc(out_s, 1)

            pipeline(v, body)

        @block.gpsimd
        def _(p):
            def body(g):
                if is_int(g) and g < 0:
                    return
                for q in range(GT):
                    p.wait_ge(h_hi_s, MC * g + (q + 1))
                    if q == 0:
                        p.wait_ge(staged, g + 1)
                    need(p, routed_s, GT * g + (q - 1))
                    p.tensor_tensor(h_lo[:, q, :], hid[:, q % 2, :], h_hi[:, q, :].bitcast(F32),
                                    ALU.subtract).then_inc(h_lo_p, 1)
                    for k in range(TOP_K):
                        p.indirect_dma_start(
                            out=rows[:, q % 2, k, :], out_offset=None, in_=d["eo"],
                            in_offset=bass.IndirectOffsetOnAxis(ap=idx_now[:, q * TOP_K + k:q * TOP_K + k + 1], axis=0),
                        ).then_inc(gathered[q % 2], 16)

            pipeline(p, body)


def cross_attention_moe(nc, d):
    T = d["x"].shape[0] * d["x"].shape[1]
    D = d["x"].shape[2]
    E = d["experts"].shape[0]
    d["x2"] = nc.dram_tensor("x2_scratch", d["x"].shape, F32, kind="Internal").ap()
    d["xn2"] = nc.dram_tensor("xn2_scratch", d["x"].shape, F32, kind="Internal").ap()
    d["table"] = nc.dram_tensor("slot_token_scratch", [E * CAPACITY, 1], I32, kind="Internal").ap()
    d["eo"] = nc.dram_tensor("expert_out_scratch", [E * CAPACITY, D], F32, kind="Internal").ap()
    d["x2_rows"], d["xn2_rows"] = (d[n].rearrange("b s n -> (b s) n") for n in ("x2", "xn2"))
    with ExitStack() as ctx:
        keep = {"slot": ctx.enter_context(nc.sbuf_tensor("keep_slot", [P, T // P * TOP_K], U32)),
                "weight": ctx.enter_context(nc.sbuf_tensor("keep_weight", [P, T // P * TOP_K], F32))}
        phase_a(nc, d, keep)
        phase_b(nc, d)
        phase_c(nc, d, keep)


def kernel(**inputs):
    import numpy as np
    import concourse.bacc as bacc
    from concourse.bass_utils import run_bass_kernel_spmd

    attn = lambda n: np.asarray(inputs["L0_xattn_" + n])
    ffn = lambda n: np.asarray(inputs["L0_ffn_" + n])
    x, ctx = np.asarray(inputs["x"]), np.asarray(inputs["ctx_2048"])
    D = x.shape[2]
    E, M, _ = ffn("Wg").shape
    MS = ffn("Sg").shape[0]

    def by_input(w):
        w = np.swapaxes(w, -1, -2)
        w = w.reshape(*w.shape[:-2], w.shape[-2] // P, P, w.shape[-1])
        return np.swapaxes(w, -3, -2)

    def by_hidden(w):
        w = np.swapaxes(w, -1, -2)
        hidden = w.shape[-2]
        chunks = -(-hidden // P)
        full = (chunks - 1) * P
        out = np.zeros((*w.shape[:-2], chunks * P, w.shape[-1]), w.dtype)
        out[..., 0:full, :] = w[..., 0:full, :]
        out[..., full + chunks * P - hidden:, :] = w[..., full:, :]
        return np.swapaxes(out.reshape(*w.shape[:-2], chunks, P, w.shape[-1]), -3, -2)

    flat = lambda w: w.reshape(E, P, -1)
    p = np.arange(P)
    consts = np.concatenate([
        np.eye(P), p[:, None] < p[None, :], np.ones((P, P)), np.broadcast_to(np.arange(E), (P, E)),
        np.broadcast_to(np.arange(E) * CAPACITY, (P, E)), p[:, None] + 1 + P * np.arange(x.shape[1] // P)[None, :]],
        1).astype(np.float32)
    arrays = {
        "x": x,
        "ctxT": np.swapaxes(ctx, 1, 2),
        "wk": attn("Wk_img"), "wq": attn("Wq"), "wv": attn("Wv_img"), "wo": attn("Wo"), "bo": attn("bo"),
        "vecs": np.stack([attn(n).reshape(D // P, P).T for n in ("bq", "gq", "bk_img", "gk_img", "bv_img")], 1),
        "gateT": ffn("gate_weight").T,
        "consts": consts,
        "experts": np.concatenate([flat(by_input(ffn("Wg"))), flat(by_input(ffn("Wu"))), flat(by_hidden(ffn("Wd")))], 2),
        "sg": by_input(ffn("Sg")), "su": by_input(ffn("Su")), "sd": by_hidden(ffn("Sd")),
    }
    arrays = {f"in_{n}_dram": np.ascontiguousarray(a) for n, a in arrays.items()}

    nc = bacc.Bacc("TRN2", target_bir_lowering=False, num_devices=1)
    d = {n[3:-5]: nc.dram_tensor(n, a.shape, mybir.dt.from_np(a.dtype), kind="ExternalInput").ap()
         for n, a in arrays.items()}
    d["out"] = nc.dram_tensor("out_0_dram", (x.shape[0] * x.shape[1], D), F32, kind="ExternalOutput").ap()
    d["m"] = M
    cross_attention_moe(nc, d)
    r = run_bass_kernel_spmd(nc, [arrays], core_ids=[0])
    return r.results[0]["out_0_dram"].reshape(x.shape)
```

```python
from contextlib import ExitStack

import concourse.bass as bass
from concourse import mybir

F32 = mybir.dt.float32
F32R = mybir.dt.float32r
BF16 = mybir.dt.bfloat16
I32 = mybir.dt.int32
U32 = mybir.dt.uint32
ALU = mybir.AluOpType
ACT = mybir.ActivationFunctionType
X = mybir.AxisListType.X

P = 128
HEAD_DIM = 32
TOP_K = 6
N_GROUP = 8
TOPK_GROUP = 3
CAPACITY = 192
RMS_EPS = 1e-6
LN_EPS = 1e-5
SCALE = float(HEAD_DIM) ** -0.5
OVER = 65536.0



def need(eng, sem, value):
    if isinstance(value, int) and value <= 0:
        return
    eng.wait_ge(sem, value)


class Kind:
    def __init__(self, prep, attend, post, scatter):
        self.prep, self.attend, self.post, self.scatter = prep, attend, post, scatter


SHARED_USES = [
    ("v0", "attend"), ("pv3", "post"), ("v1", "attend"), ("o0", "post"), ("o1", "post"), ("k0", "prep"),
    ("nT0", "post"), ("k1", "prep"), ("nT1", "post"), ("pv0", "attend"), ("logits", "post"), ("xT0", "prep"),
    ("xT1", "prep"), ("pv1", "attend"), ("q0", "prep"), ("q1", "prep"), ("pv2", "attend"), ("qT0", "prep"),
    ("pos", "post"), ("kT0", "prep"), ("qT1", "prep"), ("kT1", "prep"),
]


def shared_plan(kinds):
    before = [None, None]
    n = 0
    plans = []
    for at, kind in enumerate(kinds):
        plan = {}
        for name, stage in SHARED_USES:
            if {"attend": kind.attend, "post": kind.post, "prep": kind.prep}[stage]:
                last = before[n % 2]
                plan[name] = (n % 2, last and last[0], last and at - last[1])
                before[n % 2] = (name, at)
                n += 1
        plans.append(plan)
    return plans


def phase_a(nc, d, keep):
    B, S, D = d["x"].shape
    KC = D // P
    QT = S // P
    H = D // HEAD_DIM
    HC = P // HEAD_DIM
    CK = d["ctxT"].shape[2]
    KT = CK // P
    UNITS = KC * QT
    E = d["gateT"].shape[1]
    GE = E // N_GROUP
    assert (KC, QT, HC, KT, UNITS) == (4, 2, 4, 2, 8)

    prologue = [Kind(True, False, False, False), Kind(True, True, False, False), Kind(True, True, True, False)]
    steady = Kind(True, True, True, True)
    epilogue = [Kind(False, True, True, True), Kind(False, False, True, True), Kind(False, False, False, True)]
    LOOP = B - 3
    plans = shared_plan([*prologue, steady, steady, *epilogue])
    assert plans[len(prologue)] == plans[len(prologue) + 1]

    def pipeline(eng, body):
        for at, kind in enumerate(prologue):
            body(at - 1, kind, plans[at])
        with eng.Fori(2, 2 + LOOP) as i:
            body(i, steady, plans[len(prologue)])
        for at, kind in enumerate(epilogue):
            body(2 + LOOP + at, kind, plans[len(prologue) + 2 + at])

    with ExitStack() as ctx:
        def sb(name, shape, dt=F32):
            return ctx.enter_context(nc.sbuf_tensor(name, shape, dt))

        def ps(name, shape, dt=F32):
            return ctx.enter_context(nc.psum_tensor(name, shape, dt))

        def sem(name):
            return ctx.enter_context(nc.semaphore(name))

        w_hi = {n: sb(f"w{n}_hi", [P, KC, D], F32R) for n in "kqvo"}
        w_lo = {n: sb(f"w{n}_lo", [P, KC, D], F32R) for n in "kqvo"}
        gate = sb("gate_parts", [P, KC, 2, E], F32R)
        bv_col = sb("bv_col", [P, KC])
        bo_row, bias_row = sb("bo_row", [P, D]), {n: sb(f"b{n}_row", [P, D]) for n in "kq"}
        gain_row = sb("gain_row", [P, D])
        consts = sb("const_cols", [P, d["consts"].shape[1]])
        ident, ones = consts[:, 0:P], consts[:, 2 * P:3 * P]
        iota_e, iota_g = consts[:, 3 * P:3 * P + E], consts[:, 3 * P:3 * P + N_GROUP]
        slot_base = consts[:, 3 * P + E:3 * P + 2 * E]
        tok_col = consts[:, 3 * P + 2 * E:3 * P + 2 * E + QT]
        tri_b, ones_b = sb("tri_b", [P, P], BF16), sb("ones_b", [P, P], BF16)
        minus_half = sb("minus_half", [P, QT])
        x_raw = sb("x_raw", [P, QT, D])
        ctx_raw = sb("ctx_raw", [P, KC, CK])
        ctx_hi, ctx_lo = sb("ctx_hi", [P, KC, CK], F32R), sb("ctx_lo", [P, KC, CK], F32R)
        tT_hi, tT_lo = sb("tT_hi", [P, KC, S], F32R), sb("tT_lo", [P, KC, S], F32R)
        rows = {n: sb(f"{n}_rows", [P, QT, D]) for n in "kq"}
        squares = sb("squares", [P, 2, QT, D], BF16)
        sq_sum = {n: sb(f"{n}_sq_sum", [P, QT]) for n in "kq"}
        mean_sq = {n: sb(f"{n}_mean_sq", [P, QT]) for n in "kq"}
        rms_inv = {n: sb(f"{n}_rms_inv", [P, QT]) for n in "kq"}
        hT = {n: (sb(f"{n}T_hi", [P, KC, S], F32R), sb(f"{n}T_lo", [P, KC, S], F32R)) for n in "kq"}
        ln_stats, ln_mv = sb("ln_stats", [P, QT, 6]), sb("ln_mv", [P, QT, 2])
        ln_var, ln_rstd = sb("ln_var", [P, QT]), sb("ln_rstd", [P, QT])
        V_AT = (0, P + 2 * HEAD_DIM, 2 * P + HEAD_DIM, P)
        VC = 2 * P + 3 * HEAD_DIM
        v_hi, v_lo = sb("v_hi", [P, KT, KC, VC], F32R), sb("v_lo", [P, KT, KC, VC], F32R)
        probs = sb("probs", [P, 2, HC, CK])
        neg_max, row_sum, row_inv = sb("neg_max", [P, 2, HC]), sb("row_sum", [P, 2, HC]), sb("row_inv", [P, 2, HC])
        row_max = sb("row_max", [P, 2, HC])
        pT_hi, pT_lo = sb("pT_hi", [P, HC * KT, S], F32R), sb("pT_lo", [P, HC * KT, S], F32R)
        aT_hi, aT_lo = sb("aT_hi", [P, KC, S], F32R), sb("aT_lo", [P, KC, S], F32R)
        x2 = sb("x2_rows", [P, QT, D])
        xn2 = sb("xn2_rows", [P, QT, D])
        n2_stats, n2_mv = sb("n2_stats", [P, QT, 6]), sb("n2_mv", [P, QT, 2])
        n2_var, n2_rstd = sb("n2_var", [P, QT]), sb("n2_rstd", [P, QT])
        lg_max, lg_sum = sb("lg_max", [P, QT]), sb("lg_sum", [P, QT])
        score = sb("score", [P, QT, E])
        g_score, g_top, g_idx, g_idxf = (sb("g_score", [P, QT, N_GROUP]), sb("g_top", [P, QT, 8]),
                                         sb("g_idx", [P, QT, 8], U32), sb("g_idxf", [P, QT, 8]))
        g_hot, g_mask = sb("g_hot", [P, QT, TOPK_GROUP, N_GROUP]), sb("g_mask", [P, QT, N_GROUP])
        e_top, e_idx, e_idxf = sb("e_top", [P, QT, 8]), sb("e_idx", [P, QT, 8], U32), sb("e_idxf", [P, QT, 8])
        e_hot = sb("e_hot", [P, QT, TOP_K, E], BF16)
        e_slot = sb("e_slot", [P, QT, TOP_K, E])
        mask_f, mask_b = sb("mask_f", [P, QT, E]), sb("mask_b", [P, QT, E], BF16)
        seen, seen_b = sb("seen", [P, E]), sb("seen_b", [P, E], BF16)
        slot_val = sb("slot_val", [P, QT, E])
        last_tok = sb("last_tok", [P, E])
        slot_f, last_slot, is_last, scat_f = (sb("slot_f", [P, QT, TOP_K]), sb("last_slot", [P, QT, TOP_K]),
                                              sb("is_last", [P, QT, TOP_K]), sb("scat_f", [P, QT, TOP_K]))
        scat_idx = sb("scat_idx", [P, QT * TOP_K], U32)
        scat_tok = sb("scat_tok", [P, QT], I32)
        zero_i = sb("zero_i", [P, E * CAPACITY // P], I32)
        lastT, lastT_i = sb("lastT", [E, 1]), sb("lastT_i", [E, 1], I32)

        settled = sb("settled", [P, 8])

        scores_ps = [ps(f"scores_ps{n}", [P, HC, CK]) for n in range(2)]
        pT_ps = ps("pT_ps", [P, HC * KT, P])
        shared_ps = [ps(f"shared_ps{n}", [P, 512]) for n in range(2)]

        in_sem = sem("a_params_loaded")
        vec_sem = sem("a_vectors_loaded")
        stage_in = [sem(f"a_weight_half_loaded{n}") for n in range(2)]
        w_hi_done, w_lo_done = sem("a_weight_hi_done"), sem("a_weight_lo_done")
        gate_split, gain_s, bo_in = sem("a_gate_split"), sem("a_gain_product_done"), sem("a_bo_loaded")
        chain = {n: sem(f"a_vector_{n}_chain") for n in ("setup", "prep", "attend", "post")}
        setup_p = sem("a_setup_by_pool")
        table_zeroed = sem("a_table_zeroed")
        x_in, ctx_in, res_in = sem("a_x_loaded"), sem("a_ctx_loaded"), sem("a_residual_loaded")
        ctx_hi_s, ctx_lo_s = sem("a_ctx_hi_done"), sem("a_ctx_lo_done")
        stats1, rstd1, xn_s = sem("a_ln1_var_done"), sem("a_ln1_rstd_done"), sem("a_ln1_done")
        x_turned, x_hi_s, x_lo_s = sem("a_x_turned"), sem("a_xT_hi_done"), sem("a_xT_lo_done")
        proj = {n: sem(f"a_{n}_product_done") for n in "kq"}
        biased_s = {n: sem(f"a_{n}_biased") for n in "kq"}
        sq_s = {n: sem(f"a_{n}_squared") for n in "kq"}
        ms_s = {n: sem(f"a_{n}_mean_square_done") for n in "kq"}
        inv_s = {n: sem(f"a_{n}_rms_inverse_done") for n in "kq"}
        k_normed, turned_s = sem("a_k_normed"), {n: sem(f"a_{n}_turned") for n in "kq"}
        hi_s = {n: sem(f"a_{n}_hi_done") for n in "kq"}
        lo_s = {n: sem(f"a_{n}_lo_done") for n in "kq"}
        v_done, v_hi_s, v_lo_s = sem("a_v_product_done"), sem("a_v_hi_done"), sem("a_v_lo_done")
        head_done = sem("a_head_scores_done")
        scores_done, max_done, exp_done = sem("a_scores_done"), sem("a_max_done"), sem("a_exp_done")
        inv_done, probs_done = sem("a_row_inv_done"), sem("a_probs_normed")
        p_turned, p_hi_s, p_lo_s = sem("a_probs_turned"), sem("a_pT_hi_done"), sem("a_pT_lo_done")
        pv_done, a_hi_s, a_lo_s = sem("a_pv_done"), sem("a_aT_hi_done"), sem("a_aT_lo_done")
        bo_added, o_done, x2_s = sem("a_residual_plus_bo"), sem("a_o_product_done"), sem("a_x2_done")
        stats2, rstd2, xn2_s = sem("a_ln2_var_done"), sem("a_ln2_rstd_done"), sem("a_ln2_done")
        x2_out, xn2_out = sem("a_x2_stored"), sem("a_xn2_stored")
        n_turned, n_hi_s, n_lo_s = sem("a_xn2_turned"), sem("a_xn2T_hi_done"), sem("a_xn2T_lo_done")
        logits_done, lgmax_s, lgexp_s = sem("a_logits_done"), sem("a_logit_max_done"), sem("a_logit_exp_done")
        mask_s, pos_done, scat_rdy = sem("a_mask_done"), sem("a_positions_done"), sem("a_scatter_index_done")
        scattered = sem("a_tokens_scattered")
        lastT_s, last_i_s, last_out = (sem("a_last_turned"), sem("a_last_index_done"),
                                               sem("a_last_stored"))
        pos_read = sem("a_positions_read")

        def read_of(name):
            kind, n = name.rstrip("0123456789"), name.lstrip("abcdefghijklmnopqrstuvwxyzT")
            n = int(n) if n else 0
            return {
                "v": (v_lo_s, KT, n + 1),
                "pv": (a_lo_s, KC, n + 1 - (KC if n == KC - 1 else 0)),
                "o": (x2_s, QT, n + 1 - QT),
                "k": (biased_s["k"], QT, QT + n + 1), "q": (biased_s["q"], QT, QT + n + 1),
                "kT": (lo_s["k"], QT, QT + n + 1), "qT": (lo_s["q"], QT, QT + n + 1),
                "nT": (n_lo_s, QT, n + 1 - QT), "xT": (x_lo_s, QT, QT + n + 1),
                "logits": (lgmax_s, 1, 0), "pos": (pos_read, 1, 0),
            }[kind]

        def heads_of(bank):
            b = bank.rearrange("p (c g n) -> p c g n", g=HC, n=HEAD_DIM)
            return b[:, :, 0:HC:HC - 1, :], b[:, :, 1:3, :]

        def heads_in(v, t):
            near = v[:, t, :, 0:2 * P].rearrange("p c (g n) -> p c g n", g=2)[:, :, :, 0:HEAD_DIM]
            step = V_AT[2] - V_AT[1]
            far = v[:, t, :, V_AT[1]:VC].rearrange("p c (a n) -> p c a n", n=HEAD_DIM)[:, :, 0:step // HEAD_DIM + 1:step // HEAD_DIM, :]
            return near, far

        block = ctx.enter_context(nc.Block())
        halves = [(n, h) for n in "kqvo" for h in range(2)]
        stage = [probs[:, n, :, :].rearrange("p h t -> p (h t)") for n in range(2)]

        @block.sync
        def _(sp):
            sp.dma_start(ctx_raw[:], d["ctxT"][0].rearrange("(c p) t -> p c t", p=P)).then_inc(ctx_in, 16)
            for n, (w, h) in enumerate(halves[:2]):
                sp.dma_start(stage[n % 2],
                             d["w" + w].rearrange("(c p) n -> p c n", p=P)[:, 2 * h:2 * h + 2, :]
                             ).then_inc(stage_in[n % 2], 16)
            sp.dma_start(x_raw[:], d["x"][0].rearrange("(q p) n -> p q n", p=P)).then_inc(x_in, 16)
            sp.dma_start(consts[:], d["consts"]).then_inc(in_sem, 16)
            sp.dma_start(bv_col[:], d["bv"]).then_inc(vec_sem, 16)
            for row, n in ((bias_row["k"], "bk"), (bias_row["q"], "bq"), (gain_row, "gk"), (bo_row, "gq")):
                sp.dma_start(row[:], d[n].rearrange("(a n) -> a n", a=1).to_broadcast([P, D])).then_inc(vec_sem, 16)
            sp.dma_start(x2[:, 0, 0:KC * E].rearrange("p (c e) -> p c e", c=KC),
                         d["gateT"].rearrange("(c p) e -> p c e", p=P)).then_inc(vec_sem, 16)
            for n, (w, h) in enumerate(halves):
                if n < 2:
                    continue
                sp.wait_ge(w_hi_done, n - 1)
                sp.wait_ge(w_lo_done, n - 1)
                sp.dma_start(stage[n % 2],
                             d["w" + w].rearrange("(c p) n -> p c n", p=P)[:, 2 * h:2 * h + 2, :]
                             ).then_inc(stage_in[n % 2], 16)
            sp.wait_ge(gain_s, 1)
            sp.dma_start(bo_row[:], d["bo"].rearrange("(a n) -> a n", a=1).to_broadcast([P, D])).then_inc(bo_in, 16)
            sp.wait_ge(setup_p, 1)
            sp.dma_start(d["table"].rearrange("(p j) o -> p (j o)", p=P), zero_i[:]).then_inc(table_zeroed, 16)

            def body(i, kind, use):
                if kind.prep and not (isinstance(i, int) and i < 0):
                    b = i + 1
                    need(sp, ctx_lo_s, b)
                    need(sp, ctx_hi_s, b)
                    sp.dma_start(ctx_raw[:], d["ctxT"][b].rearrange("(c p) t -> p c t", p=P)).then_inc(ctx_in, 16)
                    sp.wait_ge(x_turned, QT * b)
                    sp.dma_start(x_raw[:], d["x"][b].rearrange("(q p) n -> p q n", p=P)).then_inc(x_in, 16)
                if kind.post:
                    b = i - 1
                    if isinstance(b, int) and b == 0:
                        sp.wait_ge(gate_split, 1)
                    else:
                        need(sp, x2_out, 16 * b)
                        need(sp, xn2_s, QT * i - QT)
                    sp.dma_start(x2[:], d["x"][b].rearrange("(q p) n -> p q n", p=P)).then_inc(res_in, 16)
                if kind.post:
                    b = i - 1
                    sp.wait_ge(x2_s, QT * b + QT)
                    sp.dma_start(d["x2"][b].rearrange("(q p) n -> p q n", p=P), x2[:]).then_inc(x2_out, 16)
                    sp.wait_ge(xn2_s, QT * b + QT)
                    sp.dma_start(d["xn2"][b].rearrange("(q p) n -> p q n", p=P), xn2[:]).then_inc(xn2_out, 16)

            pipeline(sp, body)
            sp.wait_ge(x2_out, 16 * B)
            sp.wait_ge(xn2_out, 16 * B)
            sp.wait_ge(scattered, 16 * QT * TOP_K * B)
            sp.wait_ge(last_i_s, 1)
            sp.dma_start(d["table"].rearrange("(e s) o -> e (s o)", s=CAPACITY)[:, CAPACITY - 1:CAPACITY],
                         lastT_i[:], allow_slow_non_contiguous=True).then_inc(last_out, 16)
            sp.wait_ge(last_out, 16)

        @block.tensor
        def _(pe):
            def mm3(out, a_hi, a_lo, b_hi, b_lo, first, last):
                pe.matmul(out, a_hi, b_hi, start=first, stop=False)
                pe.matmul(out, a_hi, b_lo, start=False, stop=False)
                return pe.matmul(out, a_lo, b_hi, start=False, stop=last)

            def shared(use, name, i, own=None):
                bank, before, ago = use[name]
                waits = [own] if own else []
                if before:
                    signal, a, b = read_of(before)
                    b -= a * ago
                    if own and own[0] is signal:
                        assert own[1] == a
                        waits = [(signal, a, max(b, own[2]))]
                    else:
                        waits.append((signal, a, b))
                for signal, a, b in waits:
                    need(pe, signal, a * i + b)
                return shared_ps[bank]

            def turn(use, name, src, q, i, own):
                bank = shared(use, name, i, own)
                for c in range(KC):
                    last = pe.transpose(bank[:, c * P:(c + 1) * P], src[:, q, c * P:(c + 1) * P], ident)
                return last

            def body(i, kind, use):
                def project(n, t):
                    src_hi, src_lo = (ctx_hi, ctx_lo) if n == "k" else (tT_hi, tT_lo)
                    own = None
                    if t == 0:
                        own = (ctx_lo_s, 1, 2) if n == "k" else (x_lo_s, QT, 2 * QT)
                        if isinstance(i, int) and i < 0:
                            pe.wait_ge(w_lo_done, 2 if n == "k" else 4)
                    bank = shared(use, f"{n}{t}", i, own)
                    c = slice(t * P, (t + 1) * P)
                    for kc in range(KC):
                        last = mm3(bank[:], src_hi[:, kc, c], src_lo[:, kc, c], w_hi[n][:, kc, :], w_lo[n][:, kc, :],
                                   kc == 0, kc == KC - 1)
                    last.then_inc(proj[n], 1)

                def turn_rows(n, t):
                    own = (k_normed if n == "k" else biased_s["q"], QT, QT + t + 1)
                    turn(use, f"{n}T{t}", rows[n], t, i, own).then_inc(turned_s[n], 1)

                def v_tile(t):
                    bank = shared(use, f"v{t}", i)
                    if isinstance(i, int) and i == 0 and t == 0:
                        pe.wait_ge(w_lo_done, 6)
                    for kc in range(KC):
                        last = mm3(bank[:], ctx_hi[:, kc, t * P:(t + 1) * P], ctx_lo[:, kc, t * P:(t + 1) * P],
                                   w_hi["v"][:, kc, :], w_lo["v"][:, kc, :], kc == 0, kc == KC - 1)
                    last.then_inc(v_done, 1)

                def scores(u):
                    c, q = divmod(u, QT)
                    if u == 0:
                        for n in "kq":
                            pe.wait_ge(lo_s[n], QT * (i + 1))
                    need(pe, exp_done, UNITS * i + u - 1)
                    for n, g in enumerate((0, 2, 1, 3)):
                        if n >= 2:
                            pe.wait_ge(head_done, (HC - 1) * (UNITS * i + u) + n - 1)
                        r = slice(g * HEAD_DIM, (g + 1) * HEAD_DIM)
                        last = mm3(scores_ps[u % 2][:, g, :], hT["q"][0][r, c, q * P:(q + 1) * P],
                                   hT["q"][1][r, c, q * P:(q + 1) * P], hT["k"][0][r, c, :], hT["k"][1][r, c, :],
                                   True, True)
                        last.then_inc(scores_done if n == HC - 1 else head_done, 1)

                def turn_probs(u):
                    pe.wait_ge(probs_done, UNITS * i + u + 1)
                    need(pe, p_lo_s, UNITS * i + u)
                    for g in range(HC):
                        for t in range(KT):
                            last = pe.transpose(pT_ps[:, g * KT + t, :], probs[:, u % 2, g, t * P:(t + 1) * P], ident)
                    last.then_inc(p_turned, 1)

                def pv(b, c):
                    pe.wait_ge(p_lo_s, UNITS * b + 2 * c + 2)
                    own = (v_lo_s, KT, KT) if c == 0 else None
                    bank = shared(use, f"pv{c}", i, own)
                    for g in range(HC):
                        w = slice(V_AT[g] - g * HEAD_DIM, V_AT[g] - g * HEAD_DIM + P)
                        for t in range(KT):
                            last = mm3(bank[:, 0:S], v_hi[:, t, c, w], v_lo[:, t, c, w], pT_hi[:, g * KT + t, :],
                                       pT_lo[:, g * KT + t, :], g == 0 and t == 0, g == HC - 1 and t == KT - 1)
                    last.then_inc(pv_done, 1)

                def o_tile(q):
                    if isinstance(i, int) and i == 1 and q == 0:
                        pe.wait_ge(w_lo_done, 8)
                    bank = shared(use, f"o{q}", i, (a_lo_s, KC, 0))
                    for c in range(KC):
                        last = mm3(bank[:], aT_hi[:, c, q * P:(q + 1) * P], aT_lo[:, c, q * P:(q + 1) * P],
                                   w_hi["o"][:, c, :], w_lo["o"][:, c, :], c == 0, c == KC - 1)
                    last.then_inc(o_done, 1)

                def logits():
                    bank = shared(use, "logits", i, (n_lo_s, QT, 0))
                    for q in range(QT):
                        t = slice(q * P, (q + 1) * P)
                        for c in range(KC):
                            pe.matmul(bank[:, 2 * q * E:2 * (q + 1) * E], tT_hi[:, c, t],
                                      gate[:, c, :, :].rearrange("p a e -> p (a e)"), start=c == 0, stop=False)
                            last = pe.matmul(bank[:, 2 * q * E:(2 * q + 1) * E], tT_lo[:, c, t], gate[:, c, 0, :],
                                             start=False, stop=c == KC - 1)
                    last.then_inc(logits_done, 1)

                def turn_x(q):
                    turn(use, f"xT{q}", x_raw, q, i, (xn_s, QT, QT + q + 1)).then_inc(x_turned, 1)

                def turn_xn2(q):
                    turn(use, f"nT{q}", xn2, q, i, (xn2_s, QT, q + 1 - QT)).then_inc(n_turned, 1)

                def positions():
                    bank = shared(use, "pos", i, (mask_s, 1, 0))
                    for q in range(QT):
                        o = bank[:, q * E:(q + 1) * E]
                        pe.matmul(o, tri_b[:], mask_b[:, q, :], start=True, stop=False)
                        for r in range(q):
                            pe.matmul(o, ones_b[:], mask_b[:, r, :], start=False, stop=False)
                        last = pe.matmul(o, ones_b[:], seen_b[:], start=False, stop=True)
                    last.then_inc(pos_done, 1)

                if kind.attend:
                    v_tile(0)
                if kind.post:
                    pv(i - 1, 3)
                if kind.attend:
                    scores(0)
                    scores(1)
                    v_tile(1)
                if kind.post:
                    o_tile(0)
                    o_tile(1)
                if kind.attend:
                    turn_probs(0)
                    scores(2)
                if kind.prep:
                    project("k", 0)
                if kind.post:
                    turn_xn2(0)
                if kind.attend:
                    scores(3)
                    turn_probs(1)
                if kind.prep:
                    project("k", 1)
                if kind.post:
                    turn_xn2(1)
                if kind.attend:
                    scores(4)
                    turn_probs(2)
                    pv(i, 0)
                if kind.post:
                    logits()
                if kind.prep:
                    turn_x(0)
                if kind.attend:
                    turn_probs(3)
                if kind.prep:
                    turn_x(1)
                if kind.attend:
                    scores(5)
                    scores(6)
                    pv(i, 1)
                    turn_probs(4)
                if kind.prep:
                    project("q", 0)
                if kind.attend:
                    scores(7)
                    turn_probs(5)
                if kind.prep:
                    project("q", 1)
                if kind.attend:
                    pv(i, 2)
                if kind.prep:
                    turn_rows("q", 0)
                if kind.attend:
                    turn_probs(6)
                if kind.post:
                    positions()
                if kind.prep:
                    turn_rows("k", 0)
                    turn_rows("q", 1)
                if kind.attend:
                    turn_probs(7)
                if kind.prep:
                    turn_rows("k", 1)

            pe.wait_ge(in_sem, 16)
            pipeline(pe, body)
            pe.wait_ge(scat_rdy, B)
            pe.wait_ge(pos_read, B)
            bank = plans[-2]["pos"][0]
            pe.transpose(shared_ps[bank][0:E, 0:P], last_tok[:], ident).then_inc(lastT_s, 1)

        @block.scalar
        def _(act):
            act.preload_act_table_set("natural_log_exp_and_others")
            for n, (w, h) in enumerate(halves):
                act.wait_ge(stage_in[n % 2], 16 * (n // 2 + 1))
                act.copy(w_hi[w][:, 2 * h:2 * h + 2, :].rearrange("p c n -> p (c n)"),
                         stage[n % 2]).then_inc(w_hi_done, 1)
            act.wait_ge(vec_sem, 16 * 6)
            act.wait_ge(setup_p, 3)

            def body(i, kind, use):
                def exp_unit(u):
                    q = u % QT
                    act.wait_ge(max_done, UNITS * i + u + 1)
                    need(act, p_turned, UNITS * i + u - 1)
                    need(act, inv_done, UNITS * i + u - 1)
                    if isinstance(i, int) and i == 0 and u == 0:
                        act.wait_ge(w_lo_done, len(halves))
                    for g in range(HC):
                        last = act.activation(probs[:, u % 2, g, :], scores_ps[u % 2][:, g, :], ACT.Exp,
                                              bias=neg_max[:, u % 2, g:g + 1], scale=rms_inv["q"][:, q:q + 1],
                                              accum_out=row_sum[:, u % 2, g:g + 1])
                    last.then_inc(exp_done, 1)

                def turned_hi(u):
                    q = u % QT
                    act.wait_ge(p_turned, UNITS * i + u + 1)
                    act.copy(pT_hi[:, :, q * P:(q + 1) * P], pT_ps[:]).then_inc(p_hi_s, 1)

                def attended_hi(b, c):
                    bank = use[f"pv{c}"][0]
                    act.wait_ge(pv_done, KC * b + c + 1)
                    act.activation(aT_hi[:, c, :], shared_ps[bank][:, 0:S], ACT.Identity,
                                   bias=bv_col[:, c:c + 1]).then_inc(a_hi_s, 1)

                def v_part(t):
                    bank = use[f"v{t}"][0]
                    act.wait_ge(v_done, KT * i + t + 1)
                    need(act, pv_done, KC * i)
                    for src, dst in zip(heads_of(shared_ps[bank][:]), heads_in(v_hi, t)):
                        last = act.copy(dst, src)
                    last.then_inc(v_hi_s, 1)

                def context_hi():
                    act.wait_ge(ctx_in, 16 * (i + 2))
                    need(act, v_done, KT * (i + 1))
                    act.copy(ctx_hi[:], ctx_raw[:]).then_inc(ctx_hi_s, 1)

                def row_squares(n, t):
                    act.wait_ge(biased_s[n], QT * (i + 1) + t + 1)
                    act.activation(squares[:, "kq".index(n), t, :], rows[n][:, t, :], ACT.Square,
                                   accum_out=sq_sum[n][:, t:t + 1]).then_inc(sq_s[n], 1)

                def turned_rows_hi(n, t):
                    bank = use[f"{n}T{t}"][0]
                    act.wait_ge(turned_s[n], QT * (i + 1) + t + 1)
                    if t == 0:
                        need(act, scores_done, UNITS * (i + 1))
                    act.copy(hT[n][0][:, :, t * P:(t + 1) * P],
                             shared_ps[bank][:].rearrange("p (c t) -> p c t", c=KC)).then_inc(hi_s[n], 1)

                def xn2T_hi(q):
                    bank = use[f"nT{q}"][0]
                    act.wait_ge(n_turned, QT * (i - 1) + q + 1)
                    act.copy(tT_hi[:, :, q * P:(q + 1) * P],
                             shared_ps[bank][:].rearrange("p (c t) -> p c t", c=KC)).then_inc(n_hi_s, 1)

                def xT_hi(q):
                    bank = use[f"xT{q}"][0]
                    act.wait_ge(x_turned, QT * (i + 1) + q + 1)
                    act.copy(tT_hi[:, :, q * P:(q + 1) * P],
                             shared_ps[bank][:].rearrange("p (c t) -> p c t", c=KC)).then_inc(x_hi_s, 1)

                def routing_exp():
                    act.wait_ge(lgmax_s, i)
                    for q in range(QT):
                        last = act.activation(score[:, q, :], score[:, q, :], ACT.Exp,
                                              bias=lg_max[:, q:q + 1], accum_out=lg_sum[:, q:q + 1])
                    last.then_inc(lgexp_s, 1)

                if kind.attend:
                    v_part(0)
                if kind.post:
                    attended_hi(i - 1, 3)
                if kind.attend:
                    exp_unit(0)
                    v_part(1)
                    exp_unit(1)
                if kind.prep:
                    context_hi()
                if kind.attend:
                    turned_hi(0)
                    exp_unit(2)
                if kind.post:
                    xn2T_hi(0)
                if kind.prep:
                    row_squares("k", 0)
                if kind.attend:
                    turned_hi(1)
                    exp_unit(3)
                if kind.post:
                    xn2T_hi(1)
                if kind.prep:
                    row_squares("k", 1)
                if kind.attend:
                    exp_unit(4)
                    attended_hi(i, 0)
                    turned_hi(2)
                if kind.prep:
                    xT_hi(0)
                if kind.attend:
                    turned_hi(3)
                if kind.post:
                    routing_exp()
                if kind.prep:
                    xT_hi(1)
                if kind.attend:
                    exp_unit(5)
                    turned_hi(4)
                    attended_hi(i, 1)
                    exp_unit(6)
                    turned_hi(5)
                    exp_unit(7)
                if kind.prep:
                    row_squares("q", 0)
                if kind.attend:
                    attended_hi(i, 2)
                if kind.prep:
                    turned_rows_hi("q", 0)
                if kind.attend:
                    turned_hi(6)
                if kind.prep:
                    row_squares("q", 1)
                    turned_rows_hi("k", 0)
                    turned_rows_hi("q", 1)
                if kind.attend:
                    turned_hi(7)
                if kind.prep:
                    turned_rows_hi("k", 1)

            pipeline(act, body)

        @block.vector
        def _(v):
            class Chain:

                def __init__(self, name, per, b):
                    self.sem, self.per, self.b, self.n = chain[name], per, b, 0

                def step(self, ins):
                    self.n += 1
                    ins.then_inc(self.sem, 1)
                    v.wait_ge(self.sem, self.per * self.b + self.n)

            def settle(n):
                v.memset(settled[0:1, n:n + 1], 0.0)

            PREP_STEPS, POST_STEPS = 2, 29
            v.memset(seen[:], 0.0)
            v.memset(seen_b[:], 0.0)
            v.memset(last_tok[:], 0.0)
            setup = Chain("setup", 0, 0)
            v.wait_ge(in_sem, 16)
            v.tensor_copy(tri_b[:], consts[:, P:2 * P])
            v.tensor_copy(ones_b[:], ones)
            v.wait_ge(vec_sem, 16 * 6)
            raw = x2[:, 0, 0:KC * E].rearrange("p (c e) -> p c e", c=KC)
            v.tensor_tensor(gain_row[:], gain_row[:], bo_row[:], ALU.mult).then_inc(gain_s, 1)
            setup.step(v.tensor_copy(gate[:, :, 0, :], raw))
            v.tensor_tensor(gate[:, :, 1, :], raw, gate[:, :, 0, :].bitcast(F32), ALU.subtract).then_inc(gate_split, 1)
            for n, (w, h) in enumerate(halves):
                v.wait_ge(w_hi_done, n + 1)
                c = slice(2 * h, 2 * h + 2)
                v.tensor_tensor(w_lo[w][:, c, :].rearrange("p c n -> p (c n)"),
                                stage[n % 2],
                                w_hi[w][:, c, :].rearrange("p c n -> p (c n)").bitcast(F32),
                                ALU.subtract).then_inc(w_lo_done, 1)

            def body(i, kind, use):
                prep, attend, post = Chain("prep", PREP_STEPS, i + 1), Chain("attend", UNITS, i), Chain("post", POST_STEPS, i - 1)

                def unit_max(u):
                    v.wait_ge(scores_done, UNITS * i + u + 1)
                    attend.step(v.tensor_reduce(row_max[:, u % 2, :], scores_ps[u % 2][:], X, ALU.max))
                    need(v, exp_done, UNITS * i + u - 1)
                    if u == 0:
                        v.wait_ge(inv_s["q"], i + 1)
                    v.tensor_scalar(neg_max[:, u % 2, :], row_max[:, u % 2, :], rms_inv["q"][:, u % QT:u % QT + 1],
                                    -1.0, ALU.mult, ALU.mult).then_inc(max_done, 1)

                def unit_inv(u):
                    v.wait_ge(exp_done, UNITS * i + u + 1)
                    need(v, probs_done, UNITS * i + u - 1)
                    v.reciprocal(row_inv[:, u % 2, :], row_sum[:, u % 2, :]).then_inc(inv_done, 1)

                def turned_lo(u):
                    c = slice((u % QT) * P, (u % QT + 1) * P)
                    v.wait_ge(p_hi_s, UNITS * i + u + 1)
                    v.tensor_tensor(pT_lo[:, :, c], pT_ps[:], pT_hi[:, :, c].bitcast(F32),
                                    ALU.subtract).then_inc(p_lo_s, 1)

                def attended_lo(b, c):
                    bank = use[f"pv{c}"][0]
                    v.wait_ge(a_hi_s, KC * b + c + 1)
                    v.scalar_tensor_tensor(aT_lo[:, c, :], shared_ps[bank][:, 0:S], bv_col[:, c:c + 1],
                                           aT_hi[:, c, :].bitcast(F32), ALU.add, ALU.subtract).then_inc(a_lo_s, 1)

                def v_part(t):
                    bank = use[f"v{t}"][0]
                    v.wait_ge(v_hi_s, KT * i + t + 1)
                    for src, hi, lo in zip(heads_of(shared_ps[bank][:]), heads_in(v_hi, t), heads_in(v_lo, t)):
                        last = v.tensor_tensor(lo, src, hi.bitcast(F32), ALU.subtract)
                    last.then_inc(v_lo_s, 1)

                def ln_stats_of(src, stats, mv, var, ch, at):
                    for q in range(QT):
                        last = v.bn_stats(stats[:, q, :], src[:, q, :])
                    ch.step(last)
                    settle(at)
                    for q in range(QT):
                        last = v.bn_aggr(mv[:, q, :], stats[:, q, :])
                    ch.step(last)
                    return v.tensor_scalar(var[:], mv[:, :, 1], LN_EPS, None, ALU.add)

                def biased(n, t):
                    bank = use[f"{n}{t}"][0]
                    v.wait_ge(proj[n], QT * (i + 1) + t + 1)
                    if t == 0:
                        need(v, turned_s[n], QT * (i + 1))
                    v.tensor_tensor(rows[n][:, t, :], shared_ps[bank][:], bias_row[n][:], ALU.add).then_inc(biased_s[n], 1)

                def mean_square(n):
                    unit = 1.0 if n == "k" else SCALE * SCALE
                    v.wait_ge(sq_s[n], QT * (i + 2))
                    v.tensor_scalar(mean_sq[n][:], sq_sum[n][:], 1.0 / (D * unit), RMS_EPS / unit, ALU.mult,
                                    ALU.add).then_inc(ms_s[n], 1)

                def k_norm(t):
                    if t == 0:
                        v.wait_ge(inv_s["k"], i + 2)
                    v.scalar_tensor_tensor(rows["k"][:, t, :], rows["k"][:, t, :], rms_inv["k"][:, t:t + 1], gain_row[:],
                                           ALU.mult, ALU.mult).then_inc(k_normed, 1)

                def turned_rows_lo(n, t):
                    bank = use[f"{n}T{t}"][0]
                    c = slice(t * P, (t + 1) * P)
                    v.wait_ge(hi_s[n], QT * (i + 1) + t + 1)
                    v.tensor_tensor(hT[n][1][:, :, c], shared_ps[bank][:].rearrange("p (c t) -> p c t", c=KC),
                                    hT[n][0][:, :, c].bitcast(F32), ALU.subtract).then_inc(lo_s[n], 1)

                def residual(q):
                    if q == 0:
                        v.wait_ge(bo_added, i)
                    v.wait_ge(o_done, QT * (i - 1) + q + 1)
                    v.tensor_tensor(x2[:, q, :], shared_ps[use[f"o{q}"][0]][:], x2[:, q, :], ALU.add).then_inc(x2_s, 1)

                def ln2_stats():
                    v.wait_ge(x2_s, QT * i)
                    ln_stats_of(x2, n2_stats, n2_mv, n2_var, post, 0).then_inc(stats2, 1)

                def ln2_norm(q):
                    if q == 0:
                        v.wait_ge(rstd2, i)
                        need(v, xn2_out, 16 * (i - 1))
                    v.tensor_scalar(xn2[:, q, :], x2[:, q, :], n2_mv[:, q, 0:1], n2_rstd[:, q:q + 1],
                                    ALU.subtract, ALU.mult).then_inc(xn2_s, 1)

                def ln1_stats():
                    v.wait_ge(x_in, 16 * (i + 2))
                    ln_stats_of(x_raw, ln_stats, ln_mv, ln_var, prep, 1).then_inc(stats1, 1)

                def ln1_norm(q):
                    if q == 0:
                        v.wait_ge(rstd1, i + 2)
                    v.tensor_scalar(x_raw[:, q, :], x_raw[:, q, :], ln_mv[:, q, 0:1], ln_rstd[:, q:q + 1],
                                    ALU.subtract, ALU.mult).then_inc(xn_s, 1)

                def xn2T_lo(q):
                    c = slice(q * P, (q + 1) * P)
                    v.wait_ge(n_hi_s, QT * (i - 1) + q + 1)
                    v.tensor_tensor(tT_lo[:, :, c], shared_ps[use[f"nT{q}"][0]][:]
                                    .rearrange("p (c t) -> p c t", c=KC), tT_hi[:, :, c].bitcast(F32),
                                    ALU.subtract).then_inc(n_lo_s, 1)

                def xT_lo(q):
                    c = slice(q * P, (q + 1) * P)
                    v.wait_ge(x_hi_s, QT * (i + 1) + q + 1)
                    v.tensor_tensor(tT_lo[:, :, c], shared_ps[use[f"xT{q}"][0]][:]
                                    .rearrange("p (c t) -> p c t", c=KC), tT_hi[:, :, c].bitcast(F32),
                                    ALU.subtract).then_inc(x_lo_s, 1)

                def logit_max():
                    parts = shared_ps[use["logits"][0]][:, 0:2 * QT * E].rearrange("p (q a e) -> p q a e", q=QT, a=2)
                    v.wait_ge(logits_done, i)
                    post.step(v.tensor_copy(score[:], parts[:, :, 1, :]))
                    post.step(v.tensor_tensor(score[:], parts[:, :, 0, :], score[:], ALU.add))
                    post.step(v.tensor_reduce(lg_max[:], score[:], X, ALU.max))
                    v.tensor_scalar(lg_max[:], lg_max[:], -1.0, None, ALU.mult).then_inc(lgmax_s, 1)

                groups = score[:].rearrange("p q e -> p (q e)").rearrange("p (g e) -> p g e", e=GE)

                def best_groups():
                    v.wait_ge(lgexp_s, i)
                    post.step(v.reciprocal(lg_sum[:], lg_sum[:]))
                    post.step(v.tensor_tensor(score[:], score[:], lg_sum[:].unsqueeze(2).to_broadcast([P, QT, E]),
                                              ALU.mult))
                    post.step(v.tensor_reduce(g_score[:].rearrange("p q g -> p (q g)"), groups, X, ALU.max))
                    settle(2)
                    for q in range(QT):
                        last = v.max(g_top[:, q, :], g_score[:, q, :])
                    post.step(last)
                    settle(3)
                    for q in range(QT):
                        last = v.max_index(g_idx[:, q, :], g_top[:, q, :], g_score[:, q, :])
                    post.step(last)
                    post.step(v.tensor_copy(g_idxf[:], g_idx[:]))
                    post.step(v.tensor_tensor(
                        g_hot[:], iota_g.unsqueeze(1).unsqueeze(1).to_broadcast([P, QT, TOPK_GROUP, N_GROUP]),
                        g_idxf[:, :, 0:TOPK_GROUP].unsqueeze(3).to_broadcast([P, QT, TOPK_GROUP, N_GROUP]),
                        ALU.is_equal))
                    post.step(v.tensor_reduce(g_mask[:], g_hot[:].rearrange("p q k g -> p q g k"), X, ALU.add))
                    post.step(v.tensor_tensor(groups, groups, g_mask[:].rearrange("p q g -> p (q g)").unsqueeze(2)
                                              .to_broadcast([P, QT * N_GROUP, GE]), ALU.mult))
                    settle(4)
                    for q in range(QT):
                        last = v.max(e_top[:, q, :], score[:, q, :])
                    post.step(last)

                def best_experts():
                    settle(5)
                    for q in range(QT):
                        last = v.max_index(e_idx[:, q, :], e_top[:, q, :], score[:, q, :])
                    post.step(last)
                    post.step(v.tensor_copy(e_idxf[:], e_idx[:]))
                    post.step(v.tensor_tensor(
                        e_hot[:], iota_e.unsqueeze(1).unsqueeze(1).to_broadcast([P, QT, TOP_K, E]),
                        e_idxf[:, :, 0:TOP_K].unsqueeze(3).to_broadcast([P, QT, TOP_K, E]), ALU.is_equal))
                    post.step(v.tensor_reduce(mask_f[:], e_hot[:].rearrange("p q k e -> p q e k"), X, ALU.add))
                    v.tensor_copy(mask_b[:], mask_f[:]).then_inc(mask_s, 1)
                    for q in range(QT):
                        post.step(v.scalar_tensor_tensor(last_tok[:], mask_f[:, q, :], tok_col[:, q:q + 1],
                                                         last_tok[:], ALU.mult, ALU.max))
                    v.memset(settled[0:1, 6:7], 0.0)
                    v.tensor_copy(keep["weight"][:, bass.ds((i - 1) * QT * TOP_K, QT * TOP_K)]
                                  .rearrange("p (q k) -> p q k", q=QT), e_top[:, :, 0:TOP_K])

                def slot_values():
                    v.wait_ge(pos_done, i)
                    v.scalar_tensor_tensor(slot_val[:], shared_ps[use["pos"][0]][:, 0:QT * E]
                                           .rearrange("p (q e) -> p q e", q=QT), float(CAPACITY - 1),
                                           slot_base.unsqueeze(1).to_broadcast([P, QT, E]), ALU.min,
                                           ALU.add).then_inc(pos_read, 1)

                def slots():
                    for q in range(QT):
                        post.step(v.tensor_tensor(seen[:], seen[:], mask_f[:, q, :], ALU.add))
                    v.tensor_copy(seen_b[:], seen[:])
                    v.wait_ge(pos_read, i)
                    post.step(v.tensor_tensor(e_slot[:], e_hot[:], slot_val[:].unsqueeze(2)
                                              .to_broadcast([P, QT, TOP_K, E]), ALU.mult))
                    post.step(v.tensor_reduce(slot_f[:], e_slot[:], X, ALU.add))

                def scatter_index():
                    v.memset(settled[0:1, 7:8], 0.0)
                    v.tensor_copy(keep["slot"][:, bass.ds((i - 1) * QT * TOP_K, QT * TOP_K)],
                                  slot_f[:].rearrange("p q k -> p (q k)"))
                    post.step(v.tensor_scalar(last_slot[:], e_idxf[:, :, 0:TOP_K], float(CAPACITY),
                                              float(CAPACITY - 1), ALU.mult, ALU.add))
                    post.step(v.tensor_tensor(is_last[:], slot_f[:], last_slot[:], ALU.is_equal))
                    post.step(v.scalar_tensor_tensor(scat_f[:], is_last[:], OVER, slot_f[:], ALU.mult, ALU.add))
                    need(v, scattered, 16 * QT * TOP_K * (i - 1))
                    v.tensor_copy(scat_idx[:], scat_f[:].rearrange("p q k -> p (q k)"))
                    v.tensor_scalar(scat_tok[:], tok_col, -1.0, None, ALU.add).then_inc(scat_rdy, 1)
                    post.step(v.tensor_scalar(tok_col, tok_col, float(S), None, ALU.add))

                if kind.attend:
                    v_part(0)
                if kind.post:
                    attended_lo(i - 1, 3)
                if kind.attend:
                    unit_max(0)
                    unit_max(1)
                    unit_inv(0)
                    v_part(1)
                if kind.prep:
                    ln1_stats()
                if kind.post:
                    residual(0)
                    residual(1)
                if kind.attend:
                    unit_inv(1)
                if kind.post:
                    ln2_stats()
                if kind.attend:
                    unit_max(2)
                if kind.post:
                    ln2_norm(0)
                if kind.attend:
                    turned_lo(0)
                if kind.prep:
                    biased("k", 0)
                if kind.post:
                    ln2_norm(1)
                if kind.attend:
                    unit_max(3)
                if kind.post:
                    xn2T_lo(0)
                if kind.prep:
                    ln1_norm(0)
                if kind.attend:
                    unit_inv(2)
                    turned_lo(1)
                    unit_inv(3)
                if kind.prep:
                    biased("k", 1)
                if kind.attend:
                    unit_max(4)
                if kind.post:
                    xn2T_lo(1)
                if kind.prep:
                    mean_square("k")
                    ln1_norm(1)
                if kind.attend:
                    attended_lo(i, 0)
                    turned_lo(2)
                if kind.prep:
                    k_norm(0)
                if kind.post:
                    logit_max()
                if kind.prep:
                    xT_lo(0)
                if kind.attend:
                    unit_inv(4)
                if kind.prep:
                    k_norm(1)
                if kind.attend:
                    turned_lo(3)
                    unit_max(5)
                if kind.prep:
                    xT_lo(1)
                if kind.post:
                    best_groups()
                if kind.attend:
                    unit_inv(5)
                    unit_max(6)
                    turned_lo(4)
                if kind.prep:
                    biased("q", 0)
                if kind.attend:
                    attended_lo(i, 1)
                    unit_max(7)
                    turned_lo(5)
                    unit_inv(6)
                if kind.prep:
                    biased("q", 1)
                if kind.post:
                    best_experts()
                if kind.attend:
                    attended_lo(i, 2)
                    unit_inv(7)
                if kind.prep:
                    turned_rows_lo("q", 0)
                if kind.post:
                    slot_values()
                if kind.attend:
                    turned_lo(6)
                if kind.prep:
                    mean_square("q")
                    turned_rows_lo("k", 0)
                    turned_rows_lo("q", 1)
                if kind.attend:
                    turned_lo(7)
                if kind.prep:
                    turned_rows_lo("k", 1)
                if kind.post:
                    slots()
                    scatter_index()
                assert prep.n in (0, PREP_STEPS) and attend.n in (0, UNITS) and post.n in (0, POST_STEPS)

            pipeline(v, body)
            v.wait_ge(lastT_s, 1)
            bank = plans[-2]["pos"][0]
            end = Chain("setup", 1, 1)
            end.step(v.tensor_reduce(lastT[:], shared_ps[bank][0:E, 0:P], X, ALU.max))
            end.step(v.tensor_scalar(lastT[:], lastT[:], -1.0, 0.0, ALU.add, ALU.max))
            v.tensor_copy(lastT_i[:], lastT[:]).then_inc(last_i_s, 1)

        @block.gpsimd
        def _(g):
            g.memset(zero_i[:], 0).then_inc(setup_p, 1)
            g.memset(v_hi[:].bitcast(F32), 0.0).then_inc(setup_p, 1)
            g.memset(v_lo[:].bitcast(F32), 0.0).then_inc(setup_p, 1)
            g.memset(minus_half[:], -0.5).then_inc(setup_p, 1)
            g.wait_ge(setup_p, 4)
            g.wait_ge(vec_sem, 16 * 6)
            g.wait_ge(table_zeroed, 16)

            def body(i, kind, use):
                def norm_unit(u):
                    if kind.scatter and u == 0:
                        g.wait_ge(scat_rdy, i - 1)
                    g.wait_ge(inv_done, UNITS * i + u + 1)
                    pr = probs[:, u % 2, :, :]
                    g.tensor_tensor(pr, pr, row_inv[:, u % 2, :].unsqueeze(2).to_broadcast([P, HC, CK]),
                                    ALU.mult).then_inc(probs_done, 1)

                def context_lo():
                    g.wait_ge(ctx_hi_s, i + 2)
                    g.tensor_tensor(ctx_lo[:], ctx_raw[:], ctx_hi[:].bitcast(F32), ALU.subtract).then_inc(ctx_lo_s, 1)

                def add_bo():
                    if isinstance(i, int) and i == 1:
                        g.wait_ge(bo_in, 16)
                    g.wait_ge(res_in, 16 * i)
                    g.tensor_tensor(x2[:], x2[:], bo_row[:].unsqueeze(1).to_broadcast([P, QT, D]),
                                    ALU.add).then_inc(bo_added, 1)

                def ln2_rstd():
                    g.wait_ge(stats2, i)
                    g.tensor_tensor(n2_rstd[:], n2_var[:], minus_half[:], ALU.pow).then_inc(rstd2, 1)

                def ln1_rstd():
                    g.wait_ge(stats1, i + 2)
                    g.tensor_tensor(ln_rstd[:], ln_var[:], minus_half[:], ALU.pow).then_inc(rstd1, 1)

                def rms_inverse(n):
                    g.wait_ge(ms_s[n], i + 2)
                    if n == "q":
                        need(g, exp_done, UNITS * (i + 1))
                    g.tensor_tensor(rms_inv[n][:], mean_sq[n][:], minus_half[:], ALU.pow).then_inc(inv_s[n], 1)

                def scatter(s):
                    if not kind.attend and s == 0:
                        g.wait_ge(scat_rdy, i - 1)
                    for j in (2 * s, 2 * s + 1):
                        q = j // TOP_K
                        g.indirect_dma_start(
                            out=d["table"], out_offset=bass.IndirectOffsetOnAxis(ap=scat_idx[:, j:j + 1], axis=0),
                            in_=scat_tok[:, q:q + 1], in_offset=None, bounds_check=E * CAPACITY - 1,
                            oob_is_err=False).then_inc(scattered, 16)

                if kind.post:
                    add_bo()
                if kind.attend:
                    norm_unit(0)
                if kind.prep:
                    context_lo()
                if kind.post:
                    ln2_rstd()
                if kind.attend:
                    norm_unit(1)
                if kind.prep:
                    ln1_rstd()
                if kind.attend:
                    norm_unit(2)
                if kind.scatter:
                    scatter(0)
                    scatter(1)
                if kind.prep:
                    rms_inverse("k")
                if kind.attend:
                    norm_unit(3)
                    norm_unit(4)
                if kind.scatter:
                    scatter(2)
                if kind.attend:
                    norm_unit(5)
                    norm_unit(6)
                    norm_unit(7)
                if kind.prep:
                    rms_inverse("q")
                if kind.scatter:
                    scatter(3)
                    scatter(4)
                    scatter(5)

            pipeline(g, body)
            g.wait_ge(scattered, 16 * QT * TOP_K * B)


def phase_b(nc, d):
    E = d["experts"].shape[0]
    D = d["xn2"].shape[-1]
    KC = D // P
    M = d["m"]
    ROWS = CAPACITY // 2
    MC = -(-M // P)
    col = [min(m * P, M - P) for m in range(MC)]
    GU, DN = 2 * KC * M, MC * D

    with ExitStack() as ctx:
        def sb(name, shape, dt=F32):
            return ctx.enter_context(nc.sbuf_tensor(name, shape, dt))

        def ps(name, shape, dt=F32):
            return ctx.enter_context(nc.psum_tensor(name, shape, dt))

        def sem(name):
            return ctx.enter_context(nc.semaphore(name))

        ident = sb("b_ident", [P, P])
        table_i, table_f = sb("table_i", [P, ROWS], I32), sb("table_f", [P, ROWS])
        idxT = sb("idxT", [ROWS, 2 * E], I32)
        idx_now = sb("idx_now", [ROWS, 2, 2], I32)
        rows = sb("rows", [ROWS, 2, 2, D])
        gu_raw, dn_raw = sb("gu_raw", [P, 2, GU]), sb("dn_raw", [P, 2, DN])
        gu_hi, gu_lo = sb("gu_hi", [P, 2, GU], F32R), sb("gu_lo", [P, 2, GU], F32R)
        dn_hi, dn_lo = sb("dn_hi", [P, 2, MC, D], F32R), sb("dn_lo", [P, 2, MC, D], F32R)
        bT_hi, bT_lo = sb("bT_hi", [P, 2, KC, CAPACITY], F32R), sb("bT_lo", [P, 2, KC, CAPACITY], F32R)
        gate_act, hid = sb("gate_act", [P, MC, CAPACITY]), sb("hid", [P, MC, CAPACITY])
        h_hi, h_lo = sb("h_hi", [P, 2, MC, CAPACITY], F32R), sb("h_lo", [P, 2, MC, CAPACITY], F32R)
        out_rows = sb("out_rows", [ROWS, 2, 2, D])

        gu_ps = [ps(f"gu_ps{m}", [P, 512]) for m in range(MC)]
        bT_ps = [ps(f"bT_ps{n}", [P, 512]) for n in range(2)]
        dn_ps = [ps(f"dn_ps{t}", [P, 512]) for t in range(2)]

        setup_in, idx_f_s, idx_turned, idx_s = (sem("b_table_loaded"), sem("b_table_float"), sem("b_table_turned"),
                                                sem("b_index_ready"))
        gu_in, dn_in, rows_in, stored = ([sem(f"b_{what}{n}") for n in range(2)]
                                         for what in ("gu_loaded", "down_loaded", "rows_gathered", "out_stored"))
        staged = sem("b_index_staged")
        turned, bT_hi_s, bT_lo_s = sem("b_rows_turned"), sem("b_rowsT_hi_done"), sem("b_rowsT_lo_done")
        gu_hi_s, gu_lo_s = sem("b_gu_hi_done"), sem("b_gu_lo_done")
        dn_hi_s, dn_lo_s = sem("b_down_hi_done"), sem("b_down_lo_done")
        gu_done, act_s, hid_s = sem("b_gu_product_done"), sem("b_silu_done"), sem("b_hidden_done")
        h_hi_s, h_lo_s = sem("b_hidden_hi_done"), sem("b_hidden_lo_done")
        dn_done, out_s = sem("b_down_product_done"), sem("b_out_copied")

        def pipeline(eng, body):
            for e in (-1, 0, 1, 2):
                body(e, e % 2, e // 2)
            with eng.Fori(0, (E - 6) // 2) as j:
                for s in range(2):
                    body(2 * j + (3 + s), (3 + s) % 2, j + (3 + s) // 2)
            for e in (E - 3, E - 2, E - 1, E):
                body(e, e % 2, e // 2)

        def at_most(e, last):
            return not isinstance(e, int) or e <= last

        def at_least(e, first):
            return not isinstance(e, int) or e >= first

        block = ctx.enter_context(nc.Block())

        @block.sync
        def _(sp):
            sp.dma_start(table_i[:], d["table"].rearrange("(k r) o -> k (r o)", r=ROWS)).then_inc(setup_in, 16)
            sp.dma_start(ident[:], d["consts"][:, 0:P]).then_inc(setup_in, 16)

            def body(e, par, half):
                if not at_most(e, E - 2):
                    return
                need(sp, gu_hi_s, e)
                need(sp, gu_lo_s, e)
                sp.dma_start(gu_raw[:, 1 - par, :], d["experts"][e + 1][:, 0:GU]).then_inc(gu_in[1 - par], 16)
                need(sp, dn_hi_s, e)
                need(sp, dn_lo_s, e)
                sp.dma_start(dn_raw[:, 1 - par, :], d["experts"][e + 1][:, GU:GU + DN]).then_inc(dn_in[1 - par], 16)

            pipeline(sp, body)

        @block.tensor
        def _(pe):
            def mm3(out, a_hi, a_lo, b_hi, b_lo, first, last):
                pe.matmul(out, a_hi, b_hi, start=first, stop=False)
                pe.matmul(out, a_hi, b_lo, start=False, stop=False)
                return pe.matmul(out, a_lo, b_hi, start=False, stop=last)

            pe.wait_ge(setup_in, 32)
            pe.wait_ge(idx_f_s, 1)
            pe.transpose(bT_ps[0][0:ROWS, 0:P], table_f[:], ident[:]).then_inc(idx_turned, 1)

            def body(e, par, half):
                def turn_rows():
                    nxt = 1 - par
                    pe.wait_ge(rows_in[nxt], 32 * (half + par + 1))
                    if isinstance(e, int) and e < 0:
                        pe.wait_ge(idx_s, 1)
                    for n in range(2):
                        need(pe, bT_lo_s, 2 * e + n + 1 if at_least(e, 0) else 0)
                        for k in range(2):
                            for t in range(2):
                                c = (2 * n + k) * P
                                last = pe.transpose(bT_ps[n][:, k * CAPACITY + t * ROWS:k * CAPACITY + (t + 1) * ROWS],
                                                    rows[:, nxt, t, c:c + P], ident[0:ROWS, 0:ROWS])
                        last.then_inc(turned, 1)

                def gate_up(m):
                    if m == 0:
                        pe.wait_ge(bT_lo_s, 2 * (e + 1))
                        pe.wait_ge(gu_hi_s, e + 1)
                        pe.wait_ge(gu_lo_s, e + 1)
                    need(pe, hid_s, MC * e + (m + 1 - MC) if at_least(e, 1) else 0)
                    for g in range(2):
                        for kc in range(KC):
                            w = (g * KC + kc) * M + col[m]
                            last = mm3(gu_ps[m][:, g * CAPACITY:(g + 1) * CAPACITY], gu_hi[:, par, w:w + P],
                                       gu_lo[:, par, w:w + P], bT_hi[:, par, kc, :], bT_lo[:, par, kc, :],
                                       kc == 0, kc == KC - 1)
                    last.then_inc(gu_done, 1)

                def down(t):
                    o = 1 - par
                    if t == 0:
                        pe.wait_ge(h_lo_s, MC * e)
                        pe.wait_ge(dn_hi_s, e)
                        pe.wait_ge(dn_lo_s, e)
                    need(pe, out_s, 2 * e + (t - 3))
                    r = slice(t * ROWS, (t + 1) * ROWS)
                    for m in range(MC):
                        last = mm3(dn_ps[t][0:ROWS, :], h_hi[:, o, m, r], h_lo[:, o, m, r], dn_hi[:, o, m, :],
                                   dn_lo[:, o, m, :], m == 0, m == MC - 1)
                    last.then_inc(dn_done, 1)

                mid = at_least(e, 0) and at_most(e, E - 1)
                if mid:
                    gate_up(0)
                if at_most(e, E - 2):
                    turn_rows()
                if mid:
                    gate_up(1)
                    gate_up(2)
                if at_least(e, 1):
                    down(0)
                    down(1)

            pipeline(pe, body)

        @block.scalar
        def _(act):
            def body(e, par, half):
                ahead, mid, late = at_most(e, E - 2), at_least(e, 0) and at_most(e, E - 1), at_least(e, 1)

                def rows_hi(n):
                    act.wait_ge(turned, 2 * e + (n + 3))
                    act.copy(bT_hi[:, 1 - par, 2 * n:2 * n + 2, :].rearrange("p k t -> p (k t)"),
                             bT_ps[n][:, 0:2 * CAPACITY]).then_inc(bT_hi_s, 1)

                def silu(m):
                    act.wait_ge(gu_done, MC * e + (m + 1))
                    act.activation(gate_act[:, m, :], gu_ps[m][:, 0:CAPACITY], ACT.Silu).then_inc(act_s, 1)

                def hidden_hi(m):
                    act.wait_ge(hid_s, MC * e + (m + 1))
                    act.copy(h_hi[:, par, m, :], hid[:, m, :]).then_inc(h_hi_s, 1)

                if mid:
                    silu(0)
                if ahead:
                    rows_hi(0)
                    rows_hi(1)
                if mid:
                    hidden_hi(0)
                if ahead:
                    act.wait_ge(gu_in[1 - par], 16 * (half + par + 1))
                    act.copy(gu_hi[:, 1 - par, :], gu_raw[:, 1 - par, :]).then_inc(gu_hi_s, 1)
                if mid:
                    silu(1)
                    hidden_hi(1)
                    act.wait_ge(dn_in[par], 16 * (half + 1))
                    act.copy(dn_hi[:, par, :, :].rearrange("p m n -> p (m n)"), dn_raw[:, par, :]).then_inc(dn_hi_s, 1)
                    silu(2)
                    hidden_hi(2)
                if late:
                    o = 1 - par
                    need(act, stored[o], 16 * (half + par - 1))
                    for t in range(2):
                        act.wait_ge(dn_done, 2 * e + (t - 1))
                        act.copy(out_rows[:, o, t, :], dn_ps[t][0:ROWS, :]).then_inc(out_s, 1)
                    act.wait_ge(out_s, 2 * e)
                    act.dma_start(d["eo"].rearrange("(e t r) n -> e r t n", t=2, r=ROWS)[e - 1],
                                  out_rows[:, o, :, :]).then_inc(stored[o], 16)

            pipeline(act, body)
            for n in range(2):
                act.wait_ge(stored[n], 16 * (E // 2))

        @block.vector
        def _(v):
            v.wait_ge(setup_in, 32)
            v.tensor_copy(table_f[:], table_i[:]).then_inc(idx_f_s, 1)
            v.wait_ge(idx_turned, 1)
            v.tensor_copy(idxT[:, 0:2 * E], bT_ps[0][0:ROWS, 0:P]).then_inc(idx_s, 1)

            def body(e, par, half):
                ahead, mid = at_most(e, E - 2), at_least(e, 0) and at_most(e, E - 1)

                def hidden(m):
                    v.wait_ge(act_s, MC * e + (m + 1))
                    v.tensor_tensor(hid[:, m, :], gate_act[:, m, :], gu_ps[m][:, CAPACITY:2 * CAPACITY],
                                    ALU.mult).then_inc(hid_s, 1)

                def hidden_lo(m):
                    v.wait_ge(h_hi_s, MC * e + (m + 1))
                    v.tensor_tensor(h_lo[:, par, m, :], hid[:, m, :], h_hi[:, par, m, :].bitcast(F32),
                                    ALU.subtract).then_inc(h_lo_s, 1)

                if mid:
                    hidden(0)
                if ahead:
                    for n in range(2):
                        v.wait_ge(bT_hi_s, 2 * e + (n + 3))
                        v.tensor_tensor(bT_lo[:, 1 - par, 2 * n:2 * n + 2, :].rearrange("p k t -> p (k t)"),
                                        bT_ps[n][:, 0:2 * CAPACITY],
                                        bT_hi[:, 1 - par, 2 * n:2 * n + 2, :].rearrange("p k t -> p (k t)").bitcast(F32),
                                        ALU.subtract).then_inc(bT_lo_s, 1)
                if mid:
                    hidden_lo(0)
                    hidden(1)
                    hidden_lo(1)
                if ahead:
                    v.wait_ge(gu_hi_s, e + 2)
                    v.tensor_tensor(gu_lo[:, 1 - par, :], gu_raw[:, 1 - par, :], gu_hi[:, 1 - par, :].bitcast(F32),
                                    ALU.subtract).then_inc(gu_lo_s, 1)
                if mid:
                    hidden(2)
                    hidden_lo(2)

            pipeline(v, body)

        @block.gpsimd
        def _(g):
            def stage(expert, place):
                g.tensor_copy(idx_now[:, place, :], idxT[:, bass.ds(2 * expert, 2)]).then_inc(staged, 1)

            def gather(place):
                for t in range(2):
                    g.indirect_dma_start(
                        out=rows[:, place, t, :], out_offset=None, in_=d["xn2_rows"],
                        in_offset=bass.IndirectOffsetOnAxis(ap=idx_now[:, place, t:t + 1], axis=0),
                    ).then_inc(rows_in[place], 16)

            def body(e, par, half):
                nxt = 1 - par
                if isinstance(e, int) and e < 0:
                    g.wait_ge(idx_s, 1)
                    for n in range(2):
                        stage(n, n)
                        g.wait_ge(staged, n + 1)
                        gather(n)
                    g.wait_ge(rows_in[0], 32)
                    stage(2, 0)
                    return
                if at_most(e, E - 3):
                    g.wait_ge(turned, 2 * e + 2)
                    g.wait_ge(staged, e + 3)
                    g.wait_ge(rows_in[nxt], 32 * (half + par + 1))
                if at_least(e, 1):
                    g.wait_ge(dn_hi_s, e)
                    g.tensor_tensor(dn_lo[:, nxt, :, :].rearrange("p m n -> p (m n)"), dn_raw[:, nxt, :],
                                    dn_hi[:, nxt, :, :].rearrange("p m n -> p (m n)").bitcast(F32),
                                    ALU.subtract).then_inc(dn_lo_s, 1)
                if at_most(e, E - 3):
                    gather(par)
                    if at_most(e, E - 4):
                        stage(e + 3, nxt)

            pipeline(g, body)


def phase_c(nc, d, keep):
    T, D = d["xn2_rows"].shape
    KC = D // P
    MS = d["sg"].shape[2]
    MC = -(-MS // P)
    col = [min(m * P, MS - P) for m in range(MC)]
    GT = 4
    GROUPS = T // (GT * P)
    NT = GT * P
    POOL_LO = GT

    with ExitStack() as ctx:
        def sb(name, shape, dt=F32):
            return ctx.enter_context(nc.sbuf_tensor(name, shape, dt))

        def ps(name, shape, dt=F32):
            return ctx.enter_context(nc.psum_tensor(name, shape, dt))

        def sem(name):
            return ctx.enter_context(nc.semaphore(name))

        ident = sb("c_ident", [P, P])
        raw = [sb(f"c_raw{n}", [P, max(KC * MS, MC * D)]) for n in range(2)]
        sg = [sb(f"sg_{part}", [P, KC, MS], F32R) for part in ("hi", "lo")]
        su = [sb(f"su_{part}", [P, KC, MS], F32R) for part in ("hi", "lo")]
        sd = [sb(f"sd_{part}", [P, MC, D], F32R) for part in ("hi", "lo")]
        x_rows = sb("c_x_rows", [P, GT, D])
        xT_hi, xT_lo = sb("c_xT_hi", [P, KC, NT], F32R), sb("c_xT_lo", [P, KC, NT], F32R)
        gate_act, hid = sb("c_gate_act", [P, 2, NT]), sb("c_hid", [P, 2, NT])
        h_hi, h_lo = sb("c_h_hi", [P, MC, NT], F32R), sb("c_h_lo", [P, MC, NT], F32R)
        idx_now = sb("c_idx_now", [P, GT * TOP_K], U32)
        w_now = sb("c_w_now", [P, GT * TOP_K])
        rows = sb("c_rows", [P, 2, TOP_K, D])
        acc = sb("c_acc", [P, GT, D])
        out_rows = sb("c_out_rows", [P, 2, D])

        xT_ps = [ps(f"c_xT_ps{n}", [P, NT]) for n in range(2)]
        g_ps, u_ps = [ps(f"c_g_ps{n}", [P, NT]) for n in range(2)], [ps(f"c_u_ps{n}", [P, NT]) for n in range(2)]
        dn_ps = [ps(f"c_dn_ps{n}", [P, D]) for n in range(2)]

        id_in, w_in = sem("c_ident_loaded"), [sem(f"c_weight_loaded{n}") for n in range(3)]
        w_hi_s, w_lo_s = sem("c_weight_hi_done"), sem("c_weight_lo_done")
        x_in, acc_in = sem("c_rows_loaded"), sem("c_residual_loaded")
        turned, xT_hi_s, xT_lo_s = sem("c_rows_turned"), sem("c_rowsT_hi_done"), sem("c_rowsT_lo_done")
        gu_done, act_s, hid_s = sem("c_gu_product_done"), sem("c_silu_done"), sem("c_hidden_done")
        h_hi_s, h_lo_v, h_lo_p = sem("c_hidden_hi_done"), sem("c_hidden_lo_by_vector"), sem("c_hidden_lo_by_pool")
        staged = sem("c_index_staged")
        gathered = [sem(f"c_gathered{n}") for n in range(2)]
        routed_s, step_s = sem("c_routed_done"), sem("c_routed_step")
        dn_done, out_s = sem("c_down_product_done"), sem("c_out_done")
        stored = [sem(f"c_out_stored{n}") for n in range(2)]

        def pipeline(eng, body):
            for g in (-1, 0):
                body(g)
            with eng.Fori(1, GROUPS - 1) as g:
                body(g)
            body(GROUPS - 1)

        def is_int(g):
            return isinstance(g, int)

        block = ctx.enter_context(nc.Block())

        @block.sync
        def _(sp):
            sp.dma_start(ident[:], d["consts"][:, 0:P]).then_inc(id_in, 16)
            rows_of = d["xn2_rows"].rearrange("(g q p) n -> g p q n", q=GT, p=P)
            x2_of = d["x2_rows"].rearrange("(g q p) n -> g p q n", q=GT, p=P)
            out_of = d["out"].rearrange("(g q p) n -> g p q n", q=GT, p=P)
            sp.dma_start(x_rows[:], rows_of[0]).then_inc(x_in, 16)
            sp.dma_start(raw[0][:, 0:KC * MS], d["sg"].rearrange("p c m -> p (c m)")).then_inc(w_in[0], 16)
            sp.dma_start(raw[1][:, 0:KC * MS], d["su"].rearrange("p c m -> p (c m)")).then_inc(w_in[1], 16)
            sp.wait_ge(w_hi_s, 1)
            sp.wait_ge(w_lo_s, 1)
            sp.dma_start(raw[0][:, 0:MC * D], d["sd"].rearrange("p c m -> p (c m)")).then_inc(w_in[2], 16)

            def body(g):
                if is_int(g) and g < 0:
                    sp.dma_start(acc[:], x2_of[0]).then_inc(acc_in, 16)
                    return
                if not (is_int(g) and g == GROUPS - 1):
                    sp.wait_ge(turned, KC * (g + 1))
                    sp.dma_start(x_rows[:], rows_of[g + 1]).then_inc(x_in, 16)
                for q in range(GT):
                    sp.wait_ge(out_s, GT * g + (q + 1))
                    sp.dma_start(out_of[g][:, q, :], out_rows[:, q % 2, :]).then_inc(stored[q % 2], 16)
                if not (is_int(g) and g == GROUPS - 1):
                    sp.dma_start(acc[:], x2_of[g + 1]).then_inc(acc_in, 16)

            pipeline(sp, body)
            for n in range(2):
                sp.wait_ge(stored[n], 16 * GROUPS * GT // 2)

        @block.tensor
        def _(pe):
            def mm3(out, a, b, a_at, b_at, first, last):
                pe.matmul(out, a[0][a_at], b[0][b_at], start=first, stop=False)
                pe.matmul(out, a[0][a_at], b[1][b_at], start=False, stop=False)
                return pe.matmul(out, a[1][a_at], b[0][b_at], start=False, stop=last)

            full = slice(None)

            def body(g):
                def turn_rows():
                    pe.wait_ge(x_in, 16 * (g + 2))
                    for kc in range(KC):
                        need(pe, xT_lo_s, KC * g + (KC + kc - 1) if not (is_int(g) and g < 0) else kc - 1)
                        for q in range(GT):
                            last = pe.transpose(xT_ps[kc % 2][:, q * P:(q + 1) * P], x_rows[:, q, kc * P:(kc + 1) * P],
                                                ident[:])
                        last.then_inc(turned, 1)

                def gate_up(m):
                    if m == 0:
                        pe.wait_ge(xT_lo_s, KC * (g + 1))
                    need(pe, hid_s, MC * g + (m - 1))
                    for n, (bank, w) in enumerate(((g_ps[m % 2], sg), (u_ps[m % 2], su))):
                        if is_int(g) and g == 0 and m == 0:
                            pe.wait_ge(w_lo_s, n + 1)
                        for kc in range(KC):
                            last = mm3(bank[:], w, (xT_hi, xT_lo), (full, kc, slice(col[m], col[m] + P)),
                                       (full, kc, full), kc == 0, kc == KC - 1)
                        last.then_inc(gu_done, 1)

                def down(q):
                    if q == 0:
                        pe.wait_ge(h_lo_p, POOL_LO * (g + 1))
                        pe.wait_ge(h_lo_v, (MC - POOL_LO) * (g + 1))
                        if is_int(g) and g == 0:
                            pe.wait_ge(w_lo_s, 3)
                    need(pe, out_s, GT * g + (q - 1))
                    for m in range(MC):
                        last = mm3(dn_ps[q % 2][:], (h_hi, h_lo), sd, (full, m, slice(q * P, (q + 1) * P)),
                                   (full, m, full), m == 0, m == MC - 1)
                    last.then_inc(dn_done, 1)

                if is_int(g) and g < 0:
                    pe.wait_ge(id_in, 16)
                    turn_rows()
                    return
                for m in range(MC):
                    gate_up(m)
                if not (is_int(g) and g == GROUPS - 1):
                    turn_rows()
                for q in range(GT):
                    down(q)

            pipeline(pe, body)

        @block.scalar
        def _(act):
            for n, (w, size) in enumerate(((sg, KC * MS), (su, KC * MS), (sd, MC * D))):
                act.wait_ge(w_in[n], 16)
                act.copy(w[0][:].rearrange("p c m -> p (c m)"), raw[n % 2][:, 0:size]).then_inc(w_hi_s, 1)

            def body(g):
                def rows_hi():
                    for kc in range(KC):
                        act.wait_ge(turned, KC * (g + 1) + (kc + 1))
                        act.copy(xT_hi[:, kc, :], xT_ps[kc % 2][:]).then_inc(xT_hi_s, 1)

                if is_int(g) and g < 0:
                    rows_hi()
                    return
                for m in range(MC):
                    act.wait_ge(gu_done, 2 * MC * g + (2 * m + 1))
                    need(act, hid_s, MC * g + (m - 1))
                    act.activation(gate_act[:, m % 2, :], g_ps[m % 2][:], ACT.Silu).then_inc(act_s, 1)
                    act.wait_ge(hid_s, MC * g + (m + 1))
                    if m == 0:
                        need(act, dn_done, GT * g)
                    act.copy(h_hi[:, m, :], hid[:, m % 2, :]).then_inc(h_hi_s, 1)
                if not (is_int(g) and g == GROUPS - 1):
                    rows_hi()

            pipeline(act, body)

        @block.vector
        def _(v):
            for n, (w, size) in enumerate(((sg, KC * MS), (su, KC * MS), (sd, MC * D))):
                v.wait_ge(w_hi_s, n + 1)
                v.tensor_tensor(w[1][:].rearrange("p c m -> p (c m)"), raw[n % 2][:, 0:size],
                                w[0][:].rearrange("p c m -> p (c m)").bitcast(F32), ALU.subtract).then_inc(w_lo_s, 1)

            def body(g):
                def rows_lo():
                    for kc in range(KC):
                        v.wait_ge(xT_hi_s, KC * (g + 1) + (kc + 1))
                        v.tensor_tensor(xT_lo[:, kc, :], xT_ps[kc % 2][:], xT_hi[:, kc, :].bitcast(F32),
                                        ALU.subtract).then_inc(xT_lo_s, 1)

                def routed(q):
                    v.wait_ge(gathered[q % 2], 16 * TOP_K * (2 * g + (q // 2 + 1)))
                    if q == 0:
                        v.wait_ge(acc_in, 16 * (g + 1))
                        v.wait_ge(staged, g + 1)
                    for k in range(TOP_K):
                        last = v.scalar_tensor_tensor(acc[:, q, :], rows[:, q % 2, k, :],
                                                      w_now[:, q * TOP_K + k:q * TOP_K + k + 1], acc[:, q, :],
                                                      ALU.mult, ALU.add)
                        if k < TOP_K - 1:
                            last.then_inc(step_s, 1)
                            v.wait_ge(step_s, (TOP_K - 1) * GT * g + ((TOP_K - 1) * q + k + 1))
                    last.then_inc(routed_s, 1)

                def stage(group):
                    at = bass.ds(group * (GT * TOP_K), GT * TOP_K)
                    v.tensor_scalar(w_now[:], keep["weight"][:, at], 1.0, None, ALU.mult)
                    v.tensor_copy(idx_now[:], keep["slot"][:, at]).then_inc(staged, 1)

                if is_int(g) and g < 0:
                    stage(0)
                    rows_lo()
                    return
                for m in range(MC):
                    v.wait_ge(act_s, MC * g + (m + 1))
                    v.wait_ge(gu_done, 2 * MC * g + (2 * m + 2))
                    if m < POOL_LO:
                        need(v, h_lo_p, POOL_LO * g + (m - 1 if m >= 2 else 0))
                    elif m - 2 < POOL_LO:
                        v.wait_ge(h_lo_p, POOL_LO * g + (m - 1))
                    v.tensor_tensor(hid[:, m % 2, :], gate_act[:, m % 2, :], u_ps[m % 2][:],
                                    ALU.mult).then_inc(hid_s, 1)
                    if m >= POOL_LO:
                        v.wait_ge(h_hi_s, MC * g + (m + 1))
                        v.tensor_tensor(h_lo[:, m, :], hid[:, m % 2, :], h_hi[:, m, :].bitcast(F32),
                                        ALU.subtract).then_inc(h_lo_v, 1)
                    if 1 <= m <= 3:
                        routed(m - 1)
                if not (is_int(g) and g == GROUPS - 1):
                    rows_lo()
                routed(GT - 1)
                if not (is_int(g) and g == GROUPS - 1):
                    v.wait_ge(routed_s, GT * (g + 1))
                    stage(g + 1)
                for q in range(GT):
                    v.wait_ge(dn_done, GT * g + (q + 1))
                    need(v, stored[q % 2], 16 * 2 * g + 16 * (q // 2))
                    if q == 0:
                        v.wait_ge(routed_s, GT * (g + 1))
                    v.tensor_tensor(out_rows[:, q % 2, :], dn_ps[q % 2][:], acc[:, q, :], ALU.add).then_inc(out_s, 1)

            pipeline(v, body)

        @block.gpsimd
        def _(p):
            def body(g):
                if is_int(g) and g < 0:
                    return
                for q in range(GT):
                    p.wait_ge(h_hi_s, MC * g + (q + 1))
                    if q == 0:
                        p.wait_ge(staged, g + 1)
                    need(p, routed_s, GT * g + (q - 1))
                    p.tensor_tensor(h_lo[:, q, :], hid[:, q % 2, :], h_hi[:, q, :].bitcast(F32),
                                    ALU.subtract).then_inc(h_lo_p, 1)
                    for k in range(TOP_K):
                        p.indirect_dma_start(
                            out=rows[:, q % 2, k, :], out_offset=None, in_=d["eo"],
                            in_offset=bass.IndirectOffsetOnAxis(ap=idx_now[:, q * TOP_K + k:q * TOP_K + k + 1], axis=0),
                        ).then_inc(gathered[q % 2], 16)

            pipeline(p, body)


def cross_attention_moe(nc, d):
    T = d["x"].shape[0] * d["x"].shape[1]
    D = d["x"].shape[2]
    E = d["experts"].shape[0]
    d["x2"] = nc.dram_tensor("x2_scratch", d["x"].shape, F32, kind="Internal").ap()
    d["xn2"] = nc.dram_tensor("xn2_scratch", d["x"].shape, F32, kind="Internal").ap()
    d["table"] = nc.dram_tensor("slot_token_scratch", [E * CAPACITY, 1], I32, kind="Internal").ap()
    d["eo"] = nc.dram_tensor("expert_out_scratch", [E * CAPACITY, D], F32, kind="Internal").ap()
    d["x2_rows"], d["xn2_rows"] = (d[n].rearrange("b s n -> (b s) n") for n in ("x2", "xn2"))
    with ExitStack() as ctx:
        keep = {"slot": ctx.enter_context(nc.sbuf_tensor("keep_slot", [P, T // P * TOP_K], U32)),
                "weight": ctx.enter_context(nc.sbuf_tensor("keep_weight", [P, T // P * TOP_K], F32))}
        phase_a(nc, d, keep)
        phase_b(nc, d)
        phase_c(nc, d, keep)


def kernel(**inputs):
    import numpy as np
    import concourse.bacc as bacc
    from concourse.bass_utils import run_bass_kernel_spmd

    attn = lambda n: np.asarray(inputs["L0_xattn_" + n])
    ffn = lambda n: np.asarray(inputs["L0_ffn_" + n])
    x, ctx = np.asarray(inputs["x"]), np.asarray(inputs["ctx_2048"])
    D = x.shape[2]
    E, M, _ = ffn("Wg").shape
    MS = ffn("Sg").shape[0]

    def by_input(w):
        w = np.swapaxes(w, -1, -2)
        w = w.reshape(*w.shape[:-2], w.shape[-2] // P, P, w.shape[-1])
        return np.swapaxes(w, -3, -2)

    def by_hidden(w):
        w = np.swapaxes(w, -1, -2)
        hidden = w.shape[-2]
        chunks = -(-hidden // P)
        full = (chunks - 1) * P
        out = np.zeros((*w.shape[:-2], chunks * P, w.shape[-1]), w.dtype)
        out[..., 0:full, :] = w[..., 0:full, :]
        out[..., full + chunks * P - hidden:, :] = w[..., full:, :]
        return np.swapaxes(out.reshape(*w.shape[:-2], chunks, P, w.shape[-1]), -3, -2)

    flat = lambda w: w.reshape(E, P, -1)
    p = np.arange(P)
    consts = np.concatenate([
        np.eye(P), p[:, None] < p[None, :], np.ones((P, P)), np.broadcast_to(np.arange(E), (P, E)),
        np.broadcast_to(np.arange(E) * CAPACITY, (P, E)), p[:, None] + 1 + P * np.arange(x.shape[1] // P)[None, :]],
        1).astype(np.float32)
    arrays = {
        "x": x,
        "ctxT": np.swapaxes(ctx, 1, 2),
        "wk": attn("Wk_img"), "wq": attn("Wq"), "wv": attn("Wv_img"), "wo": attn("Wo"), "bo": attn("bo"),
        "bq": attn("bq"), "gq": attn("gq"), "bk": attn("bk_img"), "gk": attn("gk_img"),
        "bv": attn("bv_img").reshape(D // P, P).T,
        "gateT": ffn("gate_weight").T,
        "consts": consts,
        "experts": np.concatenate([flat(by_input(ffn("Wg"))), flat(by_input(ffn("Wu"))), flat(by_hidden(ffn("Wd")))], 2),
        "sg": by_input(ffn("Sg")), "su": by_input(ffn("Su")), "sd": by_hidden(ffn("Sd")),
    }
    arrays = {f"in_{n}_dram": np.ascontiguousarray(a) for n, a in arrays.items()}

    nc = bacc.Bacc("TRN2", target_bir_lowering=False, num_devices=1)
    d = {n[3:-5]: nc.dram_tensor(n, a.shape, mybir.dt.from_np(a.dtype), kind="ExternalInput").ap()
         for n, a in arrays.items()}
    d["out"] = nc.dram_tensor("out_0_dram", (x.shape[0] * x.shape[1], D), F32, kind="ExternalOutput").ap()
    d["m"] = M
    cross_attention_moe(nc, d)
    r = run_bass_kernel_spmd(nc, [arrays], core_ids=[0])
    return r.results[0]["out_0_dram"].reshape(x.shape)
```

```python
from contextlib import ExitStack

import concourse.bass as bass
from concourse import mybir

F32 = mybir.dt.float32
F32R = mybir.dt.float32r
BF16 = mybir.dt.bfloat16
I32 = mybir.dt.int32
U32 = mybir.dt.uint32
ALU = mybir.AluOpType
ACT = mybir.ActivationFunctionType
X = mybir.AxisListType.X

P = 128
HEAD_DIM = 32
TOP_K = 6
N_GROUP = 8
TOPK_GROUP = 3
CAPACITY = 192
RMS_EPS = 1e-6
LN_EPS = 1e-5
SCALE = float(HEAD_DIM) ** -0.5
OVER = 65536.0



def need(eng, sem, value):
    if isinstance(value, int) and value <= 0:
        return
    eng.wait_ge(sem, value)


class Kind:
    def __init__(self, prep, attend, post, scatter):
        self.prep, self.attend, self.post, self.scatter = prep, attend, post, scatter


SHARED_USES = [
    ("v0", "attend"), ("pv3", "post"), ("o0", "post"), ("v1", "attend"), ("o1", "post"), ("k0", "prep"),
    ("pv0", "attend"), ("nT0", "post"), ("nT1", "post"), ("k1", "prep"), ("logits", "post"), ("xT0", "prep"),
    ("xT1", "prep"), ("pv1", "attend"), ("q0", "prep"), ("kT0", "prep"), ("q1", "prep"), ("pv2", "attend"),
    ("pos", "post"), ("qT0", "prep"), ("qT1", "prep"), ("kT1", "prep"),
]


def shared_plan(kinds):
    before = [None, None]
    n = 0
    plans = []
    for at, kind in enumerate(kinds):
        plan = {}
        for name, stage in SHARED_USES:
            if {"attend": kind.attend, "post": kind.post, "prep": kind.prep}[stage]:
                last = before[n % 2]
                plan[name] = (n % 2, last and last[0], last and at - last[1])
                before[n % 2] = (name, at)
                n += 1
        plans.append(plan)
    return plans


def phase_a(nc, d, keep):
    B, S, D = d["x"].shape
    KC = D // P
    QT = S // P
    H = D // HEAD_DIM
    HC = P // HEAD_DIM
    CK = d["ctxT"].shape[2]
    KT = CK // P
    UNITS = KC * QT
    E = d["gateT"].shape[1]
    GE = E // N_GROUP
    assert (KC, QT, HC, KT, UNITS) == (4, 2, 4, 2, 8)

    prologue = [Kind(True, False, False, False), Kind(True, True, False, False), Kind(True, True, True, False)]
    steady = Kind(True, True, True, True)
    epilogue = [Kind(False, True, True, True), Kind(False, False, True, True), Kind(False, False, False, True)]
    LOOP = B - 3
    plans = shared_plan([*prologue, steady, steady, *epilogue])
    assert plans[len(prologue)] == plans[len(prologue) + 1]

    def pipeline(eng, body):
        for at, kind in enumerate(prologue):
            body(at - 1, kind, plans[at])
        with eng.Fori(2, 2 + LOOP) as i:
            body(i, steady, plans[len(prologue)])
        for at, kind in enumerate(epilogue):
            body(2 + LOOP + at, kind, plans[len(prologue) + 2 + at])

    with ExitStack() as ctx:
        def sb(name, shape, dt=F32):
            return ctx.enter_context(nc.sbuf_tensor(name, shape, dt))

        def ps(name, shape, dt=F32):
            return ctx.enter_context(nc.psum_tensor(name, shape, dt))

        def sem(name):
            return ctx.enter_context(nc.semaphore(name))

        w_hi = {n: sb(f"w{n}_hi", [P, KC, D], F32R) for n in "kqvo"}
        w_lo = {n: sb(f"w{n}_lo", [P, KC, D], F32R) for n in "kqvo"}
        gate = sb("gate_parts", [P, KC, 2, E], F32R)
        bv_col = sb("bv_col", [P, KC])
        bo_row, bias_row = sb("bo_row", [P, D]), {n: sb(f"b{n}_row", [P, D]) for n in "kq"}
        gain_row = sb("gain_row", [P, D])
        consts = sb("const_cols", [P, d["consts"].shape[1]])
        ident, ones = consts[:, 0:P], consts[:, 2 * P:3 * P]
        iota_e, iota_g = consts[:, 3 * P:3 * P + E], consts[:, 3 * P:3 * P + N_GROUP]
        slot_base = consts[:, 3 * P + E:3 * P + 2 * E]
        tok_col = consts[:, 3 * P + 2 * E:3 * P + 2 * E + QT]
        tri_b, ones_b = sb("tri_b", [P, P], BF16), sb("ones_b", [P, P], BF16)
        minus_half = sb("minus_half", [P, QT])
        x_raw = sb("x_raw", [P, QT, D])
        ctx_raw = sb("ctx_raw", [P, KC, CK])
        ctx_hi, ctx_lo = sb("ctx_hi", [P, KC, CK], F32R), sb("ctx_lo", [P, KC, CK], F32R)
        tT_hi, tT_lo = sb("tT_hi", [P, KC, S], F32R), sb("tT_lo", [P, KC, S], F32R)
        rows = {n: sb(f"{n}_rows", [P, QT, D]) for n in "kq"}
        squares = sb("squares", [P, 2, QT, D], BF16)
        sq_sum = {n: sb(f"{n}_sq_sum", [P, QT]) for n in "kq"}
        mean_sq = {n: sb(f"{n}_mean_sq", [P, QT]) for n in "kq"}
        rms_inv = {n: sb(f"{n}_rms_inv", [P, QT]) for n in "kq"}
        hT = {n: (sb(f"{n}T_hi", [P, KC, S], F32R), sb(f"{n}T_lo", [P, KC, S], F32R)) for n in "kq"}
        ln_stats, ln_mv = sb("ln_stats", [P, QT, 6]), sb("ln_mv", [P, QT, 2])
        ln_var, ln_rstd = sb("ln_var", [P, QT]), sb("ln_rstd", [P, QT])
        V_AT = (0, P + 2 * HEAD_DIM, 2 * P + HEAD_DIM, P)
        VC = 2 * P + 3 * HEAD_DIM
        v_hi, v_lo = sb("v_hi", [P, KT, KC, VC], F32R), sb("v_lo", [P, KT, KC, VC], F32R)
        probs = sb("probs", [P, 2, HC, CK])
        neg_max, row_sum, row_inv = sb("neg_max", [P, 2, HC]), sb("row_sum", [P, 2, HC]), sb("row_inv", [P, 2, HC])
        row_max = sb("row_max", [P, 2, HC])
        pT_hi, pT_lo = sb("pT_hi", [P, HC * KT, S], F32R), sb("pT_lo", [P, HC * KT, S], F32R)
        aT_hi, aT_lo = sb("aT_hi", [P, KC, S], F32R), sb("aT_lo", [P, KC, S], F32R)
        x2 = sb("x2_rows", [P, QT, D])
        xn2 = sb("xn2_rows", [P, QT, D])
        n2_stats, n2_mv = sb("n2_stats", [P, QT, 6]), sb("n2_mv", [P, QT, 2])
        n2_var, n2_rstd = sb("n2_var", [P, QT]), sb("n2_rstd", [P, QT])
        lg_max, lg_sum = sb("lg_max", [P, QT]), sb("lg_sum", [P, QT])
        score = sb("score", [P, QT, E])
        g_score, g_top, g_idx, g_idxf = (sb("g_score", [P, QT, N_GROUP]), sb("g_top", [P, QT, 8]),
                                         sb("g_idx", [P, QT, 8], U32), sb("g_idxf", [P, QT, 8]))
        g_hot, g_mask = sb("g_hot", [P, QT, TOPK_GROUP, N_GROUP]), sb("g_mask", [P, QT, N_GROUP])
        e_top, e_idx, e_idxf = sb("e_top", [P, QT, 8]), sb("e_idx", [P, QT, 8], U32), sb("e_idxf", [P, QT, 8])
        e_hot = sb("e_hot", [P, QT, TOP_K, E], BF16)
        e_slot = sb("e_slot", [P, QT, TOP_K, E])
        mask_f, mask_b = sb("mask_f", [P, QT, E]), sb("mask_b", [P, QT, E], BF16)
        seen, seen_b = sb("seen", [P, E]), sb("seen_b", [P, E], BF16)
        slot_val = sb("slot_val", [P, QT, E])
        last_tok = sb("last_tok", [P, E])
        slot_f, last_slot, is_last, scat_f = (sb("slot_f", [P, QT, TOP_K]), sb("last_slot", [P, QT, TOP_K]),
                                              sb("is_last", [P, QT, TOP_K]), sb("scat_f", [P, QT, TOP_K]))
        scat_idx = sb("scat_idx", [P, QT * TOP_K], U32)
        scat_tok = sb("scat_tok", [P, QT], I32)
        zero_i = sb("zero_i", [P, E * CAPACITY // P], I32)
        lastT, lastT_i = sb("lastT", [E, 1]), sb("lastT_i", [E, 1], I32)

        settled = sb("settled", [P, 8])

        scores_ps = [ps(f"scores_ps{n}", [P, HC, CK]) for n in range(2)]
        pT_ps = ps("pT_ps", [P, HC * KT, P])
        shared_ps = [ps(f"shared_ps{n}", [P, 512]) for n in range(2)]

        in_sem = sem("a_params_loaded")
        vec_sem = sem("a_vectors_loaded")
        stage_in = [sem(f"a_weight_half_loaded{n}") for n in range(3)]
        w_hi_done, w_lo_done = sem("a_weight_hi_done"), sem("a_weight_lo_done")
        gate_split, gain_s, bo_in = sem("a_gate_split"), sem("a_gain_product_done"), sem("a_bo_loaded")
        chain = {n: sem(f"a_vector_{n}_chain") for n in ("setup", "prep", "attend", "post")}
        setup_p = sem("a_setup_by_pool")
        table_zeroed = sem("a_table_zeroed")
        x_in, ctx_in, res_in = sem("a_x_loaded"), sem("a_ctx_loaded"), sem("a_residual_loaded")
        ctx_hi_s, ctx_lo_s = sem("a_ctx_hi_done"), sem("a_ctx_lo_done")
        stats1, rstd1, xn_s = sem("a_ln1_var_done"), sem("a_ln1_rstd_done"), sem("a_ln1_done")
        x_turned, x_hi_s, x_lo_s = sem("a_x_turned"), sem("a_xT_hi_done"), sem("a_xT_lo_done")
        proj = {n: sem(f"a_{n}_product_done") for n in "kq"}
        biased_s = {n: sem(f"a_{n}_biased") for n in "kq"}
        sq_s = {n: sem(f"a_{n}_squared") for n in "kq"}
        ms_s = {n: sem(f"a_{n}_mean_square_done") for n in "kq"}
        inv_s = {n: sem(f"a_{n}_rms_inverse_done") for n in "kq"}
        k_normed, turned_s = sem("a_k_normed"), {n: sem(f"a_{n}_turned") for n in "kq"}
        hi_s = {n: sem(f"a_{n}_hi_done") for n in "kq"}
        lo_s = {n: sem(f"a_{n}_lo_done") for n in "kq"}
        v_done, v_hi_s, v_lo_s = sem("a_v_product_done"), sem("a_v_hi_done"), sem("a_v_lo_done")
        head_done = sem("a_head_scores_done")
        scores_done, max_done, exp_done = sem("a_scores_done"), sem("a_max_done"), sem("a_exp_done")
        inv_done, probs_done = sem("a_row_inv_done"), sem("a_probs_normed")
        p_turned, p_hi_s, p_lo_s = sem("a_probs_turned"), sem("a_pT_hi_done"), sem("a_pT_lo_done")
        pv_done, a_hi_s, a_lo_s = sem("a_pv_done"), sem("a_aT_hi_done"), sem("a_aT_lo_done")
        bo_added, o_done, x2_s = sem("a_residual_plus_bo"), sem("a_o_product_done"), sem("a_x2_done")
        stats2, rstd2, xn2_s = sem("a_ln2_var_done"), sem("a_ln2_rstd_done"), sem("a_ln2_done")
        x2_out, xn2_out = sem("a_x2_stored"), sem("a_xn2_stored")
        n_turned, n_hi_s, n_lo_s = sem("a_xn2_turned"), sem("a_xn2T_hi_done"), sem("a_xn2T_lo_done")
        logits_done, lgmax_s, lgexp_s = sem("a_logits_done"), sem("a_logit_max_done"), sem("a_logit_exp_done")
        mask_s, pos_done, scat_rdy = sem("a_mask_done"), sem("a_positions_done"), sem("a_scatter_index_done")
        scattered = sem("a_tokens_scattered")
        lastT_s, last_i_s, last_out = (sem("a_last_turned"), sem("a_last_index_done"),
                                               sem("a_last_stored"))
        pos_read = sem("a_positions_read")

        def read_of(name):
            kind, n = name.rstrip("0123456789"), name.lstrip("abcdefghijklmnopqrstuvwxyzT")
            n = int(n) if n else 0
            return {
                "v": (v_lo_s, KT, n + 1),
                "pv": (a_lo_s, KC, n + 1 - (KC if n == KC - 1 else 0)),
                "o": (x2_s, QT, n + 1 - QT),
                "k": (biased_s["k"], QT, QT + n + 1), "q": (biased_s["q"], QT, QT + n + 1),
                "kT": (lo_s["k"], QT, QT + n + 1), "qT": (lo_s["q"], QT, QT + n + 1),
                "nT": (n_lo_s, QT, n + 1 - QT), "xT": (x_lo_s, QT, QT + n + 1),
                "logits": (lgmax_s, 1, 0), "pos": (pos_read, 1, 0),
            }[kind]

        def heads_of(bank):
            b = bank.rearrange("p (c g n) -> p c g n", g=HC, n=HEAD_DIM)
            return b[:, :, 0:HC:HC - 1, :], b[:, :, 1:3, :]

        def heads_in(v, t):
            near = v[:, t, :, 0:2 * P].rearrange("p c (g n) -> p c g n", g=2)[:, :, :, 0:HEAD_DIM]
            step = V_AT[2] - V_AT[1]
            far = v[:, t, :, V_AT[1]:VC].rearrange("p c (a n) -> p c a n", n=HEAD_DIM)[:, :, 0:step // HEAD_DIM + 1:step // HEAD_DIM, :]
            return near, far

        block = ctx.enter_context(nc.Block())
        halves = [(n, h) for n in "kqvo" for h in range(2)]
        stage = [probs[:, n, :, :].rearrange("p h t -> p (h t)") for n in range(2)]
        stage.append(xn2[:].rearrange("p q n -> p (q n)"))
        STAGES = len(stage)

        @block.sync
        def _(sp):
            sp.dma_start(ctx_raw[:], d["ctxT"][0].rearrange("(c p) t -> p c t", p=P)).then_inc(ctx_in, 16)
            for n, (w, h) in enumerate(halves[:STAGES]):
                sp.dma_start(stage[n % STAGES],
                             d["w" + w].rearrange("(c p) n -> p c n", p=P)[:, 2 * h:2 * h + 2, :]
                             ).then_inc(stage_in[n % STAGES], 16)
            sp.dma_start(x_raw[:], d["x"][0].rearrange("(q p) n -> p q n", p=P)).then_inc(x_in, 16)
            sp.dma_start(consts[:], d["consts"]).then_inc(in_sem, 16)
            sp.dma_start(bv_col[:], d["bv"]).then_inc(vec_sem, 16)
            for row, n in ((bias_row["k"], "bk"), (bias_row["q"], "bq"), (gain_row, "gk"), (bo_row, "gq")):
                sp.dma_start(row[:], d[n].rearrange("(a n) -> a n", a=1).to_broadcast([P, D])).then_inc(vec_sem, 16)
            sp.dma_start(x2[:, 0, 0:KC * E].rearrange("p (c e) -> p c e", c=KC),
                         d["gateT"].rearrange("(c p) e -> p c e", p=P)).then_inc(vec_sem, 16)
            for n, (w, h) in enumerate(halves):
                if n < STAGES:
                    continue
                sp.wait_ge(w_lo_done, n - STAGES + 1)
                sp.dma_start(stage[n % STAGES],
                             d["w" + w].rearrange("(c p) n -> p c n", p=P)[:, 2 * h:2 * h + 2, :]
                             ).then_inc(stage_in[n % STAGES], 16)
            sp.wait_ge(gain_s, 1)
            sp.dma_start(bo_row[:], d["bo"].rearrange("(a n) -> a n", a=1).to_broadcast([P, D])).then_inc(bo_in, 16)
            sp.wait_ge(setup_p, 1)
            sp.dma_start(d["table"].rearrange("(p j) o -> p (j o)", p=P), zero_i[:]).then_inc(table_zeroed, 16)

            def body(i, kind, use):
                if kind.prep and not (isinstance(i, int) and i < 0):
                    b = i + 1
                    need(sp, ctx_lo_s, b)
                    need(sp, ctx_hi_s, b)
                    sp.dma_start(ctx_raw[:], d["ctxT"][b].rearrange("(c p) t -> p c t", p=P)).then_inc(ctx_in, 16)
                    sp.wait_ge(x_turned, QT * b)
                    sp.dma_start(x_raw[:], d["x"][b].rearrange("(q p) n -> p q n", p=P)).then_inc(x_in, 16)
                if kind.post:
                    b = i - 1
                    if isinstance(b, int) and b == 0:
                        sp.wait_ge(gate_split, 1)
                    else:
                        need(sp, x2_out, 16 * b)
                        need(sp, xn2_s, QT * i - QT)
                    sp.dma_start(x2[:], d["x"][b].rearrange("(q p) n -> p q n", p=P)).then_inc(res_in, 16)
                if kind.post:
                    b = i - 1
                    sp.wait_ge(x2_s, QT * b + QT)
                    sp.dma_start(d["x2"][b].rearrange("(q p) n -> p q n", p=P), x2[:]).then_inc(x2_out, 16)
                    sp.wait_ge(xn2_s, QT * b + QT)
                    sp.dma_start(d["xn2"][b].rearrange("(q p) n -> p q n", p=P), xn2[:]).then_inc(xn2_out, 16)

            pipeline(sp, body)
            sp.wait_ge(x2_out, 16 * B)
            sp.wait_ge(xn2_out, 16 * B)
            sp.wait_ge(table_zeroed, 16)
            sp.wait_ge(last_i_s, 1)
            sp.dma_start(d["table"].rearrange("(e s) o -> e (s o)", s=CAPACITY)[:, CAPACITY - 1:CAPACITY],
                         lastT_i[:], allow_slow_non_contiguous=True).then_inc(last_out, 16)
            sp.wait_ge(last_out, 16)

        @block.tensor
        def _(pe):
            def mm3(out, a_hi, a_lo, b_hi, b_lo, first, last):
                pe.matmul(out, a_hi, b_hi, start=first, stop=False)
                pe.matmul(out, a_hi, b_lo, start=False, stop=False)
                return pe.matmul(out, a_lo, b_hi, start=False, stop=last)

            def shared(use, name, i, own=None):
                bank, before, ago = use[name]
                waits = [own] if own else []
                if before:
                    signal, a, b = read_of(before)
                    b -= a * ago
                    if own and own[0] is signal:
                        assert own[1] == a
                        waits = [(signal, a, max(b, own[2]))]
                    else:
                        waits.append((signal, a, b))
                for signal, a, b in waits:
                    need(pe, signal, a * i + b)
                return shared_ps[bank]

            def turn(use, name, src, q, i, own):
                bank = shared(use, name, i, own)
                for c in range(KC):
                    last = pe.transpose(bank[:, c * P:(c + 1) * P], src[:, q, c * P:(c + 1) * P], ident)
                return last

            def body(i, kind, use):
                def project(n, t):
                    src_hi, src_lo = (ctx_hi, ctx_lo) if n == "k" else (tT_hi, tT_lo)
                    own = None
                    if t == 0:
                        own = (ctx_lo_s, 1, 2) if n == "k" else (x_lo_s, QT, 2 * QT)
                        if isinstance(i, int) and i < 0:
                            pe.wait_ge(w_lo_done, 2 if n == "k" else 4)
                    bank = shared(use, f"{n}{t}", i, own)
                    c = slice(t * P, (t + 1) * P)
                    for kc in range(KC):
                        last = mm3(bank[:], src_hi[:, kc, c], src_lo[:, kc, c], w_hi[n][:, kc, :], w_lo[n][:, kc, :],
                                   kc == 0, kc == KC - 1)
                    last.then_inc(proj[n], 1)

                def turn_rows(n, t):
                    own = (k_normed if n == "k" else biased_s["q"], QT, QT + t + 1)
                    turn(use, f"{n}T{t}", rows[n], t, i, own).then_inc(turned_s[n], 1)

                def v_tile(t):
                    bank = shared(use, f"v{t}", i)
                    if isinstance(i, int) and i == 0 and t == 0:
                        pe.wait_ge(w_lo_done, 6)
                    for kc in range(KC):
                        last = mm3(bank[:], ctx_hi[:, kc, t * P:(t + 1) * P], ctx_lo[:, kc, t * P:(t + 1) * P],
                                   w_hi["v"][:, kc, :], w_lo["v"][:, kc, :], kc == 0, kc == KC - 1)
                    last.then_inc(v_done, 1)

                def scores(u):
                    c, q = divmod(u, QT)
                    if u == 0:
                        for n in "kq":
                            pe.wait_ge(lo_s[n], QT * (i + 1))
                    need(pe, exp_done, UNITS * i + u - 1)
                    for n, g in enumerate((0, 2, 1, 3)):
                        if n >= 2:
                            pe.wait_ge(head_done, (HC - 1) * (UNITS * i + u) + n - 1)
                        r = slice(g * HEAD_DIM, (g + 1) * HEAD_DIM)
                        last = mm3(scores_ps[u % 2][:, g, :], hT["q"][0][r, c, q * P:(q + 1) * P],
                                   hT["q"][1][r, c, q * P:(q + 1) * P], hT["k"][0][r, c, :], hT["k"][1][r, c, :],
                                   True, True)
                        last.then_inc(scores_done if n == HC - 1 else head_done, 1)

                def turn_probs(u):
                    pe.wait_ge(probs_done, UNITS * i + u + 1)
                    need(pe, p_lo_s, UNITS * i + u)
                    for g in range(HC):
                        for t in range(KT):
                            last = pe.transpose(pT_ps[:, g * KT + t, :], probs[:, u % 2, g, t * P:(t + 1) * P], ident)
                    last.then_inc(p_turned, 1)

                def pv(b, c):
                    pe.wait_ge(p_lo_s, UNITS * b + 2 * c + 2)
                    own = (v_lo_s, KT, KT) if c == 0 else None
                    bank = shared(use, f"pv{c}", i, own)
                    for g in range(HC):
                        w = slice(V_AT[g] - g * HEAD_DIM, V_AT[g] - g * HEAD_DIM + P)
                        for t in range(KT):
                            last = mm3(bank[:, 0:S], v_hi[:, t, c, w], v_lo[:, t, c, w], pT_hi[:, g * KT + t, :],
                                       pT_lo[:, g * KT + t, :], g == 0 and t == 0, g == HC - 1 and t == KT - 1)
                    last.then_inc(pv_done, 1)

                def o_tile(q):
                    if isinstance(i, int) and i == 1 and q == 0:
                        pe.wait_ge(w_lo_done, 8)
                    bank = shared(use, f"o{q}", i, (a_lo_s, KC, 0))
                    for c in range(KC):
                        last = mm3(bank[:], aT_hi[:, c, q * P:(q + 1) * P], aT_lo[:, c, q * P:(q + 1) * P],
                                   w_hi["o"][:, c, :], w_lo["o"][:, c, :], c == 0, c == KC - 1)
                    last.then_inc(o_done, 1)

                def logits():
                    bank = shared(use, "logits", i, (n_lo_s, QT, 0))
                    for q in range(QT):
                        t = slice(q * P, (q + 1) * P)
                        for c in range(KC):
                            pe.matmul(bank[:, 2 * q * E:2 * (q + 1) * E], tT_hi[:, c, t],
                                      gate[:, c, :, :].rearrange("p a e -> p (a e)"), start=c == 0, stop=False)
                            last = pe.matmul(bank[:, 2 * q * E:(2 * q + 1) * E], tT_lo[:, c, t], gate[:, c, 0, :],
                                             start=False, stop=c == KC - 1)
                    last.then_inc(logits_done, 1)

                def turn_x(q):
                    turn(use, f"xT{q}", x_raw, q, i, (xn_s, QT, QT + q + 1)).then_inc(x_turned, 1)

                def turn_xn2(q):
                    turn(use, f"nT{q}", xn2, q, i, (xn2_s, QT, q + 1 - QT)).then_inc(n_turned, 1)

                def positions():
                    bank = shared(use, "pos", i, (mask_s, 1, 0))
                    for q in range(QT):
                        o = bank[:, q * E:(q + 1) * E]
                        pe.matmul(o, tri_b[:], mask_b[:, q, :], start=True, stop=False)
                        for r in range(q):
                            pe.matmul(o, ones_b[:], mask_b[:, r, :], start=False, stop=False)
                        last = pe.matmul(o, ones_b[:], seen_b[:], start=False, stop=True)
                    last.then_inc(pos_done, 1)

                if kind.attend:
                    v_tile(0)
                if kind.post:
                    pv(i - 1, 3)
                if kind.attend:
                    scores(0)
                    scores(1)
                if kind.post:
                    o_tile(0)
                if kind.attend:
                    v_tile(1)
                    scores(2)
                    turn_probs(0)
                if kind.post:
                    o_tile(1)
                if kind.attend:
                    scores(3)
                    turn_probs(1)
                    scores(4)
                if kind.prep:
                    project("k", 0)
                if kind.attend:
                    pv(i, 0)
                if kind.post:
                    turn_xn2(0)
                if kind.attend:
                    turn_probs(2)
                    scores(5)
                if kind.post:
                    turn_xn2(1)
                if kind.prep:
                    project("k", 1)
                if kind.attend:
                    turn_probs(3)
                if kind.post:
                    logits()
                if kind.prep:
                    turn_x(0)
                if kind.attend:
                    scores(6)
                if kind.prep:
                    turn_x(1)
                if kind.attend:
                    turn_probs(4)
                    pv(i, 1)
                if kind.prep:
                    project("q", 0)
                if kind.attend:
                    scores(7)
                if kind.prep:
                    turn_rows("k", 0)
                if kind.attend:
                    turn_probs(5)
                if kind.prep:
                    project("q", 1)
                if kind.attend:
                    pv(i, 2)
                    turn_probs(6)
                if kind.post:
                    positions()
                if kind.prep:
                    turn_rows("q", 0)
                    turn_rows("q", 1)
                if kind.attend:
                    turn_probs(7)
                if kind.prep:
                    turn_rows("k", 1)

            pe.wait_ge(in_sem, 16)
            pipeline(pe, body)
            pe.wait_ge(scat_rdy, B)
            pe.wait_ge(pos_read, B)
            bank = plans[-2]["pos"][0]
            pe.transpose(shared_ps[bank][0:E, 0:P], last_tok[:], ident).then_inc(lastT_s, 1)

        @block.scalar
        def _(act):
            act.preload_act_table_set("natural_log_exp_and_others")
            pairs = iter(range(0, len(halves), 2))

            def split_weight():
                first = next(pairs)
                for n in (first, first + 1):
                    w, h = halves[n]
                    act.wait_ge(stage_in[n % STAGES], 16 * (n // STAGES + 1))
                    act.copy(w_hi[w][:, 2 * h:2 * h + 2, :].rearrange("p c n -> p (c n)"),
                             stage[n % STAGES]).then_inc(w_hi_done, 1)

            split_weight()

            def body(i, kind, use):
                def exp_unit(u):
                    q = u % QT
                    act.wait_ge(max_done, UNITS * i + u + 1)
                    need(act, p_turned, UNITS * i + u - 1)
                    need(act, inv_done, UNITS * i + u - 1)
                    if isinstance(i, int) and i == 0 and u == 0:
                        act.wait_ge(w_lo_done, len(halves))
                    for g in range(HC):
                        last = act.activation(probs[:, u % 2, g, :], scores_ps[u % 2][:, g, :], ACT.Exp,
                                              bias=neg_max[:, u % 2, g:g + 1], scale=rms_inv["q"][:, q:q + 1],
                                              accum_out=row_sum[:, u % 2, g:g + 1])
                    last.then_inc(exp_done, 1)

                def turned_hi(u):
                    q = u % QT
                    if q == 0:
                        need(act, pv_done, KC * i + u // QT)
                    act.wait_ge(p_turned, UNITS * i + u + 1)
                    act.copy(pT_hi[:, :, q * P:(q + 1) * P], pT_ps[:]).then_inc(p_hi_s, 1)

                def attended_hi(b, c):
                    bank = use[f"pv{c}"][0]
                    act.wait_ge(pv_done, KC * b + c + 1)
                    act.activation(aT_hi[:, c, :], shared_ps[bank][:, 0:S], ACT.Identity,
                                   bias=bv_col[:, c:c + 1]).then_inc(a_hi_s, 1)

                def v_part(t):
                    bank = use[f"v{t}"][0]
                    act.wait_ge(v_done, KT * i + t + 1)
                    if isinstance(i, int) and i == 0 and t == 0:
                        act.wait_ge(vec_sem, 16 * 6)
                        act.wait_ge(setup_p, 4)
                    need(act, pv_done, KC * i)
                    for src, dst in zip(heads_of(shared_ps[bank][:]), heads_in(v_hi, t)):
                        last = act.copy(dst, src)
                    last.then_inc(v_hi_s, 1)

                def context_hi():
                    act.wait_ge(ctx_in, 16 * (i + 2))
                    need(act, v_done, KT * (i + 1))
                    act.copy(ctx_hi[:], ctx_raw[:]).then_inc(ctx_hi_s, 1)
                    if isinstance(i, int) and i < 0:
                        split_weight()

                def row_squares(n, t):
                    act.wait_ge(biased_s[n], QT * (i + 1) + t + 1)
                    act.activation(squares[:, "kq".index(n), t, :], rows[n][:, t, :], ACT.Square,
                                   accum_out=sq_sum[n][:, t:t + 1]).then_inc(sq_s[n], 1)
                    if isinstance(i, int) and i < 0 and (n, t) == ("k", QT - 1):
                        split_weight()

                def turned_rows_hi(n, t):
                    bank = use[f"{n}T{t}"][0]
                    act.wait_ge(turned_s[n], QT * (i + 1) + t + 1)
                    if t == 0:
                        need(act, scores_done, UNITS * (i + 1))
                    act.copy(hT[n][0][:, :, t * P:(t + 1) * P],
                             shared_ps[bank][:].rearrange("p (c t) -> p c t", c=KC)).then_inc(hi_s[n], 1)

                def xn2T_hi(q):
                    bank = use[f"nT{q}"][0]
                    act.wait_ge(n_turned, QT * (i - 1) + q + 1)
                    act.copy(tT_hi[:, :, q * P:(q + 1) * P],
                             shared_ps[bank][:].rearrange("p (c t) -> p c t", c=KC)).then_inc(n_hi_s, 1)

                def xT_hi(q):
                    bank = use[f"xT{q}"][0]
                    act.wait_ge(x_turned, QT * (i + 1) + q + 1)
                    act.copy(tT_hi[:, :, q * P:(q + 1) * P],
                             shared_ps[bank][:].rearrange("p (c t) -> p c t", c=KC)).then_inc(x_hi_s, 1)
                    if isinstance(i, int) and i < 0 and q == QT - 1:
                        split_weight()

                def routing_exp():
                    act.wait_ge(lgmax_s, i)
                    for q in range(QT):
                        last = act.activation(score[:, q, :], score[:, q, :], ACT.Exp,
                                              bias=lg_max[:, q:q + 1], accum_out=lg_sum[:, q:q + 1])
                    last.then_inc(lgexp_s, 1)

                if kind.attend:
                    v_part(0)
                if kind.post:
                    attended_hi(i - 1, 3)
                if kind.attend:
                    exp_unit(0)
                    exp_unit(1)
                    v_part(1)
                if kind.prep:
                    context_hi()
                if kind.attend:
                    turned_hi(0)
                    exp_unit(2)
                    turned_hi(1)
                    exp_unit(3)
                    attended_hi(i, 0)
                if kind.post:
                    xn2T_hi(0)
                if kind.attend:
                    turned_hi(2)
                if kind.prep:
                    row_squares("k", 0)
                if kind.post:
                    xn2T_hi(1)
                if kind.attend:
                    exp_unit(4)
                    turned_hi(3)
                if kind.prep:
                    row_squares("k", 1)
                    xT_hi(0)
                if kind.attend:
                    exp_unit(5)
                if kind.prep:
                    xT_hi(1)
                if kind.post:
                    routing_exp()
                if kind.attend:
                    exp_unit(6)
                    turned_hi(4)
                    attended_hi(i, 1)
                if kind.prep:
                    turned_rows_hi("k", 0)
                if kind.attend:
                    turned_hi(5)
                    exp_unit(7)
                    attended_hi(i, 2)
                    turned_hi(6)
                if kind.prep:
                    turned_rows_hi("q", 0)
                    row_squares("q", 0)
                    turned_rows_hi("q", 1)
                    row_squares("q", 1)
                if kind.attend:
                    turned_hi(7)
                if kind.prep:
                    turned_rows_hi("k", 1)

            pipeline(act, body)

        @block.vector
        def _(v):
            class Chain:

                def __init__(self, name, per, b):
                    self.sem, self.per, self.b, self.n = chain[name], per, b, 0

                def step(self, ins):
                    self.n += 1
                    ins.then_inc(self.sem, 1)
                    v.wait_ge(self.sem, self.per * self.b + self.n)

            def settle(n):
                v.memset(settled[0:1, n:n + 1], 0.0)

            PREP_STEPS, POST_STEPS = 2, 29
            v.memset(seen[:], 0.0)
            v.memset(seen_b[:], 0.0)
            v.memset(last_tok[:], 0.0)
            setup = Chain("setup", 0, 0)
            pairs = iter(range(0, len(halves), 2))

            def split_weight():
                first = next(pairs)
                for n in (first, first + 1):
                    w, h = halves[n]
                    c = slice(2 * h, 2 * h + 2)
                    v.wait_ge(w_hi_done, n + 1)
                    v.tensor_tensor(w_lo[w][:, c, :].rearrange("p c n -> p (c n)"), stage[n % STAGES],
                                    w_hi[w][:, c, :].rearrange("p c n -> p (c n)").bitcast(F32),
                                    ALU.subtract).then_inc(w_lo_done, 1)

            split_weight()
            v.wait_ge(in_sem, 16)
            v.tensor_copy(tri_b[:], consts[:, P:2 * P])
            v.tensor_copy(ones_b[:], ones)
            v.wait_ge(vec_sem, 16 * 6)
            raw = x2[:, 0, 0:KC * E].rearrange("p (c e) -> p c e", c=KC)
            v.tensor_tensor(gain_row[:], gain_row[:], bo_row[:], ALU.mult).then_inc(gain_s, 1)
            setup.step(v.tensor_copy(gate[:, :, 0, :], raw))
            v.tensor_tensor(gate[:, :, 1, :], raw, gate[:, :, 0, :].bitcast(F32), ALU.subtract).then_inc(gate_split, 1)
            def body(i, kind, use):
                prep, attend, post = Chain("prep", PREP_STEPS, i + 1), Chain("attend", UNITS, i), Chain("post", POST_STEPS, i - 1)

                def unit_max(u):
                    v.wait_ge(scores_done, UNITS * i + u + 1)
                    attend.step(v.tensor_reduce(row_max[:, u % 2, :], scores_ps[u % 2][:], X, ALU.max))
                    need(v, exp_done, UNITS * i + u - 1)
                    if u == 0:
                        v.wait_ge(inv_s["q"], i + 1)
                    v.tensor_scalar(neg_max[:, u % 2, :], row_max[:, u % 2, :], rms_inv["q"][:, u % QT:u % QT + 1],
                                    -1.0, ALU.mult, ALU.mult).then_inc(max_done, 1)

                def unit_inv(u):
                    v.wait_ge(exp_done, UNITS * i + u + 1)
                    need(v, probs_done, UNITS * i + u - 1)
                    v.reciprocal(row_inv[:, u % 2, :], row_sum[:, u % 2, :]).then_inc(inv_done, 1)

                def turned_lo(u):
                    c = slice((u % QT) * P, (u % QT + 1) * P)
                    v.wait_ge(p_hi_s, UNITS * i + u + 1)
                    v.tensor_tensor(pT_lo[:, :, c], pT_ps[:], pT_hi[:, :, c].bitcast(F32),
                                    ALU.subtract).then_inc(p_lo_s, 1)

                def attended_lo(b, c):
                    bank = use[f"pv{c}"][0]
                    v.wait_ge(a_hi_s, KC * b + c + 1)
                    v.scalar_tensor_tensor(aT_lo[:, c, :], shared_ps[bank][:, 0:S], bv_col[:, c:c + 1],
                                           aT_hi[:, c, :].bitcast(F32), ALU.add, ALU.subtract).then_inc(a_lo_s, 1)

                def v_part(t):
                    bank = use[f"v{t}"][0]
                    v.wait_ge(v_hi_s, KT * i + t + 1)
                    for src, hi, lo in zip(heads_of(shared_ps[bank][:]), heads_in(v_hi, t), heads_in(v_lo, t)):
                        last = v.tensor_tensor(lo, src, hi.bitcast(F32), ALU.subtract)
                    last.then_inc(v_lo_s, 1)

                def ln_stats_of(src, stats, mv, var, ch, at):
                    for q in range(QT):
                        last = v.bn_stats(stats[:, q, :], src[:, q, :])
                    ch.step(last)
                    settle(at)
                    for q in range(QT):
                        last = v.bn_aggr(mv[:, q, :], stats[:, q, :])
                    ch.step(last)
                    return v.tensor_scalar(var[:], mv[:, :, 1], LN_EPS, None, ALU.add)

                def biased(n, t):
                    bank = use[f"{n}{t}"][0]
                    v.wait_ge(proj[n], QT * (i + 1) + t + 1)
                    if t == 0:
                        need(v, turned_s[n], QT * (i + 1))
                    v.tensor_tensor(rows[n][:, t, :], shared_ps[bank][:], bias_row[n][:], ALU.add).then_inc(biased_s[n], 1)
                    if isinstance(i, int) and i < 0 and (n, t) == ("k", QT - 1):
                        split_weight()

                def mean_square(n):
                    unit = 1.0 if n == "k" else SCALE * SCALE
                    v.wait_ge(sq_s[n], QT * (i + 2))
                    v.tensor_scalar(mean_sq[n][:], sq_sum[n][:], 1.0 / (D * unit), RMS_EPS / unit, ALU.mult,
                                    ALU.add).then_inc(ms_s[n], 1)

                def k_norm(t):
                    if t == 0:
                        v.wait_ge(inv_s["k"], i + 2)
                    v.scalar_tensor_tensor(rows["k"][:, t, :], rows["k"][:, t, :], rms_inv["k"][:, t:t + 1], gain_row[:],
                                           ALU.mult, ALU.mult).then_inc(k_normed, 1)

                def turned_rows_lo(n, t):
                    bank = use[f"{n}T{t}"][0]
                    c = slice(t * P, (t + 1) * P)
                    v.wait_ge(hi_s[n], QT * (i + 1) + t + 1)
                    v.tensor_tensor(hT[n][1][:, :, c], shared_ps[bank][:].rearrange("p (c t) -> p c t", c=KC),
                                    hT[n][0][:, :, c].bitcast(F32), ALU.subtract).then_inc(lo_s[n], 1)

                def residual(q):
                    if q == 0:
                        v.wait_ge(bo_added, i)
                    v.wait_ge(o_done, QT * (i - 1) + q + 1)
                    v.tensor_tensor(x2[:, q, :], shared_ps[use[f"o{q}"][0]][:], x2[:, q, :], ALU.add).then_inc(x2_s, 1)

                def ln2_stats():
                    v.wait_ge(x2_s, QT * i)
                    ln_stats_of(x2, n2_stats, n2_mv, n2_var, post, 0).then_inc(stats2, 1)

                def ln2_norm(q):
                    if q == 0:
                        v.wait_ge(rstd2, i)
                        need(v, xn2_out, 16 * (i - 1))
                    v.tensor_scalar(xn2[:, q, :], x2[:, q, :], n2_mv[:, q, 0:1], n2_rstd[:, q:q + 1],
                                    ALU.subtract, ALU.mult).then_inc(xn2_s, 1)

                def ln1_stats():
                    v.wait_ge(x_in, 16 * (i + 2))
                    ln_stats_of(x_raw, ln_stats, ln_mv, ln_var, prep, 1).then_inc(stats1, 1)
                    if isinstance(i, int) and i < 0:
                        split_weight()

                def ln1_norm(q):
                    if q == 0:
                        v.wait_ge(rstd1, i + 2)
                    v.tensor_scalar(x_raw[:, q, :], x_raw[:, q, :], ln_mv[:, q, 0:1], ln_rstd[:, q:q + 1],
                                    ALU.subtract, ALU.mult).then_inc(xn_s, 1)

                def xn2T_lo(q):
                    c = slice(q * P, (q + 1) * P)
                    v.wait_ge(n_hi_s, QT * (i - 1) + q + 1)
                    v.tensor_tensor(tT_lo[:, :, c], shared_ps[use[f"nT{q}"][0]][:]
                                    .rearrange("p (c t) -> p c t", c=KC), tT_hi[:, :, c].bitcast(F32),
                                    ALU.subtract).then_inc(n_lo_s, 1)

                def xT_lo(q):
                    c = slice(q * P, (q + 1) * P)
                    v.wait_ge(x_hi_s, QT * (i + 1) + q + 1)
                    v.tensor_tensor(tT_lo[:, :, c], shared_ps[use[f"xT{q}"][0]][:]
                                    .rearrange("p (c t) -> p c t", c=KC), tT_hi[:, :, c].bitcast(F32),
                                    ALU.subtract).then_inc(x_lo_s, 1)
                    if isinstance(i, int) and i < 0 and q == QT - 1:
                        split_weight()

                def logit_max():
                    parts = shared_ps[use["logits"][0]][:, 0:2 * QT * E].rearrange("p (q a e) -> p q a e", q=QT, a=2)
                    v.wait_ge(logits_done, i)
                    post.step(v.tensor_copy(score[:], parts[:, :, 1, :]))
                    post.step(v.tensor_tensor(score[:], parts[:, :, 0, :], score[:], ALU.add))
                    post.step(v.tensor_reduce(lg_max[:], score[:], X, ALU.max))
                    v.tensor_scalar(lg_max[:], lg_max[:], -1.0, None, ALU.mult).then_inc(lgmax_s, 1)

                groups = score[:].rearrange("p q e -> p (q e)").rearrange("p (g e) -> p g e", e=GE)

                def best_groups():
                    v.wait_ge(lgexp_s, i)
                    post.step(v.reciprocal(lg_sum[:], lg_sum[:]))
                    post.step(v.tensor_tensor(score[:], score[:], lg_sum[:].unsqueeze(2).to_broadcast([P, QT, E]),
                                              ALU.mult))
                    post.step(v.tensor_reduce(g_score[:].rearrange("p q g -> p (q g)"), groups, X, ALU.max))
                    settle(2)
                    for q in range(QT):
                        last = v.max(g_top[:, q, :], g_score[:, q, :])
                    post.step(last)
                    settle(3)
                    for q in range(QT):
                        last = v.max_index(g_idx[:, q, :], g_top[:, q, :], g_score[:, q, :])
                    post.step(last)
                    post.step(v.tensor_copy(g_idxf[:], g_idx[:]))
                    post.step(v.tensor_tensor(
                        g_hot[:], iota_g.unsqueeze(1).unsqueeze(1).to_broadcast([P, QT, TOPK_GROUP, N_GROUP]),
                        g_idxf[:, :, 0:TOPK_GROUP].unsqueeze(3).to_broadcast([P, QT, TOPK_GROUP, N_GROUP]),
                        ALU.is_equal))
                    post.step(v.tensor_reduce(g_mask[:], g_hot[:].rearrange("p q k g -> p q g k"), X, ALU.add))
                    post.step(v.tensor_tensor(groups, groups, g_mask[:].rearrange("p q g -> p (q g)").unsqueeze(2)
                                              .to_broadcast([P, QT * N_GROUP, GE]), ALU.mult))
                    settle(4)
                    for q in range(QT):
                        last = v.max(e_top[:, q, :], score[:, q, :])
                    post.step(last)

                def best_experts():
                    settle(5)
                    for q in range(QT):
                        last = v.max_index(e_idx[:, q, :], e_top[:, q, :], score[:, q, :])
                    post.step(last)
                    post.step(v.tensor_copy(e_idxf[:], e_idx[:]))
                    post.step(v.tensor_tensor(
                        e_hot[:], iota_e.unsqueeze(1).unsqueeze(1).to_broadcast([P, QT, TOP_K, E]),
                        e_idxf[:, :, 0:TOP_K].unsqueeze(3).to_broadcast([P, QT, TOP_K, E]), ALU.is_equal))
                    post.step(v.tensor_reduce(mask_f[:], e_hot[:].rearrange("p q k e -> p q e k"), X, ALU.add))
                    v.tensor_copy(mask_b[:], mask_f[:]).then_inc(mask_s, 1)
                    for q in range(QT):
                        post.step(v.scalar_tensor_tensor(last_tok[:], mask_f[:, q, :], tok_col[:, q:q + 1],
                                                         last_tok[:], ALU.mult, ALU.max))
                    settle(6)
                    v.tensor_copy(keep["weight"][:, bass.ds((i - 1) * QT * TOP_K, QT * TOP_K)]
                                  .rearrange("p (q k) -> p q k", q=QT), e_top[:, :, 0:TOP_K])

                def slot_values():
                    v.wait_ge(pos_done, i)
                    v.scalar_tensor_tensor(slot_val[:], shared_ps[use["pos"][0]][:, 0:QT * E]
                                           .rearrange("p (q e) -> p q e", q=QT), float(CAPACITY - 1),
                                           slot_base.unsqueeze(1).to_broadcast([P, QT, E]), ALU.min,
                                           ALU.add).then_inc(pos_read, 1)

                def slots():
                    for q in range(QT):
                        post.step(v.tensor_tensor(seen[:], seen[:], mask_f[:, q, :], ALU.add))
                    v.tensor_copy(seen_b[:], seen[:])
                    v.wait_ge(pos_read, i)
                    post.step(v.tensor_tensor(e_slot[:], e_hot[:], slot_val[:].unsqueeze(2)
                                              .to_broadcast([P, QT, TOP_K, E]), ALU.mult))
                    post.step(v.tensor_reduce(slot_f[:], e_slot[:], X, ALU.add))

                def scatter_index():
                    settle(7)
                    v.tensor_copy(keep["slot"][:, bass.ds((i - 1) * QT * TOP_K, QT * TOP_K)],
                                  slot_f[:].rearrange("p q k -> p (q k)"))
                    post.step(v.tensor_scalar(last_slot[:], e_idxf[:, :, 0:TOP_K], float(CAPACITY),
                                              float(CAPACITY - 1), ALU.mult, ALU.add))
                    post.step(v.tensor_tensor(is_last[:], slot_f[:], last_slot[:], ALU.is_equal))
                    post.step(v.scalar_tensor_tensor(scat_f[:], is_last[:], OVER, slot_f[:], ALU.mult, ALU.add))
                    need(v, scattered, 16 * QT * TOP_K * (i - 1))
                    v.tensor_copy(scat_idx[:], scat_f[:].rearrange("p q k -> p (q k)"))
                    v.tensor_scalar(scat_tok[:], tok_col, -1.0, None, ALU.add).then_inc(scat_rdy, 1)
                    post.step(v.tensor_scalar(tok_col, tok_col, float(S), None, ALU.add))

                if kind.attend:
                    v_part(0)
                if kind.post:
                    attended_lo(i - 1, 3)
                if kind.attend:
                    unit_max(0)
                    unit_max(1)
                    unit_inv(0)
                if kind.post:
                    residual(0)
                if kind.prep:
                    ln1_stats()
                if kind.attend:
                    unit_inv(1)
                    unit_max(2)
                    v_part(1)
                    turned_lo(0)
                if kind.post:
                    residual(1)
                if kind.attend:
                    unit_inv(2)
                if kind.post:
                    ln2_stats()
                if kind.attend:
                    turned_lo(1)
                    unit_max(3)
                if kind.prep:
                    biased("k", 0)
                if kind.post:
                    ln2_norm(0)
                if kind.attend:
                    unit_max(4)
                if kind.post:
                    ln2_norm(1)
                if kind.attend:
                    unit_inv(3)
                    attended_lo(i, 0)
                if kind.post:
                    xn2T_lo(0)
                if kind.attend:
                    turned_lo(2)
                if kind.prep:
                    ln1_norm(0)
                if kind.post:
                    xn2T_lo(1)
                if kind.prep:
                    ln1_norm(1)
                if kind.attend:
                    unit_max(5)
                    unit_inv(4)
                if kind.prep:
                    biased("k", 1)
                if kind.attend:
                    turned_lo(3)
                if kind.post:
                    logit_max()
                if kind.prep:
                    xT_lo(0)
                if kind.attend:
                    unit_max(6)
                    unit_inv(5)
                if kind.prep:
                    mean_square("k")
                    xT_lo(1)
                if kind.post:
                    best_groups()
                if kind.prep:
                    k_norm(0)
                if kind.attend:
                    turned_lo(4)
                    attended_lo(i, 1)
                if kind.prep:
                    biased("q", 0)
                if kind.attend:
                    unit_max(7)
                if kind.prep:
                    turned_rows_lo("k", 0)
                if kind.attend:
                    unit_inv(6)
                    turned_lo(5)
                if kind.post:
                    best_experts()
                if kind.prep:
                    biased("q", 1)
                if kind.attend:
                    unit_inv(7)
                    attended_lo(i, 2)
                if kind.post:
                    slot_values()
                if kind.attend:
                    turned_lo(6)
                if kind.prep:
                    turned_rows_lo("q", 0)
                    k_norm(1)
                    turned_rows_lo("q", 1)
                    mean_square("q")
                if kind.attend:
                    turned_lo(7)
                if kind.prep:
                    turned_rows_lo("k", 1)
                if kind.post:
                    slots()
                    scatter_index()
                assert prep.n in (0, PREP_STEPS) and attend.n in (0, UNITS) and post.n in (0, POST_STEPS)

            pipeline(v, body)
            v.wait_ge(lastT_s, 1)
            bank = plans[-2]["pos"][0]
            end = Chain("setup", 1, 1)
            end.step(v.tensor_reduce(lastT[:], shared_ps[bank][0:E, 0:P], X, ALU.max))
            end.step(v.tensor_scalar(lastT[:], lastT[:], -1.0, 0.0, ALU.add, ALU.max))
            v.tensor_copy(lastT_i[:], lastT[:]).then_inc(last_i_s, 1)

        @block.gpsimd
        def _(g):
            g.memset(zero_i[:], 0).then_inc(setup_p, 1)
            g.memset(minus_half[:], -0.5).then_inc(setup_p, 1)
            g.wait_ge(setup_p, 2)

            def body(i, kind, use):
                def norm_unit(u):
                    if isinstance(i, int) and i == 0 and u == 0:
                        g.wait_ge(table_zeroed, 16)
                    if kind.scatter and u == 0:
                        g.wait_ge(scat_rdy, i - 1)
                    g.wait_ge(inv_done, UNITS * i + u + 1)
                    pr = probs[:, u % 2, :, :]
                    g.tensor_tensor(pr, pr, row_inv[:, u % 2, :].unsqueeze(2).to_broadcast([P, HC, CK]),
                                    ALU.mult).then_inc(probs_done, 1)

                def context_lo():
                    g.wait_ge(ctx_hi_s, i + 2)
                    g.tensor_tensor(ctx_lo[:], ctx_raw[:], ctx_hi[:].bitcast(F32), ALU.subtract).then_inc(ctx_lo_s, 1)
                    if isinstance(i, int) and i < 0:
                        g.memset(v_hi[:].bitcast(F32), 0.0).then_inc(setup_p, 1)
                        g.memset(v_lo[:].bitcast(F32), 0.0).then_inc(setup_p, 1)

                def add_bo():
                    if isinstance(i, int) and i == 1:
                        g.wait_ge(bo_in, 16)
                    g.wait_ge(res_in, 16 * i)
                    g.tensor_tensor(x2[:], x2[:], bo_row[:].unsqueeze(1).to_broadcast([P, QT, D]),
                                    ALU.add).then_inc(bo_added, 1)

                def ln2_rstd():
                    g.wait_ge(stats2, i)
                    g.tensor_tensor(n2_rstd[:], n2_var[:], minus_half[:], ALU.pow).then_inc(rstd2, 1)

                def ln1_rstd():
                    g.wait_ge(stats1, i + 2)
                    g.tensor_tensor(ln_rstd[:], ln_var[:], minus_half[:], ALU.pow).then_inc(rstd1, 1)

                def rms_inverse(n):
                    g.wait_ge(ms_s[n], i + 2)
                    if n == "q":
                        need(g, exp_done, UNITS * (i + 1))
                    g.tensor_tensor(rms_inv[n][:], mean_sq[n][:], minus_half[:], ALU.pow).then_inc(inv_s[n], 1)

                def scatter(s):
                    if not kind.attend and s == 0:
                        g.wait_ge(scat_rdy, i - 1)
                    for j in (2 * s, 2 * s + 1):
                        q = j // TOP_K
                        g.indirect_dma_start(
                            out=d["table"], out_offset=bass.IndirectOffsetOnAxis(ap=scat_idx[:, j:j + 1], axis=0),
                            in_=scat_tok[:, q:q + 1], in_offset=None, bounds_check=E * CAPACITY - 1,
                            oob_is_err=False).then_inc(scattered, 16)

                if kind.post:
                    add_bo()
                if kind.attend:
                    norm_unit(0)
                if kind.scatter:
                    scatter(0)
                if kind.attend:
                    norm_unit(1)
                if kind.prep:
                    context_lo()
                if kind.scatter:
                    scatter(1)
                if kind.post:
                    ln2_rstd()
                if kind.attend:
                    norm_unit(2)
                if kind.prep:
                    ln1_rstd()
                if kind.scatter:
                    scatter(2)
                if kind.attend:
                    norm_unit(3)
                    norm_unit(4)
                    norm_unit(5)
                if kind.prep:
                    rms_inverse("k")
                if kind.attend:
                    norm_unit(6)
                    norm_unit(7)
                if kind.scatter:
                    scatter(3)
                    scatter(4)
                    scatter(5)
                if kind.prep:
                    rms_inverse("q")

            pipeline(g, body)
            g.wait_ge(scattered, 16 * QT * TOP_K * B)


def phase_b(nc, d, shared_w, first_rows, first_in):
    E = d["experts"].shape[0]
    D = d["xn2"].shape[-1]
    KC = D // P
    M = d["m"]
    ROWS = CAPACITY // 2
    MC = -(-M // P)
    col = [min(m * P, M - P) for m in range(MC)]
    GU, DN = 2 * KC * M, MC * D
    SH = d["shared_gu"].shape[2]
    assert KC * SH == 2 * GU

    with ExitStack() as ctx:
        def sb(name, shape, dt=F32):
            return ctx.enter_context(nc.sbuf_tensor(name, shape, dt))

        def ps(name, shape, dt=F32):
            return ctx.enter_context(nc.psum_tensor(name, shape, dt))

        def sem(name):
            return ctx.enter_context(nc.semaphore(name))

        ident = sb("b_ident", [P, P])
        table_i, table_f = sb("table_i", [P, ROWS], I32), sb("table_f", [P, ROWS])
        idxT = sb("idxT", [ROWS, 2 * E], I32)
        idx_now = sb("idx_now", [ROWS, 2, 2], I32)
        rows = sb("rows", [ROWS, 2, 2, D])
        gu_raw, dn_raw = sb("gu_raw", [P, 2, GU]), sb("dn_raw", [P, 2, DN])
        gu_hi, gu_lo = sb("gu_hi", [P, 2, GU], F32R), sb("gu_lo", [P, 2, GU], F32R)
        dn_hi, dn_lo = sb("dn_hi", [P, 2, MC, D], F32R), sb("dn_lo", [P, 2, MC, D], F32R)
        bT = sb("bT", [P, 2, KC, 2, CAPACITY], F32R)
        gate, up = sb("gate", [P, MC, CAPACITY]), sb("up", [P, MC, CAPACITY])
        gate_act, hid = sb("gate_act", [P, MC, CAPACITY]), sb("hid", [P, MC, CAPACITY])
        h_hi, h_lo = sb("h_hi", [P, 2, MC, CAPACITY], F32R), sb("h_lo", [P, 2, MC, CAPACITY], F32R)
        out_rows = sb("out_rows", [ROWS, 2, 2, D])

        gate_ps, up_ps = [ps(f"gate_ps{n}", [P, 512]) for n in range(2)], [ps(f"up_ps{n}", [P, 512]) for n in range(2)]
        bT_ps = [ps(f"bT_ps{n}", [P, 512]) for n in range(2)]
        dn_ps = [ps(f"dn_ps{t}", [P, 512]) for t in range(2)]

        setup_in, idx_f_s, idx_turned, idx_s = (sem("b_table_loaded"), sem("b_table_float"), sem("b_table_turned"),
                                                sem("b_index_ready"))
        gu_in, dn_in, rows_in, stored = ([sem(f"b_{what}{n}") for n in range(2)]
                                         for what in ("gu_loaded", "down_loaded", "rows_gathered", "out_stored"))
        staged = sem("b_index_staged")
        turned, bT_hi_s, bT_lo_s = sem("b_rows_turned"), sem("b_rowsT_hi_done"), sem("b_rowsT_lo_done")
        gu_hi_s, gu_lo_s = sem("b_gu_hi_done"), sem("b_gu_lo_done")
        dn_hi_s, dn_lo_s = sem("b_down_hi_done"), sem("b_down_lo_done")
        gu_done, act_s, hid_s = sem("b_gu_product_done"), sem("b_silu_done"), sem("b_hidden_done")
        part_s, gate_s, up_s = sem("b_lo_part_copied"), sem("b_gate_summed"), sem("b_up_summed")
        h_hi_s, h_lo_s = sem("b_hidden_hi_done"), sem("b_hidden_lo_done")
        dn_done, out_s = sem("b_down_product_done"), sem("b_out_copied")

        def pipeline(eng, body):
            for e in (-1, 0, 1, 2):
                body(e, e % 2, e // 2)
            with eng.Fori(0, (E - 6) // 2) as j:
                for s in range(2):
                    body(2 * j + (3 + s), (3 + s) % 2, j + (3 + s) // 2)
            for e in (E - 3, E - 2, E - 1, E):
                body(e, e % 2, e // 2)

        def at_most(e, last):
            return not isinstance(e, int) or e <= last

        def shared_half(w, e):
            h = e - (E - 1)
            return w[:, h * KC // 2:(h + 1) * KC // 2, :].rearrange("p c m -> p (c m)")

        def parts_of(e, par):
            if at_most(e, E - 2):
                return gu_hi[:, 1 - par, :], gu_lo[:, 1 - par, :]
            return [shared_half(w[:], e) for w in shared_w]

        def at_least(e, first):
            return not isinstance(e, int) or e >= first

        block = ctx.enter_context(nc.Block())

        @block.sync
        def _(sp):
            sp.dma_start(table_i[:], d["table"].rearrange("(k r) o -> k (r o)", r=ROWS)).then_inc(setup_in, 16)
            sp.dma_start(ident[:], d["consts"][:, 0:P]).then_inc(setup_in, 16)

            out_of = d["eo"].rearrange("(e t r) n -> e r t n", t=2, r=ROWS)

            def body(e, par, half):
                need(sp, gu_lo_s, 2 * e)
                if isinstance(e, int) and e == 0:
                    sp.wait_ge(rows_in[0], 32)
                if at_most(e, E - 2):
                    weights = d["experts"][e + 1][:, 0:GU]
                else:
                    weights = shared_half(d["shared_gu"], e)
                sp.dma_start(gu_raw[:, 1 - par, :], weights).then_inc(gu_in[1 - par], 16)
                if at_least(e, 0) and at_most(e, E - 1):
                    need(sp, dn_lo_s, 2 * (e - 1))
                    sp.dma_start(dn_raw[:, par, :], d["experts"][e][:, GU:GU + DN]).then_inc(dn_in[par], 16)
                if at_least(e, 2):
                    sp.wait_ge(out_s, 2 * (e - 1))
                    sp.dma_start(out_of[e - 2], out_rows[:, par, :, :]).then_inc(stored[par], 16)

            pipeline(sp, body)
            sp.dma_start(first_rows[:], d["xn2_rows"][0:first_rows.shape[1] * P, :]
                         .rearrange("(q p) n -> p q n", p=P)).then_inc(first_in, 16)
            sp.wait_ge(out_s, 2 * E)
            sp.dma_start(out_of[E - 1], out_rows[:, (E - 1) % 2, :, :]).then_inc(stored[(E - 1) % 2], 16)
            for n in range(2):
                sp.wait_ge(stored[n], 16 * (E // 2))

        @block.tensor
        def _(pe):
            def mm3(out, a_hi, a_lo, b_hi, b_lo, first, last):
                pe.matmul(out, a_hi, b_hi, start=first, stop=False)
                pe.matmul(out, a_hi, b_lo, start=False, stop=False)
                return pe.matmul(out, a_lo, b_hi, start=False, stop=last)

            pe.wait_ge(setup_in, 32)
            pe.wait_ge(idx_f_s, 1)
            pe.transpose(bT_ps[0][0:ROWS, 0:P], table_f[:], ident[:]).then_inc(idx_turned, 1)

            def body(e, par, half):
                def turn_rows(n):
                    nxt = 1 - par
                    if n == 0:
                        pe.wait_ge(rows_in[nxt], 32 * (half + par + 1))
                        if isinstance(e, int) and e < 0:
                            pe.wait_ge(idx_s, 1)
                    need(pe, bT_lo_s, 2 * e + n + 1 if at_least(e, 0) else 0)
                    for k in range(2):
                        for t in range(2):
                            c = (2 * n + k) * P
                            last = pe.transpose(bT_ps[n][:, k * CAPACITY + t * ROWS:k * CAPACITY + (t + 1) * ROWS],
                                                rows[:, nxt, t, c:c + P], ident[0:ROWS, 0:ROWS])
                    last.then_inc(turned, 1)

                def gate_up(m):
                    if m == 0:
                        pe.wait_ge(bT_lo_s, 2 * (e + 1))
                        pe.wait_ge(gu_lo_s, 2 * (e + 1))
                    need(pe, up_s, MC * e + (m - 1))
                    n = (par + m) % 2
                    for g, bank in enumerate((gate_ps[n], up_ps[n])):
                        for kc in range(KC):
                            w = (g * KC + kc) * M + col[m]
                            pe.matmul(bank[:, 0:2 * CAPACITY], gu_hi[:, par, w:w + P],
                                      bT[:, par, kc, :, :].rearrange("p a t -> p (a t)"), start=kc == 0, stop=False)
                            last = pe.matmul(bank[:, 0:CAPACITY], gu_lo[:, par, w:w + P], bT[:, par, kc, 0, :],
                                             start=False, stop=kc == KC - 1)
                    last.then_inc(gu_done, 1)

                def down(t):
                    o = 1 - par
                    if t == 0:
                        pe.wait_ge(h_lo_s, MC * e)
                        pe.wait_ge(dn_lo_s, 2 * e)
                    need(pe, out_s, 2 * e + (t - 3))
                    r = slice(t * ROWS, (t + 1) * ROWS)
                    for m in range(MC):
                        last = mm3(dn_ps[t][0:ROWS, :], h_hi[:, o, m, r], h_lo[:, o, m, r], dn_hi[:, o, m, :],
                                   dn_lo[:, o, m, :], m == 0, m == MC - 1)
                    last.then_inc(dn_done, 1)

                ahead, mid, late = at_most(e, E - 2), at_least(e, 0) and at_most(e, E - 1), at_least(e, 1)
                if mid:
                    gate_up(0)
                    gate_up(1)
                    gate_up(2)
                if ahead:
                    turn_rows(0)
                    turn_rows(1)
                if late:
                    down(0)
                    down(1)

            pipeline(pe, body)

        @block.scalar
        def _(act):
            def body(e, par, half):
                ahead, mid, late = at_most(e, E - 2), at_least(e, 0) and at_most(e, E - 1), at_least(e, 1)

                def rows_hi(n):
                    act.wait_ge(turned, 2 * e + (n + 3))
                    act.copy(bT[:, 1 - par, 2 * n:2 * n + 2, 0, :],
                             bT_ps[n][:, 0:2 * CAPACITY].rearrange("p (k t) -> p k t", k=2)).then_inc(bT_hi_s, 1)

                def lo_part(m):
                    n = (par + m) % 2
                    act.wait_ge(gu_done, MC * e + (m + 1))
                    act.copy(gate[:, m, :], gate_ps[n][:, CAPACITY:2 * CAPACITY])
                    act.copy(up[:, m, :], up_ps[n][:, CAPACITY:2 * CAPACITY]).then_inc(part_s, 1)

                def silu(m):
                    act.wait_ge(gate_s, MC * e + (m + 1))
                    act.activation(gate_act[:, m, :], gate[:, m, :], ACT.Silu).then_inc(act_s, 1)

                def hidden_hi(m):
                    act.wait_ge(hid_s, MC * e + (m + 1))
                    act.copy(h_hi[:, par, m, :], hid[:, m, :]).then_inc(h_hi_s, 1)

                def weights_hi(g):
                    c = slice(g * KC * M, (g + 1) * KC * M)
                    act.wait_ge(gu_in[1 - par], 16 * (half + par + 1))
                    act.copy(parts_of(e, par)[0][:, c], gu_raw[:, 1 - par, c]).then_inc(gu_hi_s, 1)

                def down_hi():
                    act.wait_ge(dn_in[par], 16 * (half + 1))
                    act.copy(dn_hi[:, par, :, :].rearrange("p m n -> p (m n)"), dn_raw[:, par, :]).then_inc(dn_hi_s, 1)

                def copy_out(t):
                    if t == 0:
                        need(act, stored[1 - par], 16 * (half + par - 1))
                    act.wait_ge(dn_done, 2 * e + (t - 1))
                    act.copy(out_rows[:, 1 - par, t, :], dn_ps[t][0:ROWS, :]).then_inc(out_s, 1)

                weights_hi(0)
                if mid:
                    lo_part(0)
                weights_hi(1)
                if mid:
                    lo_part(1)
                    silu(0)
                    lo_part(2)
                    down_hi()
                if ahead:
                    rows_hi(0)
                if mid:
                    hidden_hi(0)
                if ahead:
                    rows_hi(1)
                if mid:
                    silu(1)
                    hidden_hi(1)
                if late:
                    copy_out(0)
                if mid:
                    silu(2)
                if late:
                    copy_out(1)
                if mid:
                    hidden_hi(2)

            pipeline(act, body)

        @block.vector
        def _(v):
            v.wait_ge(setup_in, 32)
            v.tensor_copy(table_f[:], table_i[:]).then_inc(idx_f_s, 1)
            v.wait_ge(idx_turned, 1)
            v.tensor_copy(idxT[:, 0:2 * E], bT_ps[0][0:ROWS, 0:P]).then_inc(idx_s, 1)

            def body(e, par, half):
                ahead, mid = at_most(e, E - 2), at_least(e, 0) and at_most(e, E - 1)

                def sums(m):
                    n = (par + m) % 2
                    v.wait_ge(part_s, MC * e + (m + 1))
                    v.tensor_tensor(gate[:, m, :], gate_ps[n][:, 0:CAPACITY], gate[:, m, :], ALU.add).then_inc(gate_s, 1)
                    v.tensor_tensor(up[:, m, :], up_ps[n][:, 0:CAPACITY], up[:, m, :], ALU.add).then_inc(up_s, 1)

                def hidden(m):
                    v.wait_ge(act_s, MC * e + (m + 1))
                    v.wait_ge(up_s, MC * e + (m + 1))
                    v.tensor_tensor(hid[:, m, :], gate_act[:, m, :], up[:, m, :], ALU.mult).then_inc(hid_s, 1)

                def hidden_lo(m):
                    v.wait_ge(h_hi_s, MC * e + (m + 1))
                    v.tensor_tensor(h_lo[:, par, m, :], hid[:, m, :], h_hi[:, par, m, :].bitcast(F32),
                                    ALU.subtract).then_inc(h_lo_s, 1)

                def rows_lo(n):
                    v.wait_ge(bT_hi_s, 2 * e + (n + 3))
                    v.tensor_tensor(bT[:, 1 - par, 2 * n:2 * n + 2, 1, :],
                                    bT_ps[n][:, 0:2 * CAPACITY].rearrange("p (k t) -> p k t", k=2),
                                    bT[:, 1 - par, 2 * n:2 * n + 2, 0, :].bitcast(F32), ALU.subtract).then_inc(bT_lo_s, 1)

                def weights_lo(g):
                    c = slice(g * KC * M, (g + 1) * KC * M)
                    v.wait_ge(gu_hi_s, 2 * e + (g + 3))
                    hi, lo = parts_of(e, par)
                    v.tensor_tensor(lo[:, c], gu_raw[:, 1 - par, c], hi[:, c].bitcast(F32), ALU.subtract).then_inc(gu_lo_s, 1)

                if mid:
                    sums(0)
                    hidden(0)
                    sums(1)
                weights_lo(0)
                weights_lo(1)
                if ahead:
                    rows_lo(0)
                if mid:
                    hidden(1)
                    hidden_lo(0)
                if ahead:
                    rows_lo(1)
                if mid:
                    hidden_lo(1)
                    sums(2)
                    hidden(2)
                    hidden_lo(2)

            pipeline(v, body)

        @block.gpsimd
        def _(g):
            def stage(expert, place):
                g.tensor_copy(idx_now[:, place, :], idxT[:, bass.ds(2 * expert, 2)]).then_inc(staged, 1)

            def gather(place):
                for t in range(2):
                    g.indirect_dma_start(
                        out=rows[:, place, t, :], out_offset=None, in_=d["xn2_rows"],
                        in_offset=bass.IndirectOffsetOnAxis(ap=idx_now[:, place, t:t + 1], axis=0),
                    ).then_inc(rows_in[place], 16)

            def body(e, par, half):
                nxt = 1 - par
                if isinstance(e, int) and e < 0:
                    g.wait_ge(idx_s, 1)
                    for n in range(2):
                        stage(n, n)
                        g.wait_ge(staged, n + 1)
                        gather(n)
                    g.wait_ge(rows_in[0], 32)
                    stage(2, 0)
                    return
                def down_lo(m0, m1):
                    g.tensor_tensor(dn_lo[:, nxt, m0:m1, :].rearrange("p m n -> p (m n)"),
                                    dn_raw[:, nxt, m0 * D:m1 * D],
                                    dn_hi[:, nxt, m0:m1, :].rearrange("p m n -> p (m n)").bitcast(F32),
                                    ALU.subtract).then_inc(dn_lo_s, 1)

                if at_least(e, 1):
                    g.wait_ge(dn_hi_s, e)
                    down_lo(0, MC - 1)
                if at_most(e, E - 3):
                    g.wait_ge(turned, 2 * e + 2)
                    g.wait_ge(staged, e + 3)
                    g.wait_ge(rows_in[nxt], 32 * (half + par + 1))
                if at_least(e, 1):
                    down_lo(MC - 1, MC)
                if at_most(e, E - 3):
                    gather(par)
                    if at_most(e, E - 4):
                        stage(e + 3, nxt)

            pipeline(g, body)


def phase_c(nc, d, keep, shared_w, x_rows, x_in):
    T, D = d["xn2_rows"].shape
    KC = D // P
    MS = d["shared_gu"].shape[2] // 2
    MC = -(-MS // P)
    FULL, TAIL = (MC - 1) * P, MS - (MC - 1) * P
    assert 2 * TAIL == P
    GT = x_rows.shape[1]
    GROUPS = T // (GT * P)
    NT = GT * P
    POOL_LO = GT

    with ExitStack() as ctx:
        def sb(name, shape, dt=F32):
            return ctx.enter_context(nc.sbuf_tensor(name, shape, dt))

        def ps(name, shape, dt=F32):
            return ctx.enter_context(nc.psum_tensor(name, shape, dt))

        def sem(name):
            return ctx.enter_context(nc.semaphore(name))

        ident = sb("c_ident", [P, P])
        sd_raw = sb("sd_raw", [P, MC, D])
        sd = [sb(f"sd_{part}", [P, MC, D], F32R) for part in ("hi", "lo")]
        xT_hi, xT_lo = sb("c_xT_hi", [P, KC, NT], F32R), sb("c_xT_lo", [P, KC, NT], F32R)
        gate_act, hid = sb("c_gate_act", [P, 2, NT]), sb("c_hid", [P, 2, NT])
        h_hi, h_lo = sb("c_h_hi", [P, MC, NT], F32R), sb("c_h_lo", [P, MC, NT], F32R)
        idx_now = sb("c_idx_now", [P, GT * TOP_K], U32)
        w_now = sb("c_w_now", [P, GT * TOP_K])
        rows = sb("c_rows", [P, 2, TOP_K, D])
        acc = sb("c_acc", [P, GT, D])
        out_rows = sb("c_out_rows", [P, 2, D])

        xT_ps = [ps(f"c_xT_ps{n}", [P, NT]) for n in range(2)]
        g_ps, u_ps = [ps(f"c_g_ps{n}", [P, NT]) for n in range(2)], [ps(f"c_u_ps{n}", [P, NT]) for n in range(2)]
        dn_ps = [ps(f"c_dn_ps{n}", [P, D]) for n in range(2)]

        zeroed = sem("c_hidden_zeros")
        id_in, w_in = sem("c_ident_loaded"), sem("c_down_loaded")
        w_hi_s, w_lo_s = sem("c_weight_hi_done"), sem("c_weight_lo_done")
        acc_in = sem("c_residual_loaded")
        turned, xT_hi_s, xT_lo_s = sem("c_rows_turned"), sem("c_rowsT_hi_done"), sem("c_rowsT_lo_done")
        gu_done, act_s, hid_s = sem("c_gu_product_done"), sem("c_silu_done"), sem("c_hidden_done")
        h_hi_s, h_lo_v, h_lo_p = sem("c_hidden_hi_done"), sem("c_hidden_lo_by_vector"), sem("c_hidden_lo_by_pool")
        staged = sem("c_index_staged")
        gathered = [sem(f"c_gathered{n}") for n in range(2)]
        routed_s, step_s = sem("c_routed_done"), sem("c_routed_step")
        dn_done, out_s = sem("c_down_product_done"), sem("c_out_done")
        stored = [sem(f"c_out_stored{n}") for n in range(2)]

        def pipeline(eng, body):
            for g in (-1, 0):
                body(g)
            with eng.Fori(1, GROUPS - 1) as g:
                body(g)
            body(GROUPS - 1)

        def part(m):
            return slice(None) if m < MC - 1 else slice(TAIL, P)

        def is_int(g):
            return isinstance(g, int)

        block = ctx.enter_context(nc.Block())

        @block.sync
        def _(sp):
            sp.dma_start(ident[:], d["consts"][:, 0:P]).then_inc(id_in, 16)
            rows_of = d["xn2_rows"].rearrange("(g q p) n -> g p q n", q=GT, p=P)
            x2_of = d["x2_rows"].rearrange("(g q p) n -> g p q n", q=GT, p=P)
            out_of = d["out"].rearrange("(g q p) n -> g p q n", q=GT, p=P)
            sp.dma_start(sd_raw[:], d["sd"]).then_inc(w_in, 16)

            def body(g):
                mid, ahead = not (is_int(g) and g < 0), not (is_int(g) and g == GROUPS - 1)

                if is_int(g) and g < 0:
                    sp.dma_start(acc[:], x2_of[0]).then_inc(acc_in, 16)
                    return
                if not (is_int(g) and g == GROUPS - 1):
                    sp.wait_ge(turned, KC * (g + 1))
                    sp.dma_start(x_rows[:], rows_of[g + 1]).then_inc(x_in, 16)
                for q in range(GT):
                    sp.wait_ge(out_s, GT * g + (q + 1))
                    sp.dma_start(out_of[g][:, q, :], out_rows[:, q % 2, :]).then_inc(stored[q % 2], 16)
                if not (is_int(g) and g == GROUPS - 1):
                    sp.dma_start(acc[:], x2_of[g + 1]).then_inc(acc_in, 16)

            pipeline(sp, body)
            for n in range(2):
                sp.wait_ge(stored[n], 16 * GROUPS * GT // 2)

        @block.tensor
        def _(pe):
            def mm3(out, a, b, a_at, b_at, first, last):
                pe.matmul(out, a[0][a_at], b[0][b_at], start=first, stop=False)
                pe.matmul(out, a[0][a_at], b[1][b_at], start=False, stop=False)
                return pe.matmul(out, a[1][a_at], b[0][b_at], start=False, stop=last)

            full = slice(None)

            def body(g):
                mid, ahead = not (is_int(g) and g < 0), not (is_int(g) and g == GROUPS - 1)

                def turn_rows(kc):
                    if kc == 0:
                        if is_int(g) and g < 0:
                            pe.wait_ge(id_in, 16)
                        pe.wait_ge(x_in, 16 * (g + 2))
                    need(pe, xT_lo_s, KC * g + (KC + kc - 1) if mid else kc - 1)
                    for q in range(GT):
                        last = pe.transpose(xT_ps[kc % 2][:, q * P:(q + 1) * P], x_rows[:, q, kc * P:(kc + 1) * P],
                                            ident[:])
                    last.then_inc(turned, 1)

                def gate_up(m):
                    if m == 0:
                        pe.wait_ge(xT_lo_s, KC * (g + 1))
                    need(pe, hid_s, MC * g + (m - 1))
                    if m < MC - 1:
                        products = ((g_ps[m % 2], m * P, 1), (u_ps[m % 2], FULL + m * P, 1))
                    else:
                        products = ((g_ps[m % 2], 2 * FULL, 2),)
                    for bank, w, count in products:
                        for kc in range(KC):
                            last = mm3(bank[:], shared_w, (xT_hi, xT_lo), (full, kc, slice(w, w + P)),
                                       (full, kc, full), kc == 0, kc == KC - 1)
                        last.then_inc(gu_done, count)

                def down(q):
                    if q == 0:
                        pe.wait_ge(h_lo_p, POOL_LO * (g + 1))
                        pe.wait_ge(h_lo_v, (MC - POOL_LO) * (g + 1))
                        if is_int(g) and g == 0:
                            pe.wait_ge(w_lo_s, 1)
                    need(pe, out_s, GT * g + (q - 1))
                    for m in range(MC):
                        last = mm3(dn_ps[q % 2][:], (h_hi, h_lo), sd, (full, m, slice(q * P, (q + 1) * P)),
                                   (full, m, full), m == 0, m == MC - 1)
                    last.then_inc(dn_done, 1)

                if mid:
                    gate_up(0)
                    gate_up(1)
                    gate_up(2)
                    gate_up(3)
                    gate_up(4)
                    gate_up(5)
                if ahead:
                    turn_rows(0)
                    turn_rows(1)
                    turn_rows(2)
                    turn_rows(3)
                if mid:
                    down(0)
                    down(1)
                    down(2)
                    down(3)

            pipeline(pe, body)

        @block.scalar
        def _(act):
            def body(g):
                mid, ahead = not (is_int(g) and g < 0), not (is_int(g) and g == GROUPS - 1)

                def rows_hi(kc):
                    act.wait_ge(turned, KC * (g + 1) + (kc + 1))
                    if kc == 0:
                        need(act, gu_done, 2 * MC * (g + 1))
                    act.copy(xT_hi[:, kc, :], xT_ps[kc % 2][:]).then_inc(xT_hi_s, 1)

                def silu(m):
                    act.wait_ge(gu_done, 2 * MC * g + (2 * m + 1))
                    need(act, hid_s, MC * g + (m - 1))
                    out, src = part(m), (slice(0, TAIL) if m == MC - 1 else slice(None))
                    act.activation(gate_act[out, m % 2, :], g_ps[m % 2][src, :], ACT.Silu).then_inc(act_s, 1)

                def hidden_hi(m):
                    act.wait_ge(hid_s, MC * g + (m + 1))
                    if m == 0:
                        need(act, dn_done, GT * g)
                        if is_int(g) and g == 0:
                            act.wait_ge(zeroed, 2)
                    act.copy(h_hi[part(m), m, :], hid[part(m), m % 2, :]).then_inc(h_hi_s, 1)

                if mid:
                    silu(0)
                    hidden_hi(0)
                    silu(1)
                    hidden_hi(1)
                    silu(2)
                    silu(3)
                    hidden_hi(2)
                    hidden_hi(3)
                    silu(4)
                    silu(5)
                if ahead:
                    rows_hi(0)
                    rows_hi(1)
                if mid:
                    hidden_hi(4)
                    hidden_hi(5)
                if ahead:
                    rows_hi(2)
                    rows_hi(3)
                if not mid:
                    act.wait_ge(w_in, 16)
                    act.copy(sd[0][:], sd_raw[:]).then_inc(w_hi_s, 1)

            pipeline(act, body)

        @block.vector
        def _(v):
            def body(g):
                mid, ahead = not (is_int(g) and g < 0), not (is_int(g) and g == GROUPS - 1)

                def rows_lo(kc):
                    v.wait_ge(xT_hi_s, KC * (g + 1) + (kc + 1))
                    v.tensor_tensor(xT_lo[:, kc, :], xT_ps[kc % 2][:], xT_hi[:, kc, :].bitcast(F32),
                                    ALU.subtract).then_inc(xT_lo_s, 1)

                def routed(q):
                    v.wait_ge(gathered[q % 2], 16 * TOP_K * (2 * g + (q // 2 + 1)))
                    if q == 0:
                        v.wait_ge(acc_in, 16 * (g + 1))
                        v.wait_ge(staged, g + 1)
                    for k in range(TOP_K):
                        last = v.scalar_tensor_tensor(acc[:, q, :], rows[:, q % 2, k, :],
                                                      w_now[:, q * TOP_K + k:q * TOP_K + k + 1], acc[:, q, :],
                                                      ALU.mult, ALU.add)
                        if k < TOP_K - 1:
                            last.then_inc(step_s, 1)
                            v.wait_ge(step_s, (TOP_K - 1) * GT * g + ((TOP_K - 1) * q + k + 1))
                    last.then_inc(routed_s, 1)

                def out_tile(q):
                    v.wait_ge(dn_done, GT * g + (q + 1))
                    v.wait_ge(routed_s, GT * g + (q + 1))
                    need(v, stored[q % 2], 16 * 2 * g + 16 * (q // 2))
                    v.tensor_tensor(out_rows[:, q % 2, :], dn_ps[q % 2][:], acc[:, q, :], ALU.add).then_inc(out_s, 1)

                def stage(group):
                    at = bass.ds(group * (GT * TOP_K), GT * TOP_K)
                    v.tensor_scalar(w_now[:], keep["weight"][:, at], 1.0, None, ALU.mult)
                    v.tensor_copy(idx_now[:], keep["slot"][:, at]).then_inc(staged, 1)

                def stage_next():
                    v.wait_ge(routed_s, GT * (g + 1))
                    stage(g + 1)

                def hidden(m):
                    v.wait_ge(act_s, MC * g + (m + 1))
                    v.wait_ge(gu_done, 2 * MC * g + (2 * m + 2))
                    if m >= 2:
                        v.wait_ge(h_lo_p, POOL_LO * g + (m - 1))
                    up = u_ps[m % 2] if m < MC - 1 else g_ps[m % 2]
                    v.tensor_tensor(hid[part(m), m % 2, :], gate_act[part(m), m % 2, :], up[part(m), :],
                                    ALU.mult).then_inc(hid_s, 1)

                def hidden_lo(m):
                    v.wait_ge(h_hi_s, MC * g + (m + 1))
                    v.tensor_tensor(h_lo[part(m), m, :], hid[part(m), m % 2, :], h_hi[part(m), m, :].bitcast(F32),
                                    ALU.subtract).then_inc(h_lo_v, 1)

                if not mid:
                    stage(0)
                if mid:
                    hidden(0)
                    hidden(1)
                    hidden(2)
                    routed(0)
                    hidden(3)
                    routed(1)
                    hidden(4)
                if ahead:
                    rows_lo(0)
                if mid:
                    hidden(5)
                    hidden_lo(4)
                if ahead:
                    rows_lo(1)
                if mid:
                    hidden_lo(5)
                    out_tile(0)
                    out_tile(1)
                    routed(2)
                if ahead:
                    rows_lo(2)
                    rows_lo(3)
                if mid:
                    routed(3)
                    out_tile(2)
                    out_tile(3)
                if mid and ahead:
                    stage_next()
                if not mid:
                    v.wait_ge(w_hi_s, 1)
                    v.tensor_tensor(sd[1][:], sd_raw[:], sd[0][:].bitcast(F32), ALU.subtract).then_inc(w_lo_s, 1)

            pipeline(v, body)

        @block.gpsimd
        def _(p):
            def body(g):
                mid, ahead = not (is_int(g) and g < 0), not (is_int(g) and g == GROUPS - 1)

                def hidden_lo(q):
                    p.wait_ge(h_hi_s, MC * g + (q + 1))
                    if q == 0:
                        p.wait_ge(staged, g + 1)
                    need(p, routed_s, GT * g + (q - 1))
                    p.tensor_tensor(h_lo[:, q, :], hid[:, q % 2, :], h_hi[:, q, :].bitcast(F32),
                                    ALU.subtract).then_inc(h_lo_p, 1)

                def gather(q):
                    for k in range(TOP_K):
                        p.indirect_dma_start(
                            out=rows[:, q % 2, k, :], out_offset=None, in_=d["eo"],
                            in_offset=bass.IndirectOffsetOnAxis(ap=idx_now[:, q * TOP_K + k:q * TOP_K + k + 1], axis=0),
                        ).then_inc(gathered[q % 2], 16)

                if not mid:
                    for h in (h_hi, h_lo):
                        p.memset(h[0:TAIL, MC - 1, :].bitcast(F32), 0.0).then_inc(zeroed, 1)
                if mid:
                    hidden_lo(0)
                    gather(0)
                    hidden_lo(1)
                    gather(1)
                    hidden_lo(2)
                    hidden_lo(3)
                    gather(2)
                    gather(3)

            pipeline(p, body)


def cross_attention_moe(nc, d):
    T = d["x"].shape[0] * d["x"].shape[1]
    D = d["x"].shape[2]
    E = d["experts"].shape[0]
    d["x2"] = nc.dram_tensor("x2_scratch", d["x"].shape, F32, kind="Internal").ap()
    d["xn2"] = nc.dram_tensor("xn2_scratch", d["x"].shape, F32, kind="Internal").ap()
    d["table"] = nc.dram_tensor("slot_token_scratch", [E * CAPACITY, 1], I32, kind="Internal").ap()
    d["eo"] = nc.dram_tensor("expert_out_scratch", [E * CAPACITY, D], F32, kind="Internal").ap()
    d["x2_rows"], d["xn2_rows"] = (d[n].rearrange("b s n -> (b s) n") for n in ("x2", "xn2"))
    with ExitStack() as ctx:
        keep = {"slot": ctx.enter_context(nc.sbuf_tensor("keep_slot", [P, T // P * TOP_K], U32)),
                "weight": ctx.enter_context(nc.sbuf_tensor("keep_weight", [P, T // P * TOP_K], F32))}
        phase_a(nc, d, keep)
        shared_w = [ctx.enter_context(nc.sbuf_tensor(f"shared_gu_{part}", d["shared_gu"].shape, F32R))
                    for part in ("hi", "lo")]
        x_rows = ctx.enter_context(nc.sbuf_tensor("group_rows", [P, 4, D], F32))
        x_in = ctx.enter_context(nc.semaphore("c_rows_loaded"))
        phase_b(nc, d, shared_w, x_rows, x_in)
        phase_c(nc, d, keep, shared_w, x_rows, x_in)


def kernel(**inputs):
    import numpy as np
    import concourse.bacc as bacc
    from concourse.bass_utils import run_bass_kernel_spmd

    attn = lambda n: np.asarray(inputs["L0_xattn_" + n])
    ffn = lambda n: np.asarray(inputs["L0_ffn_" + n])
    x, ctx = np.asarray(inputs["x"]), np.asarray(inputs["ctx_2048"])
    D = x.shape[2]
    E, M, _ = ffn("Wg").shape

    def by_input(w):
        w = np.swapaxes(w, -1, -2)
        w = w.reshape(*w.shape[:-2], w.shape[-2] // P, P, w.shape[-1])
        return np.swapaxes(w, -3, -2)

    def by_hidden(w):
        w = np.swapaxes(w, -1, -2)
        hidden = w.shape[-2]
        chunks = -(-hidden // P)
        full = (chunks - 1) * P
        out = np.zeros((*w.shape[:-2], chunks * P, w.shape[-1]), w.dtype)
        out[..., 0:full, :] = w[..., 0:full, :]
        out[..., full + chunks * P - hidden:, :] = w[..., full:, :]
        return np.swapaxes(out.reshape(*w.shape[:-2], chunks, P, w.shape[-1]), -3, -2)

    flat = lambda w: w.reshape(E, P, -1)
    sg, su = by_input(ffn("Sg")), by_input(ffn("Su"))
    full = (-(-sg.shape[2] // P) - 1) * P
    p = np.arange(P)
    consts = np.concatenate([
        np.eye(P), p[:, None] < p[None, :], np.ones((P, P)), np.broadcast_to(np.arange(E), (P, E)),
        np.broadcast_to(np.arange(E) * CAPACITY, (P, E)), p[:, None] + 1 + P * np.arange(x.shape[1] // P)[None, :]],
        1).astype(np.float32)
    arrays = {
        "x": x,
        "ctxT": np.swapaxes(ctx, 1, 2),
        "wk": attn("Wk_img"), "wq": attn("Wq"), "wv": attn("Wv_img"), "wo": attn("Wo"), "bo": attn("bo"),
        "bq": attn("bq"), "gq": attn("gq"), "bk": attn("bk_img"), "gk": attn("gk_img"),
        "bv": attn("bv_img").reshape(D // P, P).T,
        "gateT": ffn("gate_weight").T,
        "consts": consts,
        "experts": np.concatenate([flat(by_input(ffn("Wg"))), flat(by_input(ffn("Wu"))), flat(by_hidden(ffn("Wd")))], 2),
        "shared_gu": np.concatenate([sg[..., :full], su[..., :full], sg[..., full:], su[..., full:]], 2),
        "sd": by_hidden(ffn("Sd")),
    }
    arrays = {f"in_{n}_dram": np.ascontiguousarray(a) for n, a in arrays.items()}

    nc = bacc.Bacc("TRN2", target_bir_lowering=False, num_devices=1)
    d = {n[3:-5]: nc.dram_tensor(n, a.shape, mybir.dt.from_np(a.dtype), kind="ExternalInput").ap()
         for n, a in arrays.items()}
    d["out"] = nc.dram_tensor("out_0_dram", (x.shape[0] * x.shape[1], D), F32, kind="ExternalOutput").ap()
    d["m"] = M
    cross_attention_moe(nc, d)
    r = run_bass_kernel_spmd(nc, [arrays], core_ids=[0])
    return r.results[0]["out_0_dram"].reshape(x.shape)
```
